# Optimizing a Trainium2 kernel written in Bass

```python
import numpy as np
import jax
import jax.numpy as jnp

def _softmax(x, axis=-1):
    return jax.nn.softmax(x, axis=axis)

def _gelu(x):
    return jax.nn.gelu(x, approximate=True)

def _silu(x):
    return jax.nn.silu(x)

def _sigmoid(x):
    return jax.nn.sigmoid(x)

def _layernorm(x, axis=-1, eps=1e-05):
    m = jnp.mean(x, axis=axis, keepdims=True)
    v = jnp.var(x, axis=axis, keepdims=True)
    return (x - m) / jnp.sqrt(v + eps)

def _scatter_add(tgt, idx, src, axis=0):
    return tgt.at[idx].add(src)

def _segment_sum(src, seg, n):
    return jax.ops.segment_sum(src, seg, n)
kernel_name = 'mk_sandwich_d4_jaxref_r8_647c21'

def setup_inputs(seed: int=0):
    np.random.seed(seed)
    _w = jnp.asarray

    def _L0_attn_setup():
        import jax, jax.numpy as jnp
        import numpy as np
        B, S, D = (4, 256, 128)
        SCALE = 1.0 / np.sqrt(D)
        key = jax.random.key(seed)
        k1, k2, k3 = jax.random.split(key, 3)
        x = jax.random.normal(k1, (B, S, D), dtype=jnp.float32)
        bound = 1.0 / np.sqrt(D)
        W_qk = jax.random.uniform(k2, (D, D), minval=-bound, maxval=bound, dtype=jnp.float32)
        W_v = jax.random.uniform(k3, (D, D), minval=-bound, maxval=bound, dtype=jnp.float32)
        alibi_slope = jnp.full((1,), 0.5, dtype=jnp.float32)
        return {'x': x, 'W_qk': W_qk, 'W_v': W_v, 'alibi_slope': alibi_slope}
    _L0_attn_in = _L0_attn_setup()

    def _L0_ffn_setup():
        import jax, jax.numpy as jnp
        import numpy as np
        E = 8
        TOP_K = 2
        H = 128
        F = 512
        LN_EPS = 1e-12
        key = jax.random.key(seed)
        ks = jax.random.split(key, 9)
        s = lambda k, shape, scale: jax.random.normal(k, shape, dtype=jnp.float32) * scale
        return {'hidden_states': s(ks[0], (4, 256, H), 1.0), 'Wr': s(ks[1], (E, H), 0.02), 'br': jnp.zeros((E,), jnp.float32), 'W1': s(ks[2], (E, F, H), 0.02), 'b1': jnp.zeros((E, F), jnp.float32), 'W2': s(ks[3], (E, H, F), 0.02), 'b2': jnp.zeros((E, H), jnp.float32), 'ln_w': jnp.ones((H,), jnp.float32), 'ln_b': jnp.zeros((H,), jnp.float32)}
    _L0_ffn_in = _L0_ffn_setup()

    def _L1_attn_setup():
        import jax, jax.numpy as jnp
        import numpy as np
        HEADS = 16
        BIAS_STRENGTH = 0.1
        LN_EPS = 1e-05

        def _layernorm(x, gamma, beta):
            mu = jnp.mean(x, axis=-1, keepdims=True)
            var = jnp.mean((x - mu) ** 2, axis=-1, keepdims=True)
            return (x - mu) * jax.lax.rsqrt(var + LN_EPS) * gamma + beta

        def _spatial_bias(spatial_centers, N, dtype):
            diff = spatial_centers[:, None, :] - spatial_centers[None, :, :]
            dist = jnp.sqrt(jnp.sum(diff * diff, axis=-1))
            max_dist = jnp.max(dist)
            core = jnp.where(max_dist > 1e-06, -dist / max_dist, 0.0) * BIAS_STRENGTH
            P = spatial_centers.shape[0]
            bias = jnp.zeros((N, N), dtype=dtype)
            return bias.at[1:P + 1, 1:P + 1].set(core.astype(dtype))
        key = jax.random.key(seed)
        ks = jax.random.split(key, 4)
        B, N, D, P = (2, 256, 128, 128)
        return {'x': jax.random.normal(ks[0], (B, N, D), dtype=jnp.float32), 'W_qkv': jax.random.normal(ks[1], (3 * D, D), dtype=jnp.float32) * D ** (-0.5), 'W_proj': jax.random.normal(ks[2], (D, D), dtype=jnp.float32) * D ** (-0.5), 'b_proj': jnp.zeros((D,), dtype=jnp.float32), 'ln_gamma': jnp.ones((D,), dtype=jnp.float32), 'ln_beta': jnp.zeros((D,), dtype=jnp.float32), 'spatial_centers': jax.random.uniform(ks[3], (P, 2), dtype=jnp.float32)}
    _L1_attn_in = _L1_attn_setup()

    def _L1_ffn_setup():
        import jax, jax.numpy as jnp
        import numpy as np
        D_MODEL = 128
        H_SHARED = 256
        H_ROUTED = 128
        N_EXPERTS = 8
        TOP_K = 2
        key = jax.random.key(seed)
        ks = jax.random.split(key, 8)
        B, T = (2, 256)
        sc_d = 1.0 / np.sqrt(D_MODEL)
        sc_hs = 1.0 / np.sqrt(H_SHARED)
        sc_hr = 1.0 / np.sqrt(H_ROUTED)
        return {'x': jax.random.normal(ks[0], (B, T, D_MODEL), dtype=jnp.float32), 'router_w': jax.random.normal(ks[1], (N_EXPERTS, D_MODEL), dtype=jnp.float32) * sc_d, 'router_bias': jnp.zeros((N_EXPERTS,), dtype=jnp.float32), 'sw1': jax.random.normal(ks[2], (D_MODEL, H_SHARED), dtype=jnp.float32) * sc_d, 'sw3': jax.random.normal(ks[3], (D_MODEL, H_SHARED), dtype=jnp.float32) * sc_d, 'sw2': jax.random.normal(ks[4], (H_SHARED, D_MODEL), dtype=jnp.float32) * sc_hs, 'ew1': jax.random.normal(ks[5], (N_EXPERTS, D_MODEL, H_ROUTED), dtype=jnp.float32) * sc_d, 'ew2': jax.random.normal(ks[6], (N_EXPERTS, H_ROUTED, D_MODEL), dtype=jnp.float32) * sc_hr}
    _L1_ffn_in = _L1_ffn_setup()

    def _L2_attn_setup():
        import math
        import jax, jax.numpy as jnp
        import numpy as np
        B, T, C, H = (1, 512, 128, 16)
        HD = C // H

        def get_slopes(n):

            def pow2(n):
                start = 2 ** (-2 ** (-(math.log2(n) - 3)))
                return [start * start ** i for i in range(n)]
            if math.log2(n).is_integer():
                return pow2(n)
            cp2 = 2 ** math.floor(math.log2(n))
            return pow2(cp2) + get_slopes(2 * cp2)[0::2][:n - cp2]
        key = jax.random.key(seed)
        ks = jax.random.split(key, 5)
        x = jax.random.normal(ks[0], (B, T, C), dtype=jnp.float32)
        mk = lambda k: 0.02 * jax.random.normal(k, (C, C), dtype=jnp.float32)
        return {'x': x, 'Wq': mk(ks[1]), 'bq': jnp.zeros((C,), jnp.float32), 'Wk': mk(ks[2]), 'bk': jnp.zeros((C,), jnp.float32), 'Wv': mk(ks[3]), 'bv': jnp.zeros((C,), jnp.float32), 'Wo': 0.02 / math.sqrt(24) * jax.random.normal(ks[4], (C, C), dtype=jnp.float32), 'bo': jnp.zeros((C,), jnp.float32)}
    _L2_attn_in = _L2_attn_setup()

    def _L2_ffn_setup():
        import jax, jax.numpy as jnp
        import numpy as np
        H, F, E_SHARED, E_ROUTED, K = (128, 512, 1, 8, 2)

        def _expert(x, w_up, w_down):
            h = jax.nn.gelu(jnp.einsum('bsh,hf->bsf', x, w_up), approximate=False)
            return jnp.einsum('bsf,fh->bsh', h, w_down)
        key = jax.random.key(seed)
        ks = jax.random.split(key, 6)
        x = jax.random.normal(ks[0], (4, 256, H), dtype=jnp.float32)
        s = 0.02
        shared_up = jax.random.normal(ks[1], (E_SHARED, H, F), dtype=jnp.float32) * s
        shared_down = jax.random.normal(ks[2], (E_SHARED, F, H), dtype=jnp.float32) * s
        routed_up = jax.random.normal(ks[3], (E_ROUTED, H, F), dtype=jnp.float32) * s
        routed_down = jax.random.normal(ks[4], (E_ROUTED, F, H), dtype=jnp.float32) * s
        router_w = jax.random.normal(ks[5], (H, E_ROUTED), dtype=jnp.float32) * s
        return {'x': x, 'shared_up': shared_up, 'shared_down': shared_down, 'routed_up': routed_up, 'routed_down': routed_down, 'router_w': router_w}
    _L2_ffn_in = _L2_ffn_setup()

    def _L3_attn_setup():
        import jax, jax.numpy as jnp
        import numpy as np
        import math
        D_MODEL, D_STATE, D_CONV, EXPAND = (128, 64, 4, 2)
        D_INNER = D_MODEL * EXPAND
        BATCH, SEQ_LEN = (4, 256)
        CHUNK = 16

        def _ssm_forward(x, W_in, conv_w, conv_b, W_x, A_log, dt_bias, D, W_out):
            batch, seq_len, _ = x.shape
            d_inner = D.shape[0]
            d_state = A_log.shape[1]
            d_conv = conv_w.shape[1]
            xz = x @ W_in
            x_ssm, z = jnp.split(xz, 2, axis=-1)
            xc = jnp.transpose(x_ssm, (0, 2, 1))
            kern = conv_w[:, None, :]
            xc = jax.lax.conv_general_dilated(xc, kern, (1,), [(d_conv - 1, 0)], feature_group_count=d_inner)
            xc = xc + conv_b[None, :, None]
            x_conv = jax.nn.silu(jnp.transpose(xc, (0, 2, 1)))
            ssm = x_conv @ W_x
            Bm = ssm[..., :d_state]
            Cm = ssm[..., d_state:2 * d_state]
            dt = jax.nn.softplus(ssm[..., -1:] + dt_bias)
            A = -jnp.exp(A_log)
            t_idx = jnp.arange(seq_len)
            detach = (t_idx % CHUNK == 0) & (t_idx > 0)

            def step(h, inp):
                xt, Bt, Ct, dtt, det = inp
                h = jnp.where(det, jax.lax.stop_gradient(h), h)
                A_bar = jnp.exp(A[None] * dtt[:, :, None])
                h = A_bar * h + dtt[:, :, None] * Bt[:, None, :] * xt[:, :, None]
                yt = jnp.einsum('bdn,bn->bd', h, Ct)
                return (h, yt)
            h0 = jnp.zeros((batch, d_inner, d_state), x.dtype)
            xs = (jnp.moveaxis(x_conv, 1, 0), jnp.moveaxis(Bm, 1, 0), jnp.moveaxis(Cm, 1, 0), jnp.moveaxis(dt, 1, 0), detach)
            _, ys = jax.lax.scan(step, h0, xs)
            y = jnp.moveaxis(ys, 0, 1)
            y = y + D * x_conv
            y = y * jax.nn.silu(z)
            return y @ W_out
        key = jax.random.key(seed)
        ks = jax.random.split(key, 8)
        x = jax.random.normal(ks[0], (BATCH, SEQ_LEN, D_MODEL), jnp.float32)
        W_in = jax.random.normal(ks[1], (D_MODEL, 2 * D_INNER), jnp.float32) / math.sqrt(D_MODEL)
        conv_w = jax.random.normal(ks[2], (D_INNER, D_CONV), jnp.float32) / math.sqrt(D_CONV)
        conv_b = jax.random.normal(ks[3], (D_INNER,), jnp.float32) * 0.01
        W_x = jax.random.normal(ks[4], (D_INNER, 2 * D_STATE + 1), jnp.float32) / math.sqrt(D_INNER)
        A_log = jnp.broadcast_to(jnp.log(jnp.arange(1, D_STATE + 1, dtype=jnp.float32)), (D_INNER, D_STATE)) + 0.0
        dt_bias = jax.random.uniform(ks[5], (D_INNER,), jnp.float32, math.log(0.001), math.log(0.1))
        D = jnp.ones((D_INNER,), jnp.float32)
        W_out = jax.random.normal(ks[6], (D_INNER, D_MODEL), jnp.float32) / math.sqrt(D_INNER)
        return {'x': x, 'W_in': W_in, 'conv_w': conv_w, 'conv_b': conv_b, 'W_x': W_x, 'A_log': A_log, 'dt_bias': dt_bias, 'D': D, 'W_out': W_out}
    _L3_attn_in = _L3_attn_setup()

    def _L3_ffn_setup():
        import jax, jax.numpy as jnp
        import numpy as np
        TOP_K = 2

        def _moe(x, Wr, br, W1, b1, W2, b2):
            B, S, D = x.shape
            E = Wr.shape[1]
            xt = x.reshape(-1, D)
            logits = xt @ Wr + br
            top_vals, top_idx = jax.lax.top_k(logits, TOP_K)
            mask = jnp.zeros_like(logits, dtype=bool).at[jnp.arange(xt.shape[0])[:, None], top_idx].set(True)
            sparse_logits = jnp.where(mask, logits, -jnp.inf)
            gate = jax.nn.softmax(sparse_logits, axis=-1)
            h = jax.nn.relu(jnp.einsum('td,edh->teh', xt, W1) + b1)
            y = jnp.einsum('teh,ehd->ted', h, W2) + b2
            out = jnp.einsum('ted,te->td', y, gate)
            return out.reshape(B, S, D)
        key = jax.random.key(seed)
        ks = jax.random.split(key, 5)
        B, S, D, E, H = (2, 256, 128, 8, 512)
        scale = 1.0 / np.sqrt(D)
        return {'x': jax.random.normal(ks[0], (B, S, D), dtype=jnp.float32), 'Wr': jax.random.normal(ks[1], (D, E), dtype=jnp.float32) * scale, 'br': jnp.zeros((E,), dtype=jnp.float32), 'W1': jax.random.normal(ks[2], (E, D, H), dtype=jnp.float32) * scale, 'b1': jnp.zeros((E, H), dtype=jnp.float32), 'W2': jax.random.normal(ks[3], (E, H, D), dtype=jnp.float32) * (1.0 / np.sqrt(H)), 'b2': jnp.zeros((E, D), dtype=jnp.float32)}
    _L3_ffn_in = _L3_ffn_setup()
    _d = {'L0_attn_x': _L0_attn_in['x'], 'L0_attn_W_qk': _L0_attn_in['W_qk'], 'L0_attn_W_v': _L0_attn_in['W_v'], 'L0_attn_alibi_slope': _L0_attn_in['alibi_slope'], 'L0_ffn_Wr': _L0_ffn_in['Wr'], 'L0_ffn_br': _L0_ffn_in['br'], 'L0_ffn_W1': _L0_ffn_in['W1'], 'L0_ffn_b1': _L0_ffn_in['b1'], 'L0_ffn_W2': _L0_ffn_in['W2'], 'L0_ffn_b2': _L0_ffn_in['b2'], 'L0_ffn_ln_w': _L0_ffn_in['ln_w'], 'L0_ffn_ln_b': _L0_ffn_in['ln_b'], 'L1_attn_W_qkv': _L1_attn_in['W_qkv'], 'L1_attn_W_proj': _L1_attn_in['W_proj'], 'L1_attn_b_proj': _L1_attn_in['b_proj'], 'L1_attn_ln_gamma': _L1_attn_in['ln_gamma'], 'L1_attn_ln_beta': _L1_attn_in['ln_beta'], 'L1_attn_spatial_centers': _L1_attn_in['spatial_centers'], 'L1_ffn_router_w': _L1_ffn_in['router_w'], 'L1_ffn_router_bias': _L1_ffn_in['router_bias'], 'L1_ffn_sw1': _L1_ffn_in['sw1'], 'L1_ffn_sw3': _L1_ffn_in['sw3'], 'L1_ffn_sw2': _L1_ffn_in['sw2'], 'L1_ffn_ew1': _L1_ffn_in['ew1'], 'L1_ffn_ew2': _L1_ffn_in['ew2'], 'L2_attn_Wq': _L2_attn_in['Wq'], 'L2_attn_bq': _L2_attn_in['bq'], 'L2_attn_Wk': _L2_attn_in['Wk'], 'L2_attn_bk': _L2_attn_in['bk'], 'L2_attn_Wv': _L2_attn_in['Wv'], 'L2_attn_bv': _L2_attn_in['bv'], 'L2_attn_Wo': _L2_attn_in['Wo'], 'L2_attn_bo': _L2_attn_in['bo'], 'L2_ffn_shared_up': _L2_ffn_in['shared_up'], 'L2_ffn_shared_down': _L2_ffn_in['shared_down'], 'L2_ffn_routed_up': _L2_ffn_in['routed_up'], 'L2_ffn_routed_down': _L2_ffn_in['routed_down'], 'L2_ffn_router_w': _L2_ffn_in['router_w'], 'L3_attn_W_in': _L3_attn_in['W_in'], 'L3_attn_conv_w': _L3_attn_in['conv_w'], 'L3_attn_conv_b': _L3_attn_in['conv_b'], 'L3_attn_W_x': _L3_attn_in['W_x'], 'L3_attn_A_log': _L3_attn_in['A_log'], 'L3_attn_dt_bias': _L3_attn_in['dt_bias'], 'L3_attn_D': _L3_attn_in['D'], 'L3_attn_W_out': _L3_attn_in['W_out'], 'L3_ffn_Wr': _L3_ffn_in['Wr'], 'L3_ffn_br': _L3_ffn_in['br'], 'L3_ffn_W1': _L3_ffn_in['W1'], 'L3_ffn_b1': _L3_ffn_in['b1'], 'L3_ffn_W2': _L3_ffn_in['W2'], 'L3_ffn_b2': _L3_ffn_in['b2']}
    _x0 = _d['L0_attn_x']
    _d['L0_attn_x'] = jax.random.normal(jax.random.fold_in(jax.random.key(seed), 1), (8, 256, 128), dtype=_x0.dtype)
    del _x0
    return _d

def reference(L0_attn_x, L0_attn_W_qk, L0_attn_W_v, L0_attn_alibi_slope, L0_ffn_Wr, L0_ffn_br, L0_ffn_W1, L0_ffn_b1, L0_ffn_W2, L0_ffn_b2, L0_ffn_ln_w, L0_ffn_ln_b, L1_attn_W_qkv, L1_attn_W_proj, L1_attn_b_proj, L1_attn_ln_gamma, L1_attn_ln_beta, L1_attn_spatial_centers, L1_ffn_router_w, L1_ffn_router_bias, L1_ffn_sw1, L1_ffn_sw3, L1_ffn_sw2, L1_ffn_ew1, L1_ffn_ew2, L2_attn_Wq, L2_attn_bq, L2_attn_Wk, L2_attn_bk, L2_attn_Wv, L2_attn_bv, L2_attn_Wo, L2_attn_bo, L2_ffn_shared_up, L2_ffn_shared_down, L2_ffn_routed_up, L2_ffn_routed_down, L2_ffn_router_w, L3_attn_W_in, L3_attn_conv_w, L3_attn_conv_b, L3_attn_W_x, L3_attn_A_log, L3_attn_dt_bias, L3_attn_D, L3_attn_W_out, L3_ffn_Wr, L3_ffn_br, L3_ffn_W1, L3_ffn_b1, L3_ffn_W2, L3_ffn_b2):

    def _L0_attn_ref(x, W_qk, W_v, alibi_slope):
        import jax, jax.numpy as jnp
        import numpy as np
        B, S, D = (4, 256, 128)
        SCALE = 1.0 / np.sqrt(D)
        seq_len = x.shape[1]
        scores = jnp.einsum('bqe,bke->bqk', x @ W_qk, x) * SCALE
        kpos = jnp.arange(seq_len, dtype=x.dtype)[None, :]
        qpos = jnp.arange(seq_len, dtype=x.dtype)[:, None]
        scores = scores + (kpos - qpos) * alibi_slope[0]
        causal = qpos >= kpos
        scores = jnp.where(causal, scores, -jnp.inf)
        attn = jax.nn.softmax(scores, axis=-1)
        v = x @ W_v.T
        return jnp.einsum('bqk,bkd->bqd', attn, v)

    def _L0_ffn_ref(hidden_states, Wr, br, W1, b1, W2, b2, ln_w, ln_b):
        import jax, jax.numpy as jnp
        import numpy as np
        E = 8
        TOP_K = 2
        H = 128
        F = 512
        LN_EPS = 1e-12
        bsz, seqlen, h = hidden_states.shape
        x = hidden_states.reshape(-1, h)
        logits = x @ Wr.T + br
        topk_vals, topk_idx = jax.lax.top_k(logits, TOP_K)
        topk_w = jax.nn.softmax(topk_vals, axis=-1)
        out = jnp.zeros_like(x)
        for e in range(E):
            cw = jnp.sum(topk_w * (topk_idx == e), axis=-1)
            y = jax.nn.gelu(x @ W1[e].T + b1[e], approximate=False) @ W2[e].T + b2[e]
            out = out + cw[:, None] * y
        z = out + x
        mu = jnp.mean(z, axis=-1, keepdims=True)
        var = jnp.mean(jnp.square(z - mu), axis=-1, keepdims=True)
        z = (z - mu) * jax.lax.rsqrt(var + LN_EPS) * ln_w + ln_b
        return z.reshape(bsz, seqlen, h)

    def _L1_attn_ref(x, W_qkv, W_proj, b_proj, ln_gamma, ln_beta, spatial_centers):
        import jax, jax.numpy as jnp
        import numpy as np
        HEADS = 16
        BIAS_STRENGTH = 0.1
        LN_EPS = 1e-05

        def _layernorm(x, gamma, beta):
            mu = jnp.mean(x, axis=-1, keepdims=True)
            var = jnp.mean((x - mu) ** 2, axis=-1, keepdims=True)
            return (x - mu) * jax.lax.rsqrt(var + LN_EPS) * gamma + beta

        def _spatial_bias(spatial_centers, N, dtype):
            diff = spatial_centers[:, None, :] - spatial_centers[None, :, :]
            dist = jnp.sqrt(jnp.sum(diff * diff, axis=-1))
            max_dist = jnp.max(dist)
            core = jnp.where(max_dist > 1e-06, -dist / max_dist, 0.0) * BIAS_STRENGTH
            P = spatial_centers.shape[0]
            bias = jnp.zeros((N, N), dtype=dtype)
            return bias.at[1:P + 1, 1:P + 1].set(core.astype(dtype))
        B, N, D = x.shape
        H = HEADS
        hd = D // H
        scale = hd ** (-0.5)
        qkv = jnp.einsum('bnd,ed->bne', x, W_qkv)
        qkv = qkv.reshape(B, N, 3, H, hd).transpose(2, 0, 3, 1, 4)
        q, k, v = (qkv[0], qkv[1], qkv[2])
        attn = jnp.einsum('bhnd,bhmd->bhnm', q, k) * scale
        P = spatial_centers.shape[0]
        if N >= P + 1:
            attn = attn + _spatial_bias(spatial_centers, N, x.dtype)[None, None]
        attn = jax.nn.softmax(attn, axis=-1)
        out = jnp.einsum('bhnm,bhmd->bhnd', attn, v)
        out = out.transpose(0, 2, 1, 3).reshape(B, N, D)
        out = jnp.einsum('bnd,ed->bne', out, W_proj) + b_proj
        return out + _layernorm(x, ln_gamma, ln_beta)

    def _L1_ffn_ref(x, router_w, router_bias, sw1, sw3, sw2, ew1, ew2):
        import jax, jax.numpy as jnp
        import numpy as np
        D_MODEL = 128
        H_SHARED = 256
        H_ROUTED = 128
        N_EXPERTS = 8
        TOP_K = 2
        B, T, C = x.shape
        xf = x.reshape(-1, C)
        shared_out = jax.nn.silu(xf @ sw1) * (xf @ sw3) @ sw2
        s = jax.nn.sigmoid((xf @ router_w.T).astype(jnp.float32))
        sel_scores = s + router_bias.astype(jnp.float32)
        _, topk_idx = jax.lax.top_k(sel_scores, TOP_K)
        s_sel = jnp.take_along_axis(s, topk_idx, axis=1)
        denom = s_sel.sum(axis=1, keepdims=True)
        gates = jnp.where(denom > 1e-09, s_sel / (denom + 1e-09), 1.0 / TOP_K).astype(x.dtype)
        one_hot = jax.nn.one_hot(topk_idx, N_EXPERTS, dtype=x.dtype)
        comb = jnp.einsum('nke,nk->ne', one_hot, gates)
        h = jax.nn.gelu(jnp.einsum('nd,edh->neh', xf, ew1), approximate=False)
        y = jnp.einsum('neh,ehd->ned', h, ew2)
        routed_out = jnp.einsum('ned,ne->nd', y, comb)
        return (shared_out + routed_out).reshape(B, T, C)

    def _L2_attn_ref(x, Wq, bq, Wk, bk, Wv, bv, Wo, bo):
        import math
        import jax, jax.numpy as jnp
        import numpy as np
        B, T, C, H = (1, 512, 128, 16)
        HD = C // H

        def get_slopes(n):

            def pow2(n):
                start = 2 ** (-2 ** (-(math.log2(n) - 3)))
                return [start * start ** i for i in range(n)]
            if math.log2(n).is_integer():
                return pow2(n)
            cp2 = 2 ** math.floor(math.log2(n))
            return pow2(cp2) + get_slopes(2 * cp2)[0::2][:n - cp2]
        b, t, c = x.shape
        proj = lambda W, bias: (x @ W + bias).reshape(b, t, H, HD).transpose(0, 2, 1, 3)
        q, k, v = (proj(Wq, bq), proj(Wk, bk), proj(Wv, bv))
        scale = 1.0 / jnp.sqrt(jnp.asarray(HD, x.dtype))
        attn = jnp.einsum('bhqd,bhkd->bhqk', q, k) * scale
        slopes = jnp.asarray(get_slopes(H), dtype=x.dtype)
        alibi = -slopes[:, None, None] * (t - 1 - jnp.arange(t, dtype=x.dtype))[None, None, :]
        attn = attn + alibi
        causal = jnp.tril(jnp.ones((t, t), dtype=bool))[None, None]
        attn = jnp.where(causal, attn, jnp.finfo(x.dtype).min)
        p = jax.nn.softmax(attn, axis=-1)
        out = jnp.einsum('bhqk,bhkd->bhqd', p, v).transpose(0, 2, 1, 3).reshape(b, t, c)
        return out @ Wo + bo

    def _L2_ffn_ref(x, shared_up, shared_down, routed_up, routed_down, router_w):
        import jax, jax.numpy as jnp
        import numpy as np
        H, F, E_SHARED, E_ROUTED, K = (128, 512, 1, 8, 2)

        def _expert(x, w_up, w_down):
            h = jax.nn.gelu(jnp.einsum('bsh,hf->bsf', x, w_up), approximate=False)
            return jnp.einsum('bsf,fh->bsh', h, w_down)
        shared_out = jnp.zeros_like(x)
        for i in range(E_SHARED):
            shared_out = shared_out + _expert(x, shared_up[i], shared_down[i])
        probs = jax.nn.softmax(jnp.einsum('bsh,he->bse', x, router_w), axis=-1)
        top_k_prob, top_k_idx = jax.lax.top_k(probs, K)
        onehot = jax.nn.one_hot(top_k_idx, E_ROUTED, dtype=x.dtype)
        gates = jnp.einsum('bsk,bske->bse', top_k_prob, onehot)
        routed_out = jnp.zeros_like(x)
        for e in range(E_ROUTED):
            y = _expert(x, routed_up[e], routed_down[e])
            routed_out = routed_out + gates[..., e:e + 1] * y
        return shared_out + routed_out + x

    def _L3_attn_ref(x, W_in, conv_w, conv_b, W_x, A_log, dt_bias, D, W_out):
        import jax, jax.numpy as jnp
        import numpy as np
        import math
        D_MODEL, D_STATE, D_CONV, EXPAND = (128, 64, 4, 2)
        D_INNER = D_MODEL * EXPAND
        BATCH, SEQ_LEN = (4, 256)
        CHUNK = 16

        def _ssm_forward(x, W_in, conv_w, conv_b, W_x, A_log, dt_bias, D, W_out):
            batch, seq_len, _ = x.shape
            d_inner = D.shape[0]
            d_state = A_log.shape[1]
            d_conv = conv_w.shape[1]
            xz = x @ W_in
            x_ssm, z = jnp.split(xz, 2, axis=-1)
            xc = jnp.transpose(x_ssm, (0, 2, 1))
            kern = conv_w[:, None, :]
            xc = jax.lax.conv_general_dilated(xc, kern, (1,), [(d_conv - 1, 0)], feature_group_count=d_inner)
            xc = xc + conv_b[None, :, None]
            x_conv = jax.nn.silu(jnp.transpose(xc, (0, 2, 1)))
            ssm = x_conv @ W_x
            Bm = ssm[..., :d_state]
            Cm = ssm[..., d_state:2 * d_state]
            dt = jax.nn.softplus(ssm[..., -1:] + dt_bias)
            A = -jnp.exp(A_log)
            t_idx = jnp.arange(seq_len)
            detach = (t_idx % CHUNK == 0) & (t_idx > 0)

            def step(h, inp):
                xt, Bt, Ct, dtt, det = inp
                h = jnp.where(det, jax.lax.stop_gradient(h), h)
                A_bar = jnp.exp(A[None] * dtt[:, :, None])
                h = A_bar * h + dtt[:, :, None] * Bt[:, None, :] * xt[:, :, None]
                yt = jnp.einsum('bdn,bn->bd', h, Ct)
                return (h, yt)
            h0 = jnp.zeros((batch, d_inner, d_state), x.dtype)
            xs = (jnp.moveaxis(x_conv, 1, 0), jnp.moveaxis(Bm, 1, 0), jnp.moveaxis(Cm, 1, 0), jnp.moveaxis(dt, 1, 0), detach)
            _, ys = jax.lax.scan(step, h0, xs)
            y = jnp.moveaxis(ys, 0, 1)
            y = y + D * x_conv
            y = y * jax.nn.silu(z)
            return y @ W_out
        return _ssm_forward(x, W_in, conv_w, conv_b, W_x, A_log, dt_bias, D, W_out)

    def _L3_ffn_ref(x, Wr, br, W1, b1, W2, b2):
        import jax, jax.numpy as jnp
        import numpy as np
        TOP_K = 2

        def _moe(x, Wr, br, W1, b1, W2, b2):
            B, S, D = x.shape
            E = Wr.shape[1]
            xt = x.reshape(-1, D)
            logits = xt @ Wr + br
            top_vals, top_idx = jax.lax.top_k(logits, TOP_K)
            mask = jnp.zeros_like(logits, dtype=bool).at[jnp.arange(xt.shape[0])[:, None], top_idx].set(True)
            sparse_logits = jnp.where(mask, logits, -jnp.inf)
            gate = jax.nn.softmax(sparse_logits, axis=-1)
            h = jax.nn.relu(jnp.einsum('td,edh->teh', xt, W1) + b1)
            y = jnp.einsum('teh,ehd->ted', h, W2) + b2
            out = jnp.einsum('ted,te->td', y, gate)
            return out.reshape(B, S, D)
        return _moe(x, Wr, br, W1, b1, W2, b2)
    x = L0_attn_x
    x = x + _layernorm(_L0_attn_ref(_layernorm(x, axis=-1), L0_attn_W_qk, L0_attn_W_v, L0_attn_alibi_slope), axis=-1)
    x = x + _layernorm(_L0_ffn_ref(_layernorm(x, axis=-1), L0_ffn_Wr, L0_ffn_br, L0_ffn_W1, L0_ffn_b1, L0_ffn_W2, L0_ffn_b2, L0_ffn_ln_w, L0_ffn_ln_b), axis=-1)
    x = x + _layernorm(_L1_attn_ref(_layernorm(x, axis=-1), L1_attn_W_qkv, L1_attn_W_proj, L1_attn_b_proj, L1_attn_ln_gamma, L1_attn_ln_beta, L1_attn_spatial_centers), axis=-1)
    x = x + _layernorm(_L1_ffn_ref(_layernorm(x, axis=-1), L1_ffn_router_w, L1_ffn_router_bias, L1_ffn_sw1, L1_ffn_sw3, L1_ffn_sw2, L1_ffn_ew1, L1_ffn_ew2), axis=-1)
    x = x + _layernorm(_L2_attn_ref(_layernorm(x, axis=-1), L2_attn_Wq, L2_attn_bq, L2_attn_Wk, L2_attn_bk, L2_attn_Wv, L2_attn_bv, L2_attn_Wo, L2_attn_bo), axis=-1)
    x = x + _layernorm(_L2_ffn_ref(_layernorm(x, axis=-1), L2_ffn_shared_up, L2_ffn_shared_down, L2_ffn_routed_up, L2_ffn_routed_down, L2_ffn_router_w), axis=-1)
    x = x + _layernorm(_L3_attn_ref(_layernorm(x, axis=-1), L3_attn_W_in, L3_attn_conv_w, L3_attn_conv_b, L3_attn_W_x, L3_attn_A_log, L3_attn_dt_bias, L3_attn_D, L3_attn_W_out), axis=-1)
    x = x + _layernorm(_L3_ffn_ref(_layernorm(x, axis=-1), L3_ffn_Wr, L3_ffn_br, L3_ffn_W1, L3_ffn_b1, L3_ffn_W2, L3_ffn_b2), axis=-1)
    return x

_drawn_inputs = setup_inputs


def setup_inputs(seed=0):
    import zlib

    import numpy as np

    out = dict(_drawn_inputs(seed))
    spreads = {'L0_ffn_br': (0.0, 0.1),
     'L0_ffn_b1': (0.0, 0.327),
     'L0_ffn_b2': (0.0, 0.1),
     'L0_ffn_ln_w': (1.0, 0.2),
     'L0_ffn_ln_b': (0.0, 0.1),
     'L1_attn_b_proj': (0.0, 0.1),
     'L1_attn_ln_gamma': (1.0, 0.2),
     'L1_attn_ln_beta': (0.0, 0.1),
     'L1_ffn_router_bias': (0.0, 0.1),
     'L2_attn_bq': (0.0, 0.8),
     'L2_attn_bk': (0.0, 0.8),
     'L2_attn_bv': (0.0, 0.303),
     'L2_attn_bo': (0.0, 0.1),
     'L3_attn_D': (1.0, 0.2),
     'L3_ffn_br': (0.0, 0.1),
     'L3_ffn_b1': (0.0, 0.386),
     'L3_ffn_b2': (0.0, 0.273)}
    factors = {'L1_attn_spatial_centers': 8.0,
     'L2_attn_Wq': 8.0,
     'L2_attn_Wk': 8.0,
     'L2_attn_Wv': 3.156,
     'L2_ffn_shared_down': 2.775,
     'L2_ffn_routed_up': 6.372,
     'L2_ffn_routed_down': 5.774,
     'L2_ffn_router_w': 5.773,
     'L3_attn_conv_b': 6.904}
    for name, (base, spread) in spreads.items():
        noise = np.random.default_rng([zlib.crc32(name.encode()), seed]).standard_normal(out[name].shape)
        drawn = base * np.exp(spread * noise) if base else spread * noise
        out[name] = jnp.asarray(drawn.astype(out[name].dtype))
    for name, factor in factors.items():
        out[name] = (out[name] * factor).astype(out[name].dtype)
    return out
```

```python
from contextlib import ExitStack

import numpy as np

import concourse.bass as bass
from concourse import mybir

ALU = mybir.AluOpType
ACT = mybir.ActivationFunctionType
F32 = mybir.dt.float32
BF16 = mybir.dt.bfloat16
AX_X = mybir.AxisListType.X

P = 128
D = 128
SEQ = 256
NSEQ = 8
GT = 512
GROUPS = NSEQ * SEQ // GT
TILES = GT // P
PAIR = GT // SEQ
HEADS = 16
HD = D // HEADS
QUAD = 32
HG = HEADS // 4
ROW_MAX = HD
ROW_POS = HD + 1
HROWS = HD + 2
E = 8
N_STATE = 64
HALVES = 2
TAPS = 4
LN_EPS = 1e-5
BW = P + 2
MASKED = -1e30
BELOW = -3e38
TINY = 1e-30


class Steps:

    def __init__(self, engine, sem, g, per):
        self.engine, self.sem, self.g, self.per, self.n = engine, sem, g, per, 0

    def __call__(self, instruction):
        instruction.then_inc(self.sem, 1)
        self.n += 1
        self.engine.wait_ge(self.sem, self.g * self.per + self.n)

    def close(self):
        assert self.n == self.per, f"{self.n} linked steps, {self.per} stated"


HEAD = 3
NORM = HEAD + 1
TAIL = NORM + 1
TOP2 = 11
STEPS = {
    "a0": HEAD + PAIR + 1 + TILES + TAIL,
    "f0": HEAD + 1 + TOP2 + 5 + 1 + NORM + 2 + TAIL,
    "a1": HEAD + NORM + 2 + TILES + 2 + TAIL,
    "f1": HEAD + 3 + TOP2 + 11 + TAIL,
    "a2": HEAD + TILES + 1 + TAIL,
    "f2": HEAD + 1 + 3 + TOP2 + 2 + TAIL,
    "a3": HEAD + HALVES * (TAPS - 1) + HALVES + 2 * 3 + 4 + 4 + 1 + 1 + TAIL,
    "f3": HEAD + 1 + TOP2 + 5 + 1 + TAIL,
}


def build(nc, t, out):
    ctx = ExitStack()
    with ctx:
        def sb(name, shape, dt=F32):
            return ctx.enter_context(nc.sbuf_tensor(name, shape, dt))

        def sem(name):
            return ctx.enter_context(nc.semaphore(name))

        bank = ctx.enter_context(nc.psum_tensor("bank", [P, 8, 512], F32))

        stream = sb("stream", [P, GROUPS * TILES, D])
        normed = sb("normed", [P, TILES, D])
        normed_t = sb("normed_t", [P, GT])
        y = sb("y", [P, TILES, D])
        stats = sb("stats", [P, TILES, 6])
        mean = sb("mean", [P, TILES, 1])
        spread_ = sb("spread_", [P, 4, TILES])
        var_eps = sb("var_eps", [P, TILES])
        rstd = sb("rstd", [P, TILES])
        minus_half = sb("minus_half", [P, TILES])

        ident = sb("ident", [P, P])
        ident_b = sb("ident_b", [P, P], BF16)
        causal = sb("causal", [P, P], BF16)
        causal_t = sb("causal_t", [P, P], BF16)
        state_sel = sb("state_sel", [P, N_STATE, 3], BF16)
        rank8 = sb("rank8", [P, TILES, E])

        hidden_room = sb("hidden_room", [P, 8 * GT])
        rooms = [sb(f"room{n}", [P, 4 * GT]) for n in range(6)]
        room_s = sb("room_s", [P, 2 * GT])

        w = {}
        for name, shape, dt in [
            ("a0_w", [P, 2 * D], F32), ("a0_slope", [P, 1], F32),
            ("a1_w", [P, 10 * D], F32), ("a1_kbias", [P, HG, SEQ], F32), ("a1_qb", [P, HG], F32),
            ("a1_rows", [P, 4 * D], F32), ("a1_down", [P, 4], F32),
            ("a1_part", [3, 3], F32),
            ("a2_w", [P, 10 * D], F32), ("a2_kbias", [P, HG, SEQ], F32), ("a2_kb", [P, HG], F32), ("a2_qb", [P, HG], F32),
            ("a2_qc", [P, HG], F32), ("a2_rows", [P, 2 * D], F32),
            ("a3_win", [P, 4 * P], F32), ("a3_wx", [P, HALVES, 4 * P], F32), ("a3_wout", [P, HALVES, D], F32),
            ("a3_vec", [P, HALVES, TAPS + 3], F32), ("a3_alog", [P, HALVES, N_STATE], F32),
            ("f0_wr", [P, E], F32), ("f1_wr", [P, E], F32), ("f2_wr", [P, E], F32), ("f3_wr", [P, E], F32),
            ("f0_br", [P, TILES, E], F32), ("f1_br", [P, TILES, E], F32), ("f3_br", [P, TILES, E], F32),
            ("f0_b1", [P, E * 4], F32), ("f3_b1", [P, E * 4], F32), ("f0_b2", [E, D], F32), ("f3_b2", [E, D], F32),
            ("f0_ln", [P, 2 * D], F32),
            ("f1_up", [P, 2 * 256 + E * P], F32), ("f1_down", [P, (2 + E) * D], F32),
            ("f2_up", [P, (1 + E) * 512], F32), ("f2_down", [P, (1 + E) * 512], F32),
            ("f3_up", [P, E * 512], F32), ("f3_down", [P, E * 512], F32),
        ]:
            w[name] = sb(name, shape, dt)
        w["a0_rel"], w["a0_mask"] = rooms[4][:, 0:3 * P], rooms[4][:, 3 * P:6 * P]
        w["a1_across"], w["a1_inside"], a1_dist = (rooms[5][:, 2 * BW * n:2 * BW * (n + 1)].rearrange("p (a c) -> p a c", a=2)
                                                   for n in range(3))
        a1_dy = rooms[5][:, 6 * BW:7 * BW]
        w["f0_up"], w["f0_down"] = w["f3_up"], w["f3_down"]

        loaded = {k: sem(f"loaded_{k}") for k in ("x", "const", "a0", "f0", "a1", "f1", "a2", "f2", "a3", "f3")}
        setup = sem("setup")
        pool_setup = sem("pool_setup")
        act_setup = sem("act_setup")
        var_ready = sem("var_ready")
        rstd_ready = sem("rstd_ready")
        normed_ready = sem("normed_ready")
        xt_ready = sem("xt_ready")
        normed_t_ready = sem("normed_t_ready")
        stored = sem("stored")
        blocks = ("a0", "f0", "a1", "f1", "a2", "f2", "a3", "f3")
        steps = {k: sem(f"steps_{k}") for k in blocks}
        norms_per = {k: 2 for k in blocks} | {"f0": 3, "a1": 3}
        norms_before = {k: GROUPS * sum(norms_per[b] for b in blocks[:i]) for i, k in enumerate(blocks)}

        def norm_no(k, g, i):
            return norms_before[k] + g * norms_per[k] + i + 1

        def unit_no(k, g):
            return GROUPS * blocks.index(k) + g

        def moments(dve, rows, eps, link):
            for i in range(TILES):
                m = dve.bn_stats(stats[:, i, :], rows(i))
            link(m)
            total, apart, inner, outer = (spread_[:, n, :] for n in range(4))
            dve.tensor_tensor(total, stats[:, :, 1], stats[:, :, 4], ALU.add)
            dve.tensor_tensor(apart, stats[:, :, 1], stats[:, :, 4], ALU.subtract)
            link(dve.tensor_tensor(inner, stats[:, :, 2], stats[:, :, 5], ALU.add))
            dve.tensor_scalar(mean[:, :, 0], total, 0.5, None, ALU.mult)
            dve.tensor_scalar(inner, inner, 1.0 / D, eps, ALU.mult, ALU.add)
            link(dve.scalar_tensor_tensor(outer, apart, 0.25, apart, ALU.mult, ALU.mult))
            dve.tensor_tensor(var_eps[:, :], inner, outer, ALU.add).then_inc(var_ready, 1)

        def stream_tile(g, i):
            return stream[:, bass.ds(g * TILES + i, 1), :].rearrange("p a d -> p (a d)")

        def head_vector(dve, k, g, link):
            moments(dve, lambda i: stream_tile(g, i), LN_EPS, link)
            dve.wait_ge(rstd_ready, norm_no(k, g, 0))
            for i in range(TILES):
                dve.tensor_scalar(normed[:, i, :], stream_tile(g, i), mean[:, i, :], rstd[:, i:i + 1],
                                  ALU.subtract, ALU.mult).then_inc(normed_ready, 1)

        def head_tensor(pe, k, g):
            for i in range(TILES):
                pe.wait_ge(normed_ready, unit_no(k, g) * TILES + i + 1)
                pe.transpose(bank[:, 7, i * P:(i + 1) * P], normed[:, i, :], ident[:, :]).then_inc(xt_ready, 1)

        def head_scalar(act, k, g):
            act.wait_ge(xt_ready, unit_no(k, g) * TILES + TILES)
            act.activation(normed_t[:, :], bank[:, 7, :], ACT.Copy).then_inc(normed_t_ready, 1)

        def norm_of(dve, k, g, i, source, eps, link):
            moments(dve, lambda n: source[:, n, :], eps, link)
            dve.wait_ge(rstd_ready, norm_no(k, g, i))
            for n in range(TILES):
                m = dve.tensor_scalar(y[:, n, :], source[:, n, :], mean[:, n, :], rstd[:, n:n + 1],
                                      ALU.subtract, ALU.mult)
            link(m)

        def tail_vector(dve, k, g, link):
            norm_of(dve, k, g, norms_per[k] - 1, y, LN_EPS, link)
            rows = stream[:, bass.ds(g * TILES, TILES), :]
            link(dve.tensor_tensor(rows, rows, y[:, :, :], ALU.add))

        def loop(engine, body):
            with engine.Fori(0, GROUPS) as g:
                body(g)

        a0 = {k: sem(f"a0_{k}") for k in ("q_psum", "q", "v_psum", "v", "s_psum", "s", "p", "pt_psum", "pt", "o_psum")}
        a0_room = hidden_room[:, 0:2 * GT + 9 * PAIR * P]
        a0_q = a0_room[:, 0:GT]
        a0_v = a0_room[:, GT:2 * GT].rearrange("p (t d) -> p t d", d=D)
        a0_s, a0_p, a0_pt = (a0_room[:, 2 * GT + n * 3 * PAIR * P:2 * GT + (n + 1) * 3 * PAIR * P]
                             .rearrange("p (b c) -> p b c", b=PAIR) for n in range(3))
        a0_bias = sb("a0_bias", [P, 3 * P])
        row_max = sb("row_max", [P, TILES])
        row_sum = sb("row_sum", [P, TILES])
        row_rec = sb("row_rec", [P, TILES])

        def a0_tensor(pe, g):
            head_tensor(pe, "a0", g)
            pe.wait_ge(normed_t_ready, unit_no("a0", g) + 1)
            pe.matmul(bank[:, 0, :], w["a0_w"][:, 0:D], normed_t[:, :], start=True, stop=True).then_inc(a0["q_psum"], 1)
            for i in range(TILES):
                m = pe.matmul(bank[:, 1, i * D:(i + 1) * D], normed_t[:, i * P:(i + 1) * P], w["a0_w"][:, D:2 * D],
                              start=True, stop=True)
            m.then_inc(a0["v_psum"], 1)
            pe.wait_ge(a0["q"], g + 1)
            for b in range(PAIR):
                at = b * SEQ
                pe.matmul(bank[:, 2 + b, 0:P], a0_q[:, at:at + P], normed_t[:, at:at + P], start=True, stop=True)
                pe.matmul(bank[:, 2 + b, P:3 * P], a0_q[:, at + P:at + 2 * P], normed_t[:, at:at + 2 * P],
                          start=True, stop=True).then_inc(a0["s_psum"], 1)
            for b in range(PAIR):
                pe.wait_ge(a0["p"], (g * PAIR + b) * 2 + 2)
                for n in range(3):
                    m = pe.transpose(bank[:, 4 + b, n * P:(n + 1) * P], a0_p[:, b, n * P:(n + 1) * P], ident[:, :])
                m.then_inc(a0["pt_psum"], 1)
            pe.wait_ge(a0["v"], g + 1)
            for b in range(PAIR):
                pe.wait_ge(a0["pt"], g * PAIR + b + 1)
                o = bank[:, 6, b * 2 * D:(b + 1) * 2 * D]
                pe.matmul(o[:, 0:D], a0_pt[:, b, 0:P], a0_v[:, 2 * b, :], start=True, stop=True)
                pe.matmul(o[:, D:2 * D], a0_pt[:, b, P:2 * P], a0_v[:, 2 * b, :], start=True, stop=False)
                pe.matmul(o[:, D:2 * D], a0_pt[:, b, 2 * P:3 * P], a0_v[:, 2 * b + 1, :], start=False,
                          stop=True).then_inc(a0["o_psum"], 1)

        def a0_scalar(act, g):
            head_scalar(act, "a0", g)
            act.wait_ge(a0["q_psum"], g + 1)
            act.activation(a0_q[:, :], bank[:, 0, :], ACT.Copy, scale=float(D) ** -0.5).then_inc(a0["q"], 1)
            for b in range(PAIR):
                act.wait_ge(a0["s"], (g * PAIR + b) * 2 + 2)
                for n, (lo, hi) in enumerate(((0, P), (P, 3 * P))):
                    r = 2 * b + n
                    act.activation(a0_p[:, b, lo:hi], a0_s[:, b, lo:hi], ACT.Exp, bias=row_max[:, r:r + 1],
                                   accum_out=row_sum[:, r:r + 1]).then_inc(a0["p"], 1)
            for b in range(PAIR):
                act.wait_ge(a0["pt_psum"], g * PAIR + b + 1)
                act.activation(a0_pt[:, b, :], bank[:, 4 + b, 0:3 * P], ACT.Copy).then_inc(a0["pt"], 1)

        def a0_vector(dve, g):
            link = Steps(dve, steps["a0"], g, STEPS["a0"])
            head_vector(dve, "a0", g, link)
            dve.wait_ge(a0["v_psum"], g + 1)
            dve.tensor_copy(a0_v[:, :, :], bank[:, 1, :].rearrange("p (t d) -> p t d", d=D)).then_inc(a0["v"], 1)
            for b in range(PAIR):
                dve.wait_ge(a0["s_psum"], g * PAIR + b + 1)
                link(dve.tensor_tensor(a0_s[:, b, :], bank[:, 2 + b, 0:3 * P], a0_bias[:, :], ALU.add))
                for n, (lo, hi) in enumerate(((0, P), (P, 3 * P))):
                    r = 2 * b + n
                    dve.tensor_reduce(row_max[:, r:r + 1], a0_s[:, b, lo:hi], AX_X, ALU.max, negate=True)\
                       .then_inc(a0["s"], 1)
            dve.wait_ge(a0["p"], (g * PAIR + PAIR) * 2)
            link(dve.reciprocal(row_rec[:, :], row_sum[:, :]))
            dve.wait_ge(a0["o_psum"], (g + 1) * PAIR)
            for i in range(TILES):
                link(dve.tensor_scalar(y[:, i, :], bank[:, 6, i * D:(i + 1) * D], row_rec[:, i:i + 1], None, ALU.mult))
            tail_vector(dve, "a0", g, link)
            link.close()

        mh_q = rooms[0][:, :].rearrange("p (g t) -> p g t", g=HG)
        mh_k = rooms[1][:, :].rearrange("p (g t) -> p g t", g=HG)
        mh_v = rooms[2][:, :].rearrange("p (t h r) -> p t h r", t=TILES, h=HEADS)
        mh_max = rooms[3][:, :].rearrange("p (t g r) -> p t g r", t=TILES, g=HG)
        mh_p = rooms[4][:, :].rearrange("p (j c) -> p j c", j=4)
        mh_ot = rooms[5][:, :].rearrange("p (n q) -> p n q", q=SEQ)
        mh_rec = sb("mh_rec", [P, TILES, HEADS])
        mh_on = room_s[:, 0:GT].rearrange("p (t h d) -> p t h d", t=TILES, h=HEADS)
        mh_ont = room_s[:, GT:2 * GT]
        a1_bias3 = sb("a1_bias3", [P, 3, BW], BF16)
        a1_last3 = sb("a1_last3", [P, BW], BF16)
        a1_one3 = sb("a1_one3", [P, P], BF16)
        far = sb("far", [P, 1])
        far_all = sb("far_all", [P, 1])
        dy_sem = sem("dy_sem")
        MH_SEMS = ("q_psum", "q", "k_psum", "k", "v_psum", "v", "s_psum", "max", "maxt_psum", "q_full", "st_psum",
                   "p", "ot_psum", "ot", "otb_psum", "on", "ont_psum", "ont", "proj")
        mh = {k: {s: sem(f"{k}_{s}") for s in MH_SEMS} for k in ("a1", "a2")}

        def mh_tensor(pe, k, g):
            s, masked, wt = mh[k], k == "a2", w[f"{k}_w"]
            head_tensor(pe, k, g)
            pe.wait_ge(normed_t_ready, unit_no(k, g) + 1)
            for hg in range(HG):
                pe.matmul(bank[:, hg, :], wt[:, hg * P:(hg + 1) * P], normed_t[:, :], start=True, stop=True)\
                  .then_inc(s["q_psum"], 1)
            for n, hg in enumerate(range(HG)):
                b = [4, 5, 6, 0][n]
                if n == 3:
                    pe.wait_ge(s["q"], g * HG + 1)
                pe.matmul(bank[:, b, :], wt[:, (HG + hg) * P:(HG + hg + 1) * P], normed_t[:, :], start=True, stop=True)\
                  .then_inc(s["k_psum"], 1)
            for i in range(TILES):
                m = pe.matmul(bank[:, 7, i * D:(i + 1) * D], normed_t[:, i * P:(i + 1) * P], wt[:, 8 * D:9 * D],
                              start=True, stop=True)
            m.then_inc(s["v_psum"], 1)
            pe.wait_ge(s["q"], (g + 1) * HG)
            pe.wait_ge(s["k"], (g + 1) * HG)
            pe.wait_ge(s["v"], g + 1)
            for n in range(PAIR * HG):
                b, hg = divmod(n, HG)
                if n >= 2:
                    pe.wait_ge(s["max"], g * PAIR * HG + n - 1)
                for qt in range(2):
                    for j in range(4):
                        rows = slice(QUAD * j, QUAD * j + HROWS)
                        keys = P * (qt + 1) if masked else SEQ
                        to = bank[:, 4 * (n % 2) + j, qt * SEQ:qt * SEQ + keys]
                        at = b * SEQ
                        m = pe.matmul(to, mh_q[rows, hg, at + qt * P:at + (qt + 1) * P], mh_k[rows, hg, at:at + keys],
                                      start=True, stop=not masked)
                    if masked:
                        for j in range(4):
                            to = bank[:, 4 * (n % 2) + j, qt * SEQ + qt * P:qt * SEQ + (qt + 1) * P]
                            m = pe.matmul(to, ident_b[:, :], causal[:, :], start=False, stop=True)
                m.then_inc(s["s_psum"], 1)
            for hg in range(HG):
                if hg == 0:
                    pe.wait_ge(s["max"], (g + 1) * PAIR * HG)
                for i in range(TILES):
                    m = pe.transpose(bank[:, hg, i * P:(i + 1) * P], mh_max[:, i, hg, :], ident[:, :])
                m.then_inc(s["maxt_psum"], 1)

            def transposed_scores(n):
                b, hg = divmod(n, HG)
                at = b * SEQ
                if n == 0:
                    pe.wait_ge(s["q_full"], (g + 1) * HG)
                for j in range(4):
                    rows = slice(QUAD * j, QUAD * j + HROWS)
                    if n > 0:
                        pe.wait_ge(s["p"], g * PAIR * HEADS + 4 * (n - 1) + j + 1)
                    k0, k1 = mh_k[rows, hg, at:at + P], mh_k[rows, hg, at + P:at + 2 * P]
                    if masked:
                        pe.matmul(bank[:, j, 0:SEQ], k0, mh_q[rows, hg, at:at + SEQ], start=True, stop=False)
                        pe.matmul(bank[:, j, 0:P], ident_b[:, :], causal_t[:, :], start=False, stop=True)
                        pe.matmul(bank[:, j, SEQ:3 * P], k1, mh_q[rows, hg, at + P:at + SEQ], start=False, stop=False,
                                  skip_group_check=True)
                        m = pe.matmul(bank[:, j, SEQ:3 * P], ident_b[:, :], causal_t[:, :], start=False, stop=True,
                                      skip_group_check=True)
                    else:
                        pe.matmul(bank[:, j, 0:SEQ], k0, mh_q[rows, hg, at:at + SEQ], start=True, stop=False)
                        for part in range(3):
                            pe.matmul(bank[:, j, 0:BW], ident_b[:, :], a1_bias3[:, part, :], start=False,
                                      stop=part == 2)
                        pe.matmul(bank[:, j, SEQ:2 * SEQ], k1, mh_q[rows, hg, at:at + SEQ], start=False, stop=False,
                                  skip_group_check=True)
                        m = pe.matmul(bank[:, j, SEQ:SEQ + BW], a1_one3[:, :], a1_last3[:, :], start=False, stop=True,
                                      skip_group_check=True)
                    m.then_inc(s["st_psum"], 1)

            def weighted_values(n):
                b, hg = divmod(n, HG)
                pe.wait_ge(s["p"], g * PAIR * HEADS + 4 * n + 4)
                to = bank[:, 4 + n // 2, (n % 2) * SEQ:(n % 2 + 1) * SEQ]
                for kt in range(2):
                    for j in range(4):
                        rows = slice(QUAD * j, QUAD * (j + 1))
                        v = mh_v[:, 2 * b + kt, 4 * hg + j, :]
                        if masked and kt:
                            m = pe.matmul(to[rows, P:SEQ], v, mh_p[:, j, SEQ:3 * P], start=False, stop=True,
                                          skip_group_check=True)
                        else:
                            m = pe.matmul(to[rows, :], v, mh_p[:, j, kt * SEQ:(kt + 1) * SEQ], start=kt == 0,
                                          stop=kt == 1, skip_group_check=True)
                m.then_inc(s["ot_psum"], 1)

            transposed_scores(0)
            for n in range(PAIR * HG):
                weighted_values(n)
                if n + 1 < PAIR * HG:
                    transposed_scores(n + 1)
            for i in range(TILES):
                b, qt = divmod(i, 2)
                pe.wait_ge(s["ot"], g * PAIR * 2 + 2 * b + 2)
                for hg in range(HG):
                    m = pe.transpose(bank[:, i, hg * P:(hg + 1) * P], mh_ot[:, b * HG + hg, qt * P:(qt + 1) * P], ident[:, :])
                m.then_inc(s["otb_psum"], 1)
            for i in range(TILES):
                pe.wait_ge(s["on"], g * TILES + i + 1)
                m = pe.transpose(bank[:, 4, i * P:(i + 1) * P], mh_on[:, i, :, :].rearrange("p h d -> p (h d)"), ident[:, :])
            m.then_inc(s["ont_psum"], 1)
            pe.wait_ge(s["ont"], g + 1)
            for i in range(TILES):
                m = pe.matmul(bank[:, 5, i * D:(i + 1) * D], mh_ont[:, i * P:(i + 1) * P], wt[:, 9 * D:10 * D],
                              start=True, stop=True)
            m.then_inc(s["proj"], 1)

        def mh_scalar(act, k, g):
            s, masked = mh[k], k == "a2"
            head_scalar(act, k, g)
            for hg in range(HG):
                act.wait_ge(s["q_psum"], g * HG + hg + 1)
                act.activation(mh_q[:, hg, :], bank[:, hg, :], ACT.Identity, bias=w[f"{k}_qb"][:, hg:hg + 1],
                               scale=float(HD) ** -0.5).then_inc(s["q"], 1)
            for n in range(PAIR * HG):
                width = 3 * P if masked else 2 * SEQ
                if n > 0:
                    act.wait_ge(s["ot_psum"], g * PAIR * HG + n)
                for j in range(4):
                    act.wait_ge(s["st_psum"], (g * PAIR * HG + n) * 4 + j + 1)
                    act.activation(mh_p[:, j, 0:width], bank[:, j, 0:width], ACT.Exp).then_inc(s["p"], 1)
                if n % 2 and n > 1:
                    copy_ot(act, s, g, n // 2 - 1)
            copy_ot(act, s, g, PAIR * HG // 2 - 1)
            act.wait_ge(s["ont_psum"], g + 1)
            act.activation(mh_ont[:, :], bank[:, 4, :], ACT.Copy).then_inc(s["ont"], 1)

        def copy_ot(act, s, g, m):
            act.wait_ge(s["ot_psum"], g * PAIR * HG + 2 * m + 2)
            act.activation(mh_ot[:, 2 * m:2 * m + 2, :].rearrange("p a b -> p (a b)"), bank[:, 4 + m, :], ACT.Copy)\
               .then_inc(s["ot"], 1)

        def mh_vector(dve, k, g):
            s, masked = mh[k], k == "a2"
            link = Steps(dve, steps[k], g, STEPS[k])
            head_vector(dve, k, g, link)
            for n, hg in enumerate(range(HG)):
                dve.wait_ge(s["k_psum"], g * HG + hg + 1)
                dve.tensor_tensor(mh_k[:, hg, :].rearrange("p (b t) -> p b t", b=PAIR),
                                  bank[:, [4, 5, 6, 0][n], :].rearrange("p (b t) -> p b t", b=PAIR),
                                  w[f"{k}_kbias"][:, hg:hg + 1, :].to_broadcast([P, PAIR, SEQ]), ALU.add)\
                   .then_inc(s["k"], 1)
            dve.wait_ge(s["v_psum"], g + 1)
            for i in range(TILES):
                m = dve.tensor_tensor(mh_v[:, i, :, 0:HD], bank[:, 7, i * D:(i + 1) * D].rearrange("p (h d) -> p h d", d=HD),
                                      w[f"{k}_rows"][:, 0:D].rearrange("p (h d) -> p h d", d=HD), ALU.add)
            m.then_inc(s["v"], 1)
            for n in range(PAIR * HG):
                b, hg = divmod(n, HG)
                dve.wait_ge(s["s_psum"], g * PAIR * HG + n + 1)
                first = bank[:, 4 * (n % 2):4 * (n % 2) + 4, :]
                to = mh_max[:, 2 * b:2 * b + 2, hg, :].rearrange("p i (j r) -> p i j r", r=QUAD)
                for qt in range(2):
                    keys = P * (qt + 1) if masked else SEQ
                    m = dve.tensor_reduce(to[:, qt, :, ROW_MAX], first[:, :, qt * SEQ:qt * SEQ + keys], AX_X, ALU.max,
                                          negate=True)
                m.then_inc(s["max"], 1)
            for hg in range(HG):
                dve.wait_ge(s["maxt_psum"], g * HG + hg + 1)
                dve.tensor_tensor(mh_q[:, hg, :], bank[:, hg, :], mh_q[:, hg, :], ALU.add).then_inc(s["q_full"], 1)
            if k == "a1":
                norm_of(dve, k, g, 1, normed, LN_EPS, link)
                rows = w["a1_rows"]
                link(dve.tensor_tensor(y[:, :, :], y[:, :, :], rows[:, None, D:2 * D].to_broadcast([P, TILES, D]), ALU.mult))
                link(dve.tensor_tensor(y[:, :, :], y[:, :, :], rows[:, None, 2 * D:3 * D].to_broadcast([P, TILES, D]), ALU.add))
            for i in range(TILES):
                dve.wait_ge(s["otb_psum"], g * TILES + i + 1)
                parts = bank[:, i, :].rearrange("p (h r) -> p h r", r=QUAD)
                link(dve.reciprocal(mh_rec[:, i, :], parts[:, :, HD]))
                dve.tensor_tensor(mh_on[:, i, :, :], parts[:, :, 0:HD], mh_rec[:, i, :, None].to_broadcast([P, HEADS, HD]),
                                  ALU.mult).then_inc(s["on"], 1)
            dve.wait_ge(s["proj"], g + 1)
            if k == "a1":
                link(dve.tensor_tensor(y[:, :, :], bank[:, 5, :].rearrange("p (t d) -> p t d", d=D), y[:, :, :], ALU.add))
                link(dve.tensor_tensor(y[:, :, :], y[:, :, :],
                                       w["a1_rows"][:, None, 3 * D:4 * D].to_broadcast([P, TILES, D]), ALU.add))
            else:
                link(dve.tensor_tensor(y[:, :, :], bank[:, 5, :].rearrange("p (t d) -> p t d", d=D),
                                       w["a2_rows"][:, None, D:2 * D].to_broadcast([P, TILES, D]), ALU.add))
            tail_vector(dve, k, g, link)
            link.close()

        hidden = hidden_room[:, :].rearrange("p (i f t) -> p i f t", i=2, f=4)
        logits = sb("logits", [P, TILES, E])
        sel = sb("sel", [P, TILES, E])
        work = sb("work", [P, TILES, E])
        work2 = sb("work2", [P, TILES, E])
        hot1 = sb("hot1", [P, TILES, E])
        hot2 = sb("hot2", [P, TILES, E])
        gates = sb("gates", [P, TILES, E])
        gates_t = sb("gates_t", [E, GT])
        top = sb("top", [P, 8, TILES])
        silu1 = room_s[:, :].rearrange("p (f t) -> p f t", f=2)
        MOE_SEMS = ("logit_psum", "exp_in", "exp_out", "gates", "gt_psum", "gt", "b2_psum", "up_psum", "hidden", "down_psum", "added", "silu", "shared")
        moe = {k: {s: sem(f"{k}_{s}") for s in MOE_SEMS} for k in ("f0", "f1", "f2", "f3")}

        EXPERTS = {"f0": [(4, e) for e in range(E)], "f1": [(2, None)] + [(1, e) for e in range(E)],
                   "f2": [(4, None)] + [(4, e) for e in range(E)], "f3": [(4, e) for e in range(E)]}

        def up_tiles(k, i):
            return sum((2 if k == "f1" and gate is None else 1) * n for n, gate in EXPERTS[k][:i])

        def hid_tiles(k, i):
            return sum(n for n, _ in EXPERTS[k][:i])

        def moe_tensor(pe, k, g):
            s, ex, up, down = moe[k], EXPERTS[k], w[f"{k}_up"], w[f"{k}_down"]
            n_shared = 4 if k == "f1" else 0
            own = up_tiles(k, len(ex)) - n_shared
            head_tensor(pe, k, g)
            pe.wait_ge(normed_t_ready, unit_no(k, g) + 1)
            for i in range(TILES):
                m = pe.matmul(bank[:, 6, i * E:(i + 1) * E], normed_t[:, i * P:(i + 1) * P], w[f"{k}_wr"][:, :],
                              start=True, stop=True)
            m.then_inc(s["logit_psum"], 1)

            def up_to(i):
                n_tiles, gate = ex[i]
                n_up = 2 * n_tiles if k == "f1" and gate is None else n_tiles
                for f in range(n_up):
                    u = up_tiles(k, i) + f
                    if u >= 4:
                        if k == "f1" and u < 6:
                            pe.wait_ge(s["silu"], g * 2 + u - 4 + 1)
                        elif k == "f1" and u < 8:
                            pe.wait_ge(s["shared"], g * 2 + u - 6 + 1)
                        else:
                            pe.wait_ge(s["hidden"], g * own + u - 4 - n_shared + 1)
                    pe.matmul(bank[:, u % 4, :], up[:, u * P:(u + 1) * P], normed_t[:, :], start=True, stop=True)\
                      .then_inc(s["up_psum"], 1)

            def down_from(i):
                n_tiles, _ = ex[i]
                h0 = hid_tiles(k, i)
                if k == "f1" and i == 0:
                    pe.wait_ge(s["shared"], (g + 1) * 2)
                else:
                    pe.wait_ge(s["hidden"], g * own + up_tiles(k, i) + n_tiles - n_shared)
                if i >= 2:
                    pe.wait_ge(s["added"], g * len(ex) + i - 1)
                for t_ in range(TILES):
                    for f in range(n_tiles):
                        m = pe.matmul(bank[:, 4 + i % 2, t_ * D:(t_ + 1) * D], hidden[:, i % 2, f, t_ * P:(t_ + 1) * P],
                                      down[:, (h0 + f) * D:(h0 + f + 1) * D], start=f == 0, stop=f == n_tiles - 1)
                m.then_inc(s["down_psum"], 1)

            up_to(0)
            for i in range(len(ex)):
                if i + 1 < len(ex):
                    up_to(i + 1)
                if i == 0 and k in ("f0", "f3"):
                    pe.wait_ge(s["gates"], g + 1)
                    for t_ in range(TILES):
                        m = pe.transpose(bank[0:E, 7, t_ * P:(t_ + 1) * P], gates[:, t_, :], ident[:, :])
                    m.then_inc(s["gt_psum"], 1)
                    pe.wait_ge(s["gt"], g + 1)
                    for t_ in range(TILES):
                        m = pe.matmul(bank[:, 6, t_ * D:(t_ + 1) * D], gates_t[:, t_ * P:(t_ + 1) * P], w[f"{k}_b2"][:, :],
                                      start=True, stop=True)
                    m.then_inc(s["b2_psum"], 1)
                down_from(i)

        def moe_scalar(act, k, g):
            s, ex = moe[k], EXPERTS[k]
            ups = up_tiles(k, len(ex))
            head_scalar(act, k, g)
            if k == "f1":
                act.wait_ge(s["exp_in"], g + 1)
                act.activation(work[:, :, :], logits[:, :, :], ACT.Exp, scale=-1.0).then_inc(s["exp_out"], 1)
            elif k == "f2":
                act.wait_ge(s["exp_in"], g + 1)
                act.activation(work[:, :, :], work[:, :, :], ACT.Exp).then_inc(s["exp_out"], 1)
            else:
                act.wait_ge(s["exp_in"], g + 1)
                act.activation(top[:, 5, :], top[:, 4, :], ACT.Exp).then_inc(s["exp_out"], 1)
            for i, (n_tiles, gate) in enumerate(ex):
                if k == "f1" and gate is None:
                    for f in range(n_tiles):
                        act.wait_ge(s["up_psum"], g * ups + f + 1)
                        act.activation(silu1[:, f, :], bank[:, f, :], ACT.Silu).then_inc(s["silu"], 1)
                    continue
                if i >= 2:
                    act.wait_ge(s["down_psum"], g * len(ex) + i - 1)
                for f in range(n_tiles):
                    u = up_tiles(k, i) + f
                    act.wait_ge(s["up_psum"], g * ups + u + 1)
                    func = ACT.Relu if k == "f3" else ACT.Gelu
                    if k in ("f0", "f3"):
                        m = act.activation(hidden[:, i % 2, f, :], bank[:, u % 4, :], func, bias=w[f"{k}_b1"][:, u:u + 1])
                    else:
                        m = act.activation(hidden[:, i % 2, f, :], bank[:, u % 4, :], func)
                    m.then_inc(s["hidden"], 1)

        def moe_vector(dve, k, g):
            s, ex = moe[k], EXPERTS[k]
            ups = up_tiles(k, len(ex))
            link = Steps(dve, steps[k], g, STEPS[k])
            head_vector(dve, k, g, link)
            dve.wait_ge(s["logit_psum"], g + 1)
            logit_psum = bank[:, 6, 0:TILES * E].rearrange("p (t e) -> p t e", e=E)

            def spread(a):
                return a[:, :, None].to_broadcast([P, TILES, E])

            def top_one(scores, best, hot):
                link(dve.tensor_reduce(best, scores, AX_X, ALU.max))
                link(dve.tensor_tensor(work2[:, :, :], scores, spread(best), ALU.is_ge))
                link(dve.tensor_tensor(work2[:, :, :], work2[:, :, :], rank8[:, :, :], ALU.mult))
                link(dve.tensor_reduce(top[:, 7, :], work2[:, :, :], AX_X, ALU.max))
                link(dve.tensor_tensor(hot, work2[:, :, :], spread(top[:, 7, :]), ALU.is_equal))

            def top_two(scores):
                top_one(scores, top[:, 0, :], hot1[:, :, :])
                link(dve.scalar_tensor_tensor(sel[:, :, :], hot1[:, :, :], BELOW, scores, ALU.mult, ALU.add))
                top_one(sel[:, :, :], top[:, 1, :], hot2[:, :, :])

            if k in ("f0", "f3"):
                link(dve.tensor_tensor(logits[:, :, :], logit_psum, w[f"{k}_br"][:, :, :], ALU.add))
                top_two(logits[:, :, :])
                dve.tensor_tensor(top[:, 4, :], top[:, 1, :], top[:, 0, :], ALU.subtract).then_inc(s["exp_in"], 1)
                dve.wait_ge(s["exp_out"], g + 1)
                link(dve.tensor_scalar(top[:, 6, :], top[:, 5, :], 1.0, None, ALU.add))
                link(dve.reciprocal(top[:, 2, :], top[:, 6, :]))
                link(dve.tensor_tensor(top[:, 3, :], top[:, 5, :], top[:, 2, :], ALU.mult))
                link(dve.tensor_tensor(hot1[:, :, :], hot1[:, :, :], spread(top[:, 2, :]), ALU.mult))
                link(dve.tensor_tensor(hot2[:, :, :], hot2[:, :, :], spread(top[:, 3, :]), ALU.mult))
                dve.tensor_tensor(gates[:, :, :], hot1[:, :, :], hot2[:, :, :], ALU.add).then_inc(s["gates"], 1)
                dve.wait_ge(s["gt_psum"], g + 1)
                dve.tensor_copy(gates_t[:, :], bank[0:E, 7, :]).then_inc(s["gt"], 1)
                dve.wait_ge(s["b2_psum"], g + 1)
                if k == "f0":
                    link(dve.tensor_tensor(y[:, :, :], bank[:, 6, :].rearrange("p (t d) -> p t d", d=D), normed[:, :, :], ALU.add))
                else:
                    link(dve.tensor_copy(y[:, :, :], bank[:, 6, :].rearrange("p (t d) -> p t d", d=D)))
            elif k == "f1":
                dve.tensor_copy(logits[:, :, :], logit_psum).then_inc(s["exp_in"], 1)
                dve.wait_ge(s["exp_out"], g + 1)
                link(dve.tensor_scalar(work[:, :, :], work[:, :, :], 1.0, None, ALU.add))
                link(dve.reciprocal(gates[:, :, :], work[:, :, :]))
                link(dve.tensor_tensor(logits[:, :, :], gates[:, :, :], w["f1_br"][:, :, :], ALU.add))
                top_two(logits[:, :, :])
                link(dve.tensor_tensor(hot1[:, :, :], hot1[:, :, :], hot2[:, :, :], ALU.add))
                link(dve.tensor_tensor(gates[:, :, :], gates[:, :, :], hot1[:, :, :], ALU.mult))
                link(dve.tensor_reduce(top[:, 2, :], gates[:, :, :], AX_X, ALU.add))
                link(dve.tensor_scalar(top[:, 3, :], top[:, 2, :], 1e-9, None, ALU.is_gt))
                link(dve.tensor_scalar(top[:, 4, :], top[:, 2, :], 1e-9, None, ALU.add))
                link(dve.reciprocal(top[:, 5, :], top[:, 4, :]))
                link(dve.tensor_tensor(top[:, 5, :], top[:, 5, :], top[:, 3, :], ALU.mult))
                link(dve.tensor_scalar(top[:, 6, :], top[:, 3, :], -0.5, 0.5, ALU.mult, ALU.add))
                link(dve.tensor_tensor(gates[:, :, :], gates[:, :, :], spread(top[:, 5, :]), ALU.mult))
                link(dve.tensor_tensor(hot1[:, :, :], hot1[:, :, :], spread(top[:, 6, :]), ALU.mult))
                link(dve.tensor_tensor(gates[:, :, :], gates[:, :, :], hot1[:, :, :], ALU.add))
                for f in range(2):
                    dve.wait_ge(s["silu"], g * 2 + f + 1)
                    dve.wait_ge(s["up_psum"], g * ups + 2 + f + 1)
                    dve.tensor_tensor(hidden[:, 0, f, :], bank[:, 2 + f, :], silu1[:, f, :], ALU.mult).then_inc(s["shared"], 1)
            else:
                link(dve.tensor_reduce(top[:, 2, :], logit_psum, AX_X, ALU.max))
                dve.tensor_tensor(work[:, :, :], logit_psum, spread(top[:, 2, :]), ALU.subtract).then_inc(s["exp_in"], 1)
                dve.wait_ge(s["exp_out"], g + 1)
                link(dve.tensor_reduce(top[:, 3, :], work[:, :, :], AX_X, ALU.add))
                link(dve.reciprocal(top[:, 4, :], top[:, 3, :]))
                link(dve.tensor_tensor(logits[:, :, :], work[:, :, :], spread(top[:, 4, :]), ALU.mult))
                top_two(logits[:, :, :])
                link(dve.tensor_tensor(hot1[:, :, :], hot1[:, :, :], hot2[:, :, :], ALU.add))
                link(dve.tensor_tensor(gates[:, :, :], logits[:, :, :], hot1[:, :, :], ALU.mult))

            for i, (_, gate) in enumerate(ex):
                dve.wait_ge(s["down_psum"], g * len(ex) + i + 1)
                for t_ in range(TILES):
                    part = bank[:, 4 + i % 2, t_ * D:(t_ + 1) * D]
                    if gate is not None:
                        m = dve.scalar_tensor_tensor(y[:, t_, :], part, gates[:, t_, gate:gate + 1], y[:, t_, :],
                                                     ALU.mult, ALU.add)
                    elif k == "f1":
                        m = dve.tensor_copy(y[:, t_, :], part)
                    else:
                        m = dve.tensor_tensor(y[:, t_, :], part, normed[:, t_, :], ALU.add)
                m.then_inc(s["added"], 1)
                dve.wait_ge(s["added"], g * len(ex) + i + 1)
            if k == "f0":
                norm_of(dve, k, g, 1, y, 1e-12, link)
                link(dve.tensor_tensor(y[:, :, :], y[:, :, :], w["f0_ln"][:, None, 0:D].to_broadcast([P, TILES, D]), ALU.mult))
                link(dve.tensor_tensor(y[:, :, :], y[:, :, :], w["f0_ln"][:, None, D:2 * D].to_broadcast([P, TILES, D]), ALU.add))
            tail_vector(dve, k, g, link)
            link.close()

        ROW = HALVES * GT
        SSM_SEMS = ("in_psum", "x_raw", "conv", "xc", "bc_psum", "dt_psum", "v", "e", "w1", "ln", "dt", "bc", "y0",
                    "bb", "cb", "decay", "c_sb", "dbx", "h", "hc", "y_part", "y_all", "yz", "proj")
        ss = {s: sem(f"a3_{s}") for s in SSM_SEMS}
        def halves(a):
            return a.rearrange("p (h t) -> p h t", h=HALVES)

        def two(a):
            return a.rearrange("p (i h t) -> p i h t", i=2, h=HALVES)

        hs, hc, decay = two(rooms[0][:, :]), two(rooms[1][:, :]), two(rooms[4][:, :])
        xc, zs = halves(rooms[5][:, 0:ROW]), halves(rooms[5][:, ROW:2 * ROW])
        dt_s, u_in = halves(rooms[3][:, 0:ROW]), halves(rooms[3][:, ROW:2 * ROW])
        c_sb = halves(room_s[:, :])
        raw_words = HALVES * PAIR * (TAPS - 1 + SEQ)
        x_raw = rooms[2][:, 0:raw_words].rearrange("p (h b t) -> p h b t", h=HALVES, b=PAIR)
        bc_stack = rooms[2][:, 4 * GT - 3 * GT // 2:].bitcast(BF16).rearrange("p (c t) -> p c t", c=3)
        assert raw_words + 3 * GT // 2 <= 4 * GT
        a_neg = sb("a_neg", [P, HALVES, N_STATE])
        d_diag = sb("d_diag", [P, HALVES, P])
        tmp_a, tmp_b, tmp_c = hs[:, 0, :, :], hs[:, 1, :, :], hc[:, 0, :, :]
        vec = w["a3_vec"]
        DT_BIAS, CONV_B, SKIP = TAPS, TAPS + 1, TAPS + 2

        def ssm_tensor(pe, g):
            head_tensor(pe, "a3", g)
            pe.wait_ge(normed_t_ready, unit_no("a3", g) + 1)
            for n in range(4):
                pe.matmul(bank[:, n, :], w["a3_win"][:, n * P:(n + 1) * P], normed_t[:, :], start=True, stop=True)\
                  .then_inc(ss["in_psum"], 1)
            pe.wait_ge(ss["xc"], (g + 1) * HALVES)
            for n in range(4):
                for h in range(HALVES):
                    m = pe.matmul(bank[:, 4 + n, :], w["a3_wx"][:, h, n * P:(n + 1) * P], xc[:, h, :],
                                  start=h == 0, stop=h == HALVES - 1)
                m.then_inc(ss["bc_psum"], 1)
            for h in range(HALVES):
                m = pe.matmul(bank[:, h, :], d_diag[:, h, :], xc[:, h, :], start=True, stop=False, skip_group_check=True)
            m.then_inc(ss["y0"], 1)
            pe.wait_ge(ss["bc"], g + 1)

            def spread(n, i):
                for c, done in ((0, "bb"), (1, "cb")):
                    to = bank[:, 4 + 2 * c + i, :]
                    pe.matmul(to, sel_at(n, 0), bc_stack[:, c, :], start=True, stop=False)
                    pe.matmul(to, sel_at(n, 1 + c), bc_stack[:, 2, :], start=False, stop=True).then_inc(ss[done], 1)

            def sel_at(n, c):
                return state_sel[:, bass.ds(n, 1), c].to_broadcast([P, P])

            def collect(n, i):
                pe.wait_ge(ss["hc"], g * N_STATE + n + 1)
                for h in range(HALVES):
                    m = pe.matmul(bank[:, h, :], ident[:, :], hc[:, i, h, :], start=False, stop=False, skip_group_check=True)
                m.then_inc(ss["y_part"], 1)

            for n in range(2):
                spread(n, n)
            with pe.Fori(0, N_STATE // 2 - 1) as n2:
                for i in range(2):
                    n = n2 * 2 + i
                    pe.wait_ge(ss["dbx"], g * N_STATE + n + 1)
                    pe.wait_ge(ss["c_sb"], g * N_STATE + n + 1)
                    spread(n + 2, i)
                    collect(n, i)
            for i in range(2):
                collect(N_STATE - 2 + i, i)
            pe.wait_ge(ss["yz"], (g + 1) * HALVES)
            for t_ in range(TILES):
                for h in range(HALVES):
                    m = pe.matmul(bank[:, 4, t_ * D:(t_ + 1) * D], xc[:, h, t_ * P:(t_ + 1) * P], w["a3_wout"][:, h, :],
                                  start=h == 0, stop=h == HALVES - 1)
            m.then_inc(ss["proj"], 1)

        def ssm_scalar(act, g):
            head_scalar(act, "a3", g)
            for h in range(HALVES):
                act.wait_ge(ss["in_psum"], g * 4 + h + 1)
                act.activation(x_raw[:, h, :, TAPS - 1:], bank[:, h, :].rearrange("p (b t) -> p b t", b=PAIR), ACT.Copy)\
                   .then_inc(ss["x_raw"], 1)
            for h in range(HALVES):
                act.wait_ge(ss["in_psum"], g * 4 + 2 + h + 1)
                act.activation(zs[:, h, :], bank[:, 2 + h, :], ACT.Silu)
            for h in range(HALVES):
                act.wait_ge(ss["conv"], g * HALVES + h + 1)
                act.activation(xc[:, h, :], u_in[:, h, :], ACT.Silu, bias=vec[:, h, CONV_B:CONV_B + 1]).then_inc(ss["xc"], 1)
            act.wait_ge(ss["v"], (g + 1) * HALVES)
            act.activation(tmp_b, tmp_b, ACT.Exp, scale=-1.0).then_inc(ss["e"], 1)
            act.wait_ge(ss["w1"], g + 1)
            act.activation(u_in[:, :, :], tmp_c, ACT.Ln).then_inc(ss["ln"], 1)
            act.wait_ge(ss["dt"], g + 1)

            def one(n, i, first):
                if not first:
                    act.wait_ge(ss["h"], g * N_STATE + n - 1)
                for h in range(HALVES):
                    m = act.activation(decay[:, i, h, :].rearrange("p (b t) -> p b t", b=PAIR)[:, :, 1:],
                                       dt_s[:, h, :].rearrange("p (b t) -> p b t", b=PAIR)[:, :, 1:], ACT.Exp,
                                       scale=a_neg[:, h, bass.ds(n, 1)])
                m.then_inc(ss["decay"], 1)
                act.wait_ge(ss["cb"], g * N_STATE + n + 1)
                if not first:
                    act.wait_ge(ss["hc"], g * N_STATE + n - 1)
                act.activation(c_sb[:, i, :], bank[:, 6 + i, :], ACT.Copy).then_inc(ss["c_sb"], 1)

            for i in range(2):
                one(i, i, True)
            with act.Fori(1, N_STATE // 2) as n2:
                for i in range(2):
                    one(n2 * 2 + i, i, False)

        def ssm_pool(pool, g):
            def one(n, i):
                pool.wait_ge(ss["h"], g * N_STATE + n + 1)
                pool.wait_ge(ss["c_sb"], g * N_STATE + n + 1)
                pool.tensor_tensor(hc[:, i, :, :], hs[:, i, :, :], c_sb[:, i:i + 1, :].to_broadcast([P, HALVES, GT]), ALU.mult)\
                    .then_inc(ss["hc"], 1)

            for i in range(2):
                one(i, i)
            with pool.Fori(1, N_STATE // 2) as n2:
                for i in range(2):
                    pool.wait_ge(ss["y_part"], g * N_STATE + n2 * 2 + i - 1)
                    one(n2 * 2 + i, i)

        def ssm_vector(dve, g):
            link = Steps(dve, steps["a3"], g, STEPS["a3"])
            head_vector(dve, "a3", g, link)
            for h in range(HALVES):
                dve.wait_ge(ss["x_raw"], g * HALVES + h + 1)
                acc = u_in[:, h, :].rearrange("p (b t) -> p b t", b=PAIR)
                for k in range(TAPS):
                    x_k = x_raw[:, h, :, k:k + SEQ]
                    if k == 0:
                        link(dve.tensor_scalar(acc, x_k, vec[:, h, 0:1], None, ALU.mult))
                    elif k < TAPS - 1:
                        link(dve.scalar_tensor_tensor(acc, x_k, vec[:, h, k:k + 1], acc, ALU.mult, ALU.add))
                    else:
                        dve.scalar_tensor_tensor(acc, x_k, vec[:, h, k:k + 1], acc, ALU.mult, ALU.add).then_inc(ss["conv"], 1)
            dve.wait_ge(ss["bc_psum"], g * 4 + 4)
            for h in range(HALVES):
                link(dve.tensor_scalar(tmp_a[:, h, :], bank[:, 7, :], vec[:, h, DT_BIAS:DT_BIAS + 1], None, ALU.add))
                dve.scalar_tensor_tensor(tmp_b[:, h, :], tmp_a[:, h, :], -1.0, tmp_a[:, h, :], ALU.mult, ALU.max).then_inc(ss["v"], 1)
            for c in range(2):
                src = bank[:, 4 + c, :]
                link(dve.tensor_copy(bc_stack[:, c, :], src))
                link(dve.tensor_tensor(tmp_c[:, 0, :], src, bc_stack[:, c, :], ALU.subtract))
                link(dve.tensor_copy(bc_stack[P // 2:P, c, :], tmp_c[P // 2:P, 0, :]))
            src = bank[:, 6, :]
            low = bc_stack[:, 2, :]
            link(dve.tensor_copy(low, src))
            link(dve.tensor_tensor(tmp_c[:, 0, :], src, low, ALU.subtract))
            link(dve.tensor_copy(low, tmp_c[:, 0, :]))
            link(dve.tensor_tensor(tmp_c[:, 1, :], tmp_c[:, 0, :], low, ALU.subtract))
            dve.tensor_copy(low, tmp_c[:, 1, :]).then_inc(ss["bc"], 1)
            dve.wait_ge(ss["e"], g + 1)
            dve.wait_ge(ss["bc"], g + 1)
            dve.tensor_scalar(tmp_c, tmp_b, 1.0, None, ALU.add).then_inc(ss["w1"], 1)
            dve.wait_ge(ss["ln"], g + 1)
            link(dve.tensor_scalar(tmp_c, tmp_c, 1.0, TINY, ALU.subtract, ALU.max))
            link(dve.reciprocal(tmp_c, tmp_c))
            link(dve.scalar_tensor_tensor(u_in[:, :, :], u_in[:, :, :], TINY, tmp_b, ALU.max, ALU.mult))
            link(dve.tensor_tensor(tmp_c, u_in[:, :, :], tmp_c, ALU.mult))
            dve.scalar_tensor_tensor(dt_s[:, :, :], tmp_a, 0.0, tmp_c, ALU.max, ALU.add).then_inc(ss["dt"], 1)
            dve.wait_ge(ss["dt"], g + 1)
            link(dve.tensor_tensor(u_in[:, :, :], dt_s[:, :, :], xc[:, :, :], ALU.mult))

            dbx = bank[:, 2:4, :]

            def one(n, i, first):
                dve.wait_ge(ss["bb"], g * N_STATE + n + 1)
                if not first:
                    dve.wait_ge(ss["h"], g * N_STATE + n)
                dve.tensor_tensor(dbx, u_in[:, :, :], bank[:, 4 + i:5 + i, :].to_broadcast([P, HALVES, GT]), ALU.mult)\
                   .then_inc(ss["dbx"], 1)
                dve.wait_ge(ss["dbx"], g * N_STATE + n + 1)
                dve.wait_ge(ss["decay"], g * N_STATE + n + 1)
                if not first:
                    dve.wait_ge(ss["hc"], g * N_STATE + n - 1)
                dve.tensor_tensor_scan(hs[:, i, :, :].rearrange("p h t -> p (h t)"),
                                       decay[:, i, :, :].rearrange("p h t -> p (h t)"),
                                       dbx.rearrange("p h t -> p (h t)"), 0.0, ALU.mult, ALU.add).then_inc(ss["h"], 1)

            one(0, 0, True)
            dve.wait_ge(ss["h"], g * N_STATE + 1)
            one(1, 1, True)
            with dve.Fori(1, N_STATE // 2) as n2:
                for i in range(2):
                    one(n2 * 2 + i, i, False)
            dve.wait_ge(ss["y_part"], (g + 1) * N_STATE)
            for h in range(HALVES):
                dve.tensor_tensor(xc[:, h, :], bank[:, h, :], zs[:, h, :], ALU.mult).then_inc(ss["yz"], 1)
            dve.wait_ge(ss["proj"], g + 1)
            link(dve.tensor_copy(y[:, :, :], bank[:, 4, :].rearrange("p (t d) -> p t d", d=D)))
            tail_vector(dve, "a3", g, link)
            link.close()

        with_x = t["x"].rearrange("(g t p) d -> g p t d", t=TILES, p=P)
        out_x = out.rearrange("(g t p) d -> g p t d", t=TILES, p=P)
        LOADS = {
            "const": ["ident", "rank8", "causal2", "state_sel"],
            "a0": ["a0_w", "a0_rel", "a0_mask", "a0_slope"],
            "f0": ["f0_wr", "f0_br", "f0_b1", "f0_b2", "f0_ln", "f0_up", "f0_down"],
            "a1": ["a1_w", "a1_kbias", "a1_qb", "a1_rows", "a1_across", "a1_down", "a1_inside", "a1_part"],
            "f1": ["f1_wr", "f1_br", "f1_up", "f1_down"],
            "a2": ["a2_w", "a2_kbias", "a2_kb", "a2_qb", "a2_qc", "a2_rows"],
            "f2": ["f2_wr", "f2_up", "f2_down"],
            "a3": ["a3_win", "a3_wx", "a3_wout", "a3_vec", "a3_alog"],
            "f3": ["f3_wr", "f3_br", "f3_b1", "f3_b2", "f3_up", "f3_down"],
        }
        causal2_f = rooms[0][:, 0:2 * P].rearrange("p (a c) -> p a c", a=2)
        state_sel_f = rooms[1][:, 0:3 * N_STATE].rearrange("p (n c) -> p n c", c=3)
        tiles = dict(w, ident=ident, rank8=rank8, causal2=causal2_f, state_sel=state_sel_f)

        def need(engine, *names):
            for k in names:
                engine.wait_ge(loaded[k], 16 * (GROUPS if k == "x" else len(LOADS[k])))

        block = ctx.enter_context(nc.Block())

        @block.sync
        def _(sp):
            for g in range(GROUPS):
                sp.dma_start(stream[:, g * TILES:(g + 1) * TILES, :], with_x[g]).then_inc(loaded["x"], 16)
            for k, names in LOADS.items():
                if k == "f3":
                    sp.wait_ge(moe["f0"]["down_psum"], GROUPS * E)
                for name in names:
                    to = tiles[name]
                    sp.dma_start(to[tuple([slice(None)] * len(to.shape))], t[name]).then_inc(loaded[k], 16)
            sp.wait_ge(steps["f3"], GROUPS * STEPS["f3"])
            for g in range(GROUPS):
                sp.dma_start(out_x[g], stream[:, g * TILES:(g + 1) * TILES, :]).then_inc(stored, 16)
            sp.wait_ge(stored, 16 * GROUPS)

        SETUP_SQUARES, SETUP_MAX, SETUP_ALL = 16, 17, 37

        @block.gpsimd
        def _(pool):
            pool.memset(minus_half[:, :], -0.5).then_inc(pool_setup, 1)
            pool.wait_ge(setup, SETUP_MAX)
            pool.partition_all_reduce(far_all[:, :], far[:, :], P, bass.bass_isa.ReduceOp.max).then_inc(pool_setup, 1)

            def norms(k, g, n, m):
                for i in range(n, m):
                    pool.wait_ge(var_ready, norm_no(k, g, i))
                    pool.tensor_tensor(rstd[:, :], var_eps[:, :], minus_half[:, :], ALU.pow).then_inc(rstd_ready, 1)

            pool.wait_ge(pool_setup, 2)
            for k in blocks:
                with pool.Fori(0, GROUPS) as g:
                    norms(k, g, 0, 1)
                    if k == "a3":
                        ssm_pool(pool, g)
                    norms(k, g, 1, norms_per[k])

        @block.scalar
        def _(act):
            act.wait_ge(setup, SETUP_SQUARES)
            act.activation(a1_dist[:, :, :], a1_dist[:, :, :], ACT.Sqrt).then_inc(act_setup, 1)
            need(act, "a3")
            act.activation(a_neg[:, :, :], w["a3_alog"][:, :, :], ACT.Exp).then_inc(act_setup, 1)
            act.wait_ge(setup, SETUP_ALL)
            need(act, "f0", "a1", "a2")
            for k in blocks:
                if k == "f3":
                    need(act, "f3")
                with act.Fori(0, GROUPS) as g:
                    if k == "a0":
                        a0_scalar(act, g)
                    elif k in ("a1", "a2"):
                        mh_scalar(act, k, g)
                    elif k == "a3":
                        ssm_scalar(act, g)
                    else:
                        moe_scalar(act, k, g)

        @block.tensor
        def _(pe):
            pe.wait_ge(setup, SETUP_ALL)
            for k in blocks:
                need(pe, k)
                with pe.Fori(0, GROUPS) as g:
                    if k == "a0":
                        a0_tensor(pe, g)
                    elif k in ("a1", "a2"):
                        mh_tensor(pe, k, g)
                    elif k == "a3":
                        ssm_tensor(pe, g)
                    else:
                        moe_tensor(pe, k, g)

        @block.vector
        def _(dve):
            link = Steps(dve, setup, 0, SETUP_ALL)
            link(dve.memset(rooms[2][:, :], 0.0))
            link(dve.memset(mh_v[:, :, :, HD:HD + 1], 1.0))
            link(dve.memset(rooms[3][:, :], 0.0))
            dve.memset(a1_last3[:, :], 0.0)
            link(dve.memset(a1_one3[:, :], 0.0))
            link(dve.memset(a1_one3[:, 0:1], 1.0))
            need(dve, "const", "a0", "a1", "a2", "a3")
            link(dve.tensor_copy(ident_b[:, :], ident[:, :]))
            link(dve.tensor_copy(causal[:, :], causal2_f[:, 0, :]))
            link(dve.tensor_copy(causal_t[:, :], causal2_f[:, 1, :]))
            link(dve.tensor_copy(state_sel[:, :, :], state_sel_f))
            link(dve.scalar_tensor_tensor(a0_bias[:, :], w["a0_rel"][:, :], w["a0_slope"][:, 0:1], w["a0_mask"][:, :],
                                          ALU.mult, ALU.add))
            for n in range(2):
                dx, dy = a1_dist[:, n, :], a1_dy[:, :]
                link(dve.tensor_scalar(dx, w["a1_across"][:, 0, :], w["a1_down"][:, 2 * n:2 * n + 1], None, ALU.subtract))
                link(dve.tensor_tensor(dx, dx, dx, ALU.mult))
                dve.tensor_scalar(dy, w["a1_across"][:, 1, :], w["a1_down"][:, 2 * n + 1:2 * n + 2], None, ALU.subtract)\
                   .then_inc(dy_sem, 1)
                dve.wait_ge(dy_sem, 2 * n + 1)
                dve.tensor_tensor(dy, dy, dy, ALU.mult).then_inc(dy_sem, 1)
                dve.wait_ge(dy_sem, 2 * n + 2)
                link(dve.tensor_tensor(dx, dx, dy, ALU.add))
            assert link.n == SETUP_SQUARES
            dve.wait_ge(act_setup, 1)
            link(dve.tensor_reduce(far[:, :], a1_dist[:, :, :].rearrange("p a c -> p (a c)"), AX_X, ALU.max))
            assert link.n == SETUP_MAX
            dve.wait_ge(pool_setup, 2)
            link(dve.tensor_scalar(far[:, :], far_all[:, :], 1e-6, -0.1, ALU.is_gt, ALU.mult))
            link(dve.tensor_scalar(far_all[:, :], far_all[:, :], 1e-6, None, ALU.max))
            link(dve.reciprocal(far_all[:, :], far_all[:, :]))
            link(dve.tensor_tensor(far[:, :], far[:, :], far_all[:, :], ALU.mult))
            link(dve.scalar_tensor_tensor(a1_dist[:, :, :], a1_dist[:, :, :], far[:, 0:1], w["a1_inside"][:, :, :],
                                          ALU.mult, ALU.mult))
            for part in range(3):
                link(dve.tensor_copy(a1_bias3[:, part, :], a1_dist[:, 0, :]))
                if part < 2:
                    link(dve.tensor_tensor(a1_dist[:, 0, :], a1_dist[:, 0, :], a1_bias3[:, part, :], ALU.subtract))
            link(dve.memset(a1_dy[0:3, :], 0.0))
            for part in range(3):
                dve.tensor_copy(a1_last3[0:3, :], a1_dist[0:3, 1, :]).then_inc(dy_sem, 1)
                dve.wait_ge(dy_sem, 4 + 3 * part + 1)
                dve.scalar_tensor_tensor(a1_dy[0:3, :], a1_last3[0:3, :], w["a1_part"][:, part:part + 1], a1_dy[0:3, :],
                                         ALU.mult, ALU.add).then_inc(dy_sem, 1)
                dve.tensor_tensor(a1_dist[0:3, 1, :], a1_dist[0:3, 1, :], a1_last3[0:3, :], ALU.subtract).then_inc(dy_sem, 1)
                dve.wait_ge(dy_sem, 4 + 3 * part + 3)
            link(dve.tensor_copy(a1_last3[0:3, :], a1_dy[0:3, :]))
            for hg in range(HG):
                link(dve.tensor_scalar(w["a2_kbias"][:, hg, :], w["a2_kbias"][:, hg, :], w["a2_kb"][:, hg:hg + 1], None, ALU.add))
            link(dve.scalar_tensor_tensor(w["a2_qb"][:, :], w["a2_qb"][:, :], float(HD) ** -0.5, w["a2_qc"][:, :],
                                          ALU.mult, ALU.add))
            dve.wait_ge(act_setup, 2)
            link(dve.tensor_scalar(a_neg[:, :, :], a_neg[:, :, :], -1.0, None, ALU.mult))
            for h in range(HALVES):
                link(dve.tensor_scalar(d_diag[:, h, :], ident[:, :], vec[:, h, SKIP:SKIP + 1], None, ALU.mult))
            link.close()
            need(dve, "x", "f0", "f1")
            for k in blocks:
                if k == "f3":
                    need(dve, "f3")
                if k == "a3":
                    dve.memset(x_raw[:, :, :, 0:TAPS - 1], 0.0).then_inc(dy_sem, 1)
                    dve.memset(rooms[4][:, :].rearrange("p (r t) -> p r t", t=SEQ)[:, :, 0:1], 0.0).then_inc(dy_sem, 1)
                with dve.Fori(0, GROUPS) as g:
                    if k == "a0":
                        a0_vector(dve, g)
                    elif k in ("a1", "a2"):
                        mh_vector(dve, k, g)
                    elif k == "a3":
                        ssm_vector(dve, g)
                    else:
                        moe_vector(dve, k, g)


def heads_apart(mat):
    out = np.zeros((mat.shape[0], HG, 4, QUAD), mat.dtype)
    out[..., 0:HD] = mat.reshape(-1, HG, 4, HD)
    return out.reshape(mat.shape[0], HG * P)


def arrange(a):
    f = np.float32

    def cat(*parts):
        return np.concatenate(parts, axis=1)

    def rows(*vs):
        return np.broadcast_to(np.concatenate(vs)[None, :], (P, sum(len(v) for v in vs)))

    def tiled(v):
        return np.broadcast_to(v[None, None, :], (P, TILES, E))

    def halves(mat):
        return mat.reshape(HALVES, P, -1).transpose(1, 0, 2)

    t = {"x": a["L0_attn_x"].reshape(-1, D)}
    pos = np.arange(P)
    late = (pos[None, :] > pos[:, None])
    t["ident"] = np.eye(P, dtype=f)
    t["rank8"] = tiled(np.arange(E, 0, -1).astype(f))
    t["causal2"] = np.stack([late * f(MASKED), late.T * f(MASKED)], axis=1).astype(f)
    state = np.arange(N_STATE)
    t["state_sel"] = np.stack([pos[:, None] % N_STATE == state, pos[:, None] == state, pos[:, None] == state + N_STATE],
                              axis=2).astype(f)
    rel = (pos[None, :] - pos[:, None]).astype(f)
    t["a0_rel"] = cat(rel, rel - P, rel)
    t["a0_mask"] = cat(late * f(BELOW), 0 * late, late * f(BELOW)).astype(f)
    t["a0_slope"] = np.broadcast_to(a["L0_attn_alibi_slope"][None, :], (P, 1))
    t["a0_w"] = cat(a["L0_attn_W_qk"], a["L0_attn_W_v"].T)

    ones_row = np.zeros((4, QUAD), f)
    ones_row[:, ROW_MAX] = 1
    wq, wk, wv = a["L1_attn_W_qkv"].reshape(3, D, D).transpose(0, 2, 1)
    t["a1_w"] = cat(heads_apart(wq), heads_apart(wk), wv, a["L1_attn_W_proj"].T)
    t["a1_kbias"] = np.broadcast_to(ones_row.reshape(P, 1, 1), (P, HG, SEQ))
    t["a1_qb"] = np.zeros((P, HG), f)
    t["a1_rows"] = rows(np.zeros(D, f), a["L1_attn_ln_gamma"], a["L1_attn_ln_beta"], a["L1_attn_b_proj"])
    at = np.clip(np.arange(BW) - 1, 0, P - 1)
    c = a["L1_attn_spatial_centers"]
    t["a1_across"] = np.broadcast_to(c[at].T[None], (P, 2, BW))
    t["a1_down"] = cat(c[at[0:P]], np.broadcast_to(c[P - 1][None], (P, 2)))
    inside = np.zeros((P, 2, BW), f)
    inside[1:, 0, 1:P + 1] = 1
    inside[:, 1, 1:P + 1] = 1
    t["a1_inside"] = inside
    t["a1_part"] = np.eye(3, dtype=f)

    t["a2_w"] = cat(heads_apart(a["L2_attn_Wq"]), heads_apart(a["L2_attn_Wk"]), a["L2_attn_Wv"], a["L2_attn_Wo"])
    kbias = np.zeros((HG, 4, QUAD, SEQ), f)
    kbias[:, :, ROW_MAX, :] = 1
    start = 2 ** (-2 ** (-(np.log2(HEADS) - 3)))
    slopes = np.array([start * start ** i for i in range(HEADS)]).astype(f).reshape(HG, 4)
    kbias[:, :, ROW_POS, :] = slopes[:, :, None] * (np.arange(SEQ) - (SEQ - 1)).astype(f)
    t["a2_kbias"] = kbias.reshape(HG, P, SEQ).transpose(1, 0, 2)
    t["a2_kb"] = heads_apart(a["L2_attn_bk"][None]).reshape(HG, P).T
    t["a2_qb"] = heads_apart(a["L2_attn_bq"][None]).reshape(HG, P).T
    pos_row = np.zeros((4, QUAD), f)
    pos_row[:, ROW_POS] = 1
    t["a2_qc"] = np.broadcast_to(pos_row.reshape(P, 1), (P, HG))
    t["a2_rows"] = rows(a["L2_attn_bv"], a["L2_attn_bo"])

    t["a3_win"] = a["L3_attn_W_in"]
    wx = a["L3_attn_W_x"]
    b_, c_, d_ = wx[:, 0:N_STATE], wx[:, N_STATE:2 * N_STATE], wx[:, 2 * N_STATE:]
    t["a3_wx"] = halves(cat(b_, b_, c_, c_, b_, c_, np.broadcast_to(d_, (HALVES * P, P))))
    t["a3_wout"] = halves(a["L3_attn_W_out"])
    t["a3_vec"] = halves(cat(a["L3_attn_conv_w"], a["L3_attn_dt_bias"][:, None], a["L3_attn_conv_b"][:, None],
                             a["L3_attn_D"][:, None]))
    t["a3_alog"] = halves(a["L3_attn_A_log"])

    def up(m):
        return m.transpose(1, 0, 2).reshape(D, -1)

    def down(m):
        return m.reshape(-1, P, D).transpose(1, 0, 2).reshape(P, -1)

    t["f0_wr"], t["f0_br"] = a["L0_ffn_Wr"].T, tiled(a["L0_ffn_br"])
    t["f0_up"], t["f0_down"] = up(a["L0_ffn_W1"].transpose(0, 2, 1)), down(a["L0_ffn_W2"].transpose(0, 2, 1))
    t["f0_b1"], t["f0_b2"] = a["L0_ffn_b1"].reshape(-1, P).T, a["L0_ffn_b2"]
    t["f0_ln"] = rows(a["L0_ffn_ln_w"], a["L0_ffn_ln_b"])
    t["f1_wr"], t["f1_br"] = a["L1_ffn_router_w"].T, tiled(a["L1_ffn_router_bias"])
    t["f1_up"] = cat(a["L1_ffn_sw1"], a["L1_ffn_sw3"], up(a["L1_ffn_ew1"]))
    t["f1_down"] = cat(down(a["L1_ffn_sw2"]), down(a["L1_ffn_ew2"]))
    t["f2_wr"] = a["L2_ffn_router_w"]
    t["f2_up"] = cat(up(a["L2_ffn_shared_up"]), up(a["L2_ffn_routed_up"]))
    t["f2_down"] = cat(down(a["L2_ffn_shared_down"]), down(a["L2_ffn_routed_down"]))
    t["f3_wr"], t["f3_br"] = a["L3_ffn_Wr"], tiled(a["L3_ffn_br"])
    t["f3_up"], t["f3_down"] = up(a["L3_ffn_W1"]), down(a["L3_ffn_W2"])
    t["f3_b1"], t["f3_b2"] = a["L3_ffn_b1"].reshape(-1, P).T, a["L3_ffn_b2"]
    return t


def kernel(**inputs):
    import concourse.bacc as bacc
    from concourse.bass_utils import run_bass_kernel_spmd

    nc = bacc.Bacc("TRN2", target_bir_lowering=False, num_devices=1)
    arrays = {k: np.ascontiguousarray(v) for k, v in arrange({k: np.asarray(v) for k, v in inputs.items()}).items()}
    t = {k: nc.dram_tensor(f"in_{k}", v.shape, mybir.dt.from_np(v.dtype), kind="ExternalInput").ap()
         for k, v in arrays.items()}
    out = nc.dram_tensor("out_x", (NSEQ * SEQ, D), F32, kind="ExternalOutput").ap()
    build(nc, t, out)
    r = run_bass_kernel_spmd(nc, [{f"in_{k}": v for k, v in arrays.items()}], core_ids=[0])
    return r.results[0]["out_x"].reshape(NSEQ, SEQ, D)
```

```python
from contextlib import ExitStack

import numpy as np

import concourse.bass as bass
from concourse import mybir

ALU = mybir.AluOpType
ACT = mybir.ActivationFunctionType
F32 = mybir.dt.float32
BF16 = mybir.dt.bfloat16
AX_X = mybir.AxisListType.X

P = 128
D = 128
SEQ = 256
NSEQ = 8
GT = 512
GROUPS = NSEQ * SEQ // GT
TILES = GT // P
PAIR = GT // SEQ
HEADS = 16
HD = D // HEADS
QUAD = 32
HG = HEADS // 4
PARTS = 3
BLOCK = PARTS * HD
PRODUCTS = PARTS * BLOCK
E = 8
N_STATE = 64
HALVES = 2
TAPS = 4
LN_EPS = 1e-5
BW = P + 2
MASKED = -1e30
BELOW = -3e38


class Steps:

    def __init__(self, engine, sem, g, per):
        self.engine, self.sem, self.g, self.per, self.n = engine, sem, g, per, 0

    def __call__(self, instruction):
        instruction.then_inc(self.sem, 1)
        self.n += 1
        self.engine.wait_ge(self.sem, self.g * self.per + self.n)

    def close(self, missing=0):
        assert self.n + missing == self.per, f"{self.n} linked steps, {self.per} stated"


HEAD = 3
NORM = HEAD + 1
TAIL = NORM + 1
SPLIT = 2 * (PARTS - 1)
TOP2 = 11
STEPS = {
    "a0": HEAD + PAIR + 1 + TILES + TAIL,
    "f0": HEAD + 1 + TOP2 + 5 + 1 + NORM + 2 + TAIL,
    "a1": HEAD + SPLIT + NORM + 2 + PAIR * SPLIT + TILES + 1 + TAIL,
    "f1": HEAD + 3 + TOP2 + 11 + TAIL,
    "a2": HEAD + SPLIT + PAIR * SPLIT + TILES + TAIL,
    "f2": HEAD + 1 + 3 + TOP2 + 2 + TAIL,
    "a3": HEAD + HALVES * (TAPS - 1) + HALVES + 2 + 1 + 1 + TAIL,
    "f3": HEAD + 1 + TOP2 + 5 + 1 + TAIL,
}


def build(nc, t, out):
    ctx = ExitStack()
    with ctx:
        def sb(name, shape, dt=F32):
            return ctx.enter_context(nc.sbuf_tensor(name, shape, dt))

        def sem(name):
            return ctx.enter_context(nc.semaphore(name))

        bank = ctx.enter_context(nc.psum_tensor("bank", [P, 8, 512], F32))

        stream = sb("stream", [P, GROUPS * TILES, D])
        normed = sb("normed", [P, TILES, D])
        normed_t = sb("normed_t", [P, GT])
        y = sb("y", [P, TILES, D])
        stats = sb("stats", [P, TILES, 6])
        mean = sb("mean", [P, TILES, 1])
        spread_ = sb("spread_", [P, 4, TILES])
        var_eps = sb("var_eps", [P, TILES])
        rstd = sb("rstd", [P, TILES])
        minus_half = sb("minus_half", [P, TILES])

        ident = sb("ident", [P, P])
        ident_b = sb("ident_b", [P, P], BF16)
        causal = sb("causal", [P, P], BF16)
        causal_t = sb("causal_t", [P, P], BF16)
        row_sel = sb("row_sel", [PARTS * QUAD, QUAD], BF16)
        rank8 = sb("rank8", [P, TILES, E])

        hidden_room = sb("hidden_room", [P, 8 * GT])
        rooms_ab = [sb(f"rooms_{n}", [P, 8 * GT]) for n in range(2)]
        rooms = [sb(f"room{n}", [P, 4 * GT]) for n in range(2)]
        rooms += [r[:, n * 4 * GT:(n + 1) * 4 * GT] for r in rooms_ab for n in range(2)]
        room_s = sb("room_s", [P, 2 * GT])

        w = {}
        for name, shape, dt in [
            ("a0_w", [P, 2 * D], F32), ("a0_slope", [P, 1], F32),
            ("a1_w", [P, 4 * D], F32),
            ("a1_rows", [P, 4 * D], F32), ("a1_down", [P, 4], F32),
            ("a1_part", [3, 3], F32),
            ("a2_w", [P, 4 * D], F32), ("a2_qkb", [P, 2], F32), ("part_masks", [P, PARTS - 1], F32),
            ("a2_rows", [P, 2 * D], F32),
            ("a3_win", [P, 4 * P], F32), ("a3_wx", [P, HALVES, 4 * P], F32), ("a3_wout", [P, HALVES, D], F32),
            ("a3_vec", [P, HALVES, TAPS + 3], F32), ("a3_alog", [P, HALVES, N_STATE], F32),
            ("f0_wr", [P, E], F32), ("f1_wr", [P, E], F32), ("f2_wr", [P, E], F32), ("f3_wr", [P, E], F32),
            ("f0_br", [P, TILES, E], F32), ("f1_br", [P, TILES, E], F32), ("f3_br", [P, TILES, E], F32),
            ("f0_b1", [P, E * 4], F32), ("f3_b1", [P, E * 4], F32), ("f0_b2", [E, D], F32), ("f3_b2", [E, D], F32),
            ("f0_ln", [P, 2 * D], F32),
            ("f1_up", [P, 2 * 256 + E * P], F32), ("f1_down", [P, (2 + E) * D], F32),
            ("f2_up", [P, (1 + E) * 512], F32), ("f2_down", [P, (1 + E) * 512], F32),
            ("f3_up", [P, E * 512], F32), ("f3_down", [P, E * 512], F32),
        ]:
            w[name] = sb(name, shape, dt)
        w["a0_rel"], w["a0_mask"] = rooms[2][:, 0:3 * P], rooms[2][:, 3 * P:6 * P]
        w["a2_pos"] = rooms[3][0:HEADS, 0:SEQ]
        w["a1_across"], w["a1_inside"], a1_dist = (rooms[5][:, 2 * BW * n:2 * BW * (n + 1)].rearrange("p (a c) -> p a c", a=2)
                                                   for n in range(3))
        a1_dy = rooms[5][:, 6 * BW:7 * BW]
        w["f0_up"], w["f0_down"] = w["f3_up"], w["f3_down"]

        loaded = {k: sem(f"loaded_{k}") for k in ("x", "const", "a0", "f0", "a1", "f1", "a2", "f2", "a3", "f3")}
        setup = sem("setup")
        pool_setup = sem("pool_setup")
        act_setup = sem("act_setup")
        head_var = sem("head_var")
        head_rstd = sem("head_rstd")
        var_ready = sem("var_ready")
        rstd_ready = sem("rstd_ready")
        normed_ready = sem("normed_ready")
        xt_ready = sem("xt_ready")
        normed_t_ready = sem("normed_t_ready")
        stored = sem("stored")
        blocks = ("a0", "f0", "a1", "f1", "a2", "f2", "a3", "f3")
        steps = {k: sem(f"steps_{k}") for k in blocks}
        first_steps = sem("first_steps")
        first_qk = sem("first_qk")
        norms_per = {k: 1 for k in blocks} | {"f0": 2, "a1": 2}
        norms_before = {k: GROUPS * sum(norms_per[b] for b in blocks[:i]) for i, k in enumerate(blocks)}

        def norm_no(k, g, i):
            return norms_before[k] + g * norms_per[k] + i + 1

        def unit_no(k, g):
            return GROUPS * blocks.index(k) + g

        def following(g):
            return (g + 1) % GROUPS

        def moments(dve, rows, eps, link, done):
            for i in range(TILES):
                m = dve.bn_stats(stats[:, i, :], rows(i))
            link(m)
            total, apart, inner, outer = (spread_[:, n, :] for n in range(4))
            dve.tensor_tensor(total, stats[:, :, 1], stats[:, :, 4], ALU.add)
            dve.tensor_tensor(apart, stats[:, :, 1], stats[:, :, 4], ALU.subtract)
            link(dve.tensor_tensor(inner, stats[:, :, 2], stats[:, :, 5], ALU.add))
            dve.tensor_scalar(mean[:, :, 0], total, 0.5, None, ALU.mult)
            dve.tensor_scalar(inner, inner, 1.0 / D, eps, ALU.mult, ALU.add)
            link(dve.scalar_tensor_tensor(outer, apart, 0.25, apart, ALU.mult, ALU.mult))
            dve.tensor_tensor(var_eps[:, :], inner, outer, ALU.add).then_inc(done, 1)

        def stream_tile(g, i):
            return stream[:, bass.ds(g * TILES + i, 1), :].rearrange("p a d -> p (a d)")

        def head_moments(dve, g, link):
            moments(dve, lambda i: stream_tile(g, i), LN_EPS, link, head_var)

        def head_normalize(dve, u, g):
            dve.wait_ge(head_rstd, u + 1)
            for i in range(TILES):
                dve.tensor_scalar(normed[:, i, :], stream_tile(g, i), mean[:, i, :], rstd[:, i:i + 1],
                                  ALU.subtract, ALU.mult).then_inc(normed_ready, 1)

        def head_vector(dve, u, g, link):
            head_moments(dve, g, link)
            head_normalize(dve, u, g)

        def head_pool(pool, u):
            pool.wait_ge(head_var, u + 1)
            pool.tensor_tensor(rstd[:, :], var_eps[:, :], minus_half[:, :], ALU.pow).then_inc(head_rstd, 1)

        def head_tensor(pe, u, b):
            for i in range(TILES):
                pe.wait_ge(normed_ready, u * TILES + i + 1)
                m = pe.transpose(bank[:, b, i * P:(i + 1) * P], normed[:, i, :], ident[:, :])
            m.then_inc(xt_ready, 1)

        def head_scalar(act, u, b):
            act.wait_ge(xt_ready, u + 1)
            act.activation(normed_t[:, :], bank[:, b, :], ACT.Copy).then_inc(normed_t_ready, 1)

        def norm_of(dve, k, g, i, source, eps, link):
            moments(dve, lambda n: source[:, n, :], eps, link, var_ready)
            dve.wait_ge(rstd_ready, norm_no(k, g, i))
            for n in range(TILES):
                m = dve.tensor_scalar(y[:, n, :], source[:, n, :], mean[:, n, :], rstd[:, n:n + 1],
                                      ALU.subtract, ALU.mult)
            link(m)

        def norm_pool(pool, k, g, i):
            pool.wait_ge(var_ready, norm_no(k, g, i))
            pool.tensor_tensor(rstd[:, :], var_eps[:, :], minus_half[:, :], ALU.pow).then_inc(rstd_ready, 1)

        def tail_vector(dve, k, g, link):
            norm_of(dve, k, g, norms_per[k] - 1, y, LN_EPS, link)
            rows = stream[:, bass.ds(g * TILES, TILES), :]
            link(dve.tensor_tensor(rows, rows, y[:, :, :], ALU.add))

        a0 = {k: sem(f"a0_{k}") for k in ("q_psum", "q", "v_psum", "v", "s_psum", "s", "p", "pt_psum", "pt", "o_psum")}
        a0_room = hidden_room[:, 0:2 * GT + 9 * PAIR * P]
        a0_q = a0_room[:, 0:GT]
        a0_v = a0_room[:, GT:2 * GT].rearrange("p (t d) -> p t d", d=D)
        a0_s, a0_p, a0_pt = (a0_room[:, 2 * GT + n * 3 * PAIR * P:2 * GT + (n + 1) * 3 * PAIR * P]
                             .rearrange("p (b c) -> p b c", b=PAIR) for n in range(3))
        a0_bias = sb("a0_bias", [P, 3 * P])
        row_max = sb("row_max", [P, TILES])
        row_sum = sb("row_sum", [P, TILES])
        row_rec = sb("row_rec", [P, TILES])

        def a0_tensor(pe, g):
            pe.wait_ge(normed_t_ready, unit_no("a0", g) + 1)
            pe.matmul(bank[:, 0, :], w["a0_w"][:, 0:D], normed_t[:, :], start=True, stop=True).then_inc(a0["q_psum"], 1)
            for i in range(TILES):
                m = pe.matmul(bank[:, 1, i * D:(i + 1) * D], normed_t[:, i * P:(i + 1) * P], w["a0_w"][:, D:2 * D],
                              start=True, stop=True)
            m.then_inc(a0["v_psum"], 1)
            pe.wait_ge(a0["q"], g + 1)
            for b in range(PAIR):
                at = b * SEQ
                pe.matmul(bank[:, 2 + b, 0:P], a0_q[:, at:at + P], normed_t[:, at:at + P], start=True, stop=True)
                pe.matmul(bank[:, 2 + b, P:3 * P], a0_q[:, at + P:at + 2 * P], normed_t[:, at:at + 2 * P],
                          start=True, stop=True).then_inc(a0["s_psum"], 1)
            for b in range(PAIR):
                pe.wait_ge(a0["p"], (g * PAIR + b) * 2 + 2)
                for n in range(3):
                    m = pe.transpose(bank[:, 4 + b, n * P:(n + 1) * P], a0_p[:, b, n * P:(n + 1) * P], ident[:, :])
                m.then_inc(a0["pt_psum"], 1)
            pe.wait_ge(a0["v"], g + 1)
            for b in range(PAIR):
                pe.wait_ge(a0["pt"], g * PAIR + b + 1)
                o = bank[:, 6, b * 2 * D:(b + 1) * 2 * D]
                pe.matmul(o[:, 0:D], a0_pt[:, b, 0:P], a0_v[:, 2 * b, :], start=True, stop=True)
                pe.matmul(o[:, D:2 * D], a0_pt[:, b, P:2 * P], a0_v[:, 2 * b, :], start=True, stop=False)
                pe.matmul(o[:, D:2 * D], a0_pt[:, b, 2 * P:3 * P], a0_v[:, 2 * b + 1, :], start=False,
                          stop=True).then_inc(a0["o_psum"], 1)
            head_tensor(pe, unit_no("a0", g) + 1, 7)

        def a0_scalar(act, g):
            act.wait_ge(a0["q_psum"], g + 1)
            act.activation(a0_q[:, :], bank[:, 0, :], ACT.Copy, scale=float(D) ** -0.5).then_inc(a0["q"], 1)
            for b in range(PAIR):
                act.wait_ge(a0["s"], (g * PAIR + b) * 2 + 2)
                for n, (lo, hi) in enumerate(((0, P), (P, 3 * P))):
                    r = 2 * b + n
                    act.activation(a0_p[:, b, lo:hi], a0_s[:, b, lo:hi], ACT.Exp, bias=row_max[:, r:r + 1],
                                   accum_out=row_sum[:, r:r + 1]).then_inc(a0["p"], 1)
            for b in range(PAIR):
                act.wait_ge(a0["pt_psum"], g * PAIR + b + 1)
                act.activation(a0_pt[:, b, :], bank[:, 4 + b, 0:3 * P], ACT.Copy).then_inc(a0["pt"], 1)
            head_scalar(act, unit_no("a0", g) + 1, 7)

        def a0_vector(dve, g):
            link = Steps(dve, steps["a0"], g, STEPS["a0"])
            dve.wait_ge(a0["v_psum"], g + 1)
            dve.tensor_copy(a0_v[:, :, :], bank[:, 1, :].rearrange("p (t d) -> p t d", d=D)).then_inc(a0["v"], 1)
            for b in range(PAIR):
                dve.wait_ge(a0["s_psum"], g * PAIR + b + 1)
                link(dve.tensor_tensor(a0_s[:, b, :], bank[:, 2 + b, 0:3 * P], a0_bias[:, :], ALU.add))
                for n, (lo, hi) in enumerate(((0, P), (P, 3 * P))):
                    r = 2 * b + n
                    dve.tensor_reduce(row_max[:, r:r + 1], a0_s[:, b, lo:hi], AX_X, ALU.max, negate=True)\
                       .then_inc(a0["s"], 1)
            head_vector(dve, unit_no("a0", g) + 1, following(g), link)
            dve.wait_ge(a0["p"], (g * PAIR + PAIR) * 2)
            link(dve.reciprocal(row_rec[:, :], row_sum[:, :]))
            dve.wait_ge(a0["o_psum"], (g + 1) * PAIR)
            for i in range(TILES):
                link(dve.tensor_scalar(y[:, i, :], bank[:, 6, i * D:(i + 1) * D], row_rec[:, i:i + 1], None, ALU.mult))
            tail_vector(dve, "a0", g, link)
            link.close()

        mh_room = room_s[:, :].rearrange("p (c t) -> p c t", c=2)
        mh_parts = sb("mh_parts", [P, 2, PARTS, GT], BF16)

        q_stack, k_stack = (r[:, :].bitcast(BF16).rearrange("p (h b t) -> p h b t", b=PAIR, h=HEADS) for r in rooms_ab)
        POS_ROWS = slice(PRODUCTS, PRODUCTS + PARTS)
        ROWS = 3 * QUAD
        MAX_ROWS = slice(ROWS, ROWS + PARTS)
        mh_v = rooms[0][:, :].rearrange("p (t h r) -> p t h r", t=TILES, h=HEADS)
        mh_max = sb("mh_max", [P, TILES, PARTS, QUAD])
        pos_b = sb("pos_b", [HEADS, PARTS, SEQ], BF16)
        pos_done = sem("pos_done")
        k_rows = sem("k_rows")
        max_f = sb("max_f", [PARTS * QUAD, GT])
        max_b = sb("max_b", [PARTS * QUAD, GT], BF16)
        mh_p = hidden_room[:, :].rearrange("p (j c) -> p j c", j=8)
        mh_ot = rooms[1][:, :].rearrange("p (n q) -> p n q", q=SEQ)
        ones_row = sb("ones_row", [1, P])
        mh_rec = sb("mh_rec", [P, TILES, HEADS])
        mh_on = hidden_room[:, 0:GT].rearrange("p (t h d) -> p t h d", t=TILES, h=HEADS)
        mh_ont = hidden_room[:, GT:2 * GT]
        q_scr = nc.dram_tensor("q_scr", [PARTS, HD, HEADS, GT], BF16).ap()
        k_scr = nc.dram_tensor("k_scr", [2 * PARTS - 1, HD, HEADS, GT], BF16).ap()
        pos_scr = nc.dram_tensor("pos_scr", [PARTS, HEADS, SEQ], BF16).ap()
        a1_bias3 = sb("a1_bias3", [P, 3, BW], BF16)
        a1_last3 = sb("a1_last3", [P, BW], BF16)
        a1_one3 = sb("a1_one3", [P, P], BF16)
        far = sb("far", [P, 1])
        far_all = sb("far_all", [P, 1])
        dy_sem = sem("dy_sem")
        MH_SEMS = ("q_psum", "q", "q_parts", "k_psum", "k", "k_round", "k_left", "v_psum", "v", "written", "stacked0", "stacked1",
                   "s_psum", "max", "max3", "maxt_psum", "max_parts", "max_rows", "st_psum",
                   "p", "ot_psum", "ot", "otb_psum", "on", "ont_psum", "ont", "proj", "proj_read")
        mh = {s: sem(f"mh_{s}") for s in MH_SEMS}

        REDUCES = 4 + 16

        def mh_unit(k, g):
            return g if k == "a1" else g + GROUPS

        def qk_tensor(pe, k, g):
            pe.wait_ge(normed_t_ready, unit_no(k, g) + 1)
            for c, name in enumerate(("q", "k")):
                pe.matmul(bank[:, 7 - c, :], w[f"{k}_w"][:, c * D:(c + 1) * D], normed_t[:, :], start=True, stop=True)\
                  .then_inc(mh[f"{name}_psum"], 1)

        def qk_scalar(act, k, g):
            s, masked, m0 = mh, k == "a2", mh_unit(k, g)
            for c, (name, scale) in enumerate((("q", float(HD) ** -0.5), ("k", 1.0))):
                act.wait_ge(s[f"{name}_psum"], m0 + 1)
                if masked:
                    m = act.activation(mh_room[:, c, :], bank[:, 7 - c, :], ACT.Identity, bias=w["a2_qkb"][:, c:c + 1],
                                       scale=scale)
                else:
                    m = act.activation(mh_room[:, c, :], bank[:, 7 - c, :], ACT.Copy, scale=scale)
                m.then_inc(s[name], 1)

        def round_keys(act, k, g, part):
            m0 = mh_unit(k, g)
            if part == 0:
                act.wait_ge(mh["k"], m0 + 1)
            else:
                act.wait_ge(mh["k_left"], m0 * (PARTS - 1) + part)
            act.activation(mh_parts[:, 1, part, :], mh_room[:, 1, :], ACT.Copy).then_inc(mh["k_round"], 1)

        def split_queries(dve, k, g, link):
            dve.wait_ge(mh["q"], mh_unit(k, g) + 1)
            left = mh_room[:, 0, :]
            for part in range(PARTS - 1):
                link(dve.tensor_copy(mh_parts[:, 0, part, :], left))
                link(dve.tensor_tensor(left, left, mh_parts[:, 0, part, :], ALU.subtract))
            dve.tensor_copy(mh_parts[:, 0, PARTS - 1, :], left).then_inc(mh["q_parts"], 1)

        def mh_tensor(pe, k, g, last):
            s, masked, m0, wt = mh, k == "a2", mh_unit(k, g), w[f"{k}_w"]
            rows, all_rows = slice(0, ROWS), slice(0, MAX_ROWS.stop)
            def row_scores(b, qt, h0, heads, at):
                keys = P * (qt + 1) if masked else SEQ
                for j in range(heads):
                    to = bank[:, at + j // 2, (j % 2) * SEQ:(j % 2) * SEQ + keys]
                    m = pe.matmul(to, q_stack[rows, h0 + j, b, qt * P:(qt + 1) * P], k_stack[rows, h0 + j, b, 0:keys],
                                  start=not (masked and j % 2), stop=True, skip_group_check=masked and j % 2 == 1)
                    if masked and j % 2:
                        both = bank[:, at + j // 2, :].rearrange("p (c k) -> p c k", c=2)[:, :, qt * P:(qt + 1) * P]
                        m = pe.matmul(both, ident_b[:, :], causal[:, None, :].to_broadcast([P, 2, P]),
                                      start=False, stop=True, skip_group_check=True)
                m.then_inc(s["s_psum"], 1)

            def turned_maxima(b, at):
                pe.wait_ge(s["max3"], m0 * PAIR + b + 1)
                for i in range(2):
                    m = pe.transpose(bank[0:PARTS * QUAD, at, i * P:(i + 1) * P],
                                     mh_max[:, 2 * b + i, :, :].rearrange("p a h -> p (a h)"), ident[:, :])
                m.then_inc(s["maxt_psum"], 1)

            pe.wait_ge(s["stacked0"], (m0 + 1) * 16 * 2 * PARTS)
            for n in range(4):
                if n >= 2:
                    pe.wait_ge(s["max"], m0 * REDUCES + n - 1)
                if n == 1:
                    pe.wait_ge(s["proj_read"], m0)
                row_scores(0, n // 2, 8 * (n % 2), 8, 4 * (n % 2))
            turned_maxima(0, 0)
            pe.wait_ge(s["k"], m0 + 1)
            for i in range(TILES):
                m = pe.matmul(bank[:, 6, i * D:(i + 1) * D], normed_t[:, i * P:(i + 1) * P], wt[:, 2 * D:3 * D],
                              start=True, stop=not masked)
                if masked:
                    m = pe.matmul(bank[:, 6, i * D:(i + 1) * D], ones_row[:, :], w["a2_rows"][0:1, 0:D], start=False, stop=True)
            m.then_inc(s["v_psum"], 1)

            def row_chunk(c):
                if c == 0:
                    pe.wait_ge(s["stacked1"], (m0 + 1) * 16 * 2 * PARTS)
                    pe.wait_ge(s["v"], m0 + 1)
                if c >= 2:
                    pe.wait_ge(s["max"], m0 * REDUCES + 4 + c - 1)
                row_scores(1, c // 8, 2 * (c % 8), 2, 6 + c % 2)

            def transposed_scores(n):
                b, hg = divmod(n, HG)
                if n in (0, HG):
                    pe.wait_ge(s["max_rows"], (m0 * PAIR + b + 1) * 16 * PARTS)
                for j in range(4):
                    h = 4 * hg + j
                    if n > 0:
                        pe.wait_ge(s["p"], m0 * PAIR * HEADS + 4 * (n - 1) + j + 1)
                    k0, k1 = k_stack[all_rows, h, b, 0:P], k_stack[all_rows, h, b, P:2 * P]
                    q = q_stack[all_rows, h, b, :]
                    pe.matmul(bank[:, j, 0:SEQ], k0, q, start=True, stop=True)
                    if masked:
                        pe.matmul(bank[:, j, 0:P], ident_b[:, :], causal_t[:, :], start=False, stop=False,
                                  skip_group_check=True)
                        pe.matmul(bank[:, j, SEQ:3 * P], k1, q[:, P:SEQ], start=False, stop=False, skip_group_check=True)
                        m = pe.matmul(bank[:, j, SEQ:3 * P], ident_b[:, :], causal_t[:, :], start=False, stop=True,
                                      skip_group_check=True)
                    else:
                        for part in range(3):
                            pe.matmul(bank[:, j, 0:BW], ident_b[:, :], a1_bias3[:, part, :], start=False, stop=False,
                                      skip_group_check=True)
                        pe.matmul(bank[:, j, SEQ:2 * SEQ], k1, q, start=False, stop=False, skip_group_check=True)
                        m = pe.matmul(bank[:, j, SEQ:SEQ + BW], a1_one3[:, :], a1_last3[:, :], start=False, stop=True,
                                      skip_group_check=True)
                    m.then_inc(s["st_psum"], 1)
                    if n < 2:
                        for c in range(2):
                            row_chunk(8 * n + 2 * j + c)

            def weighted_values(n):
                b, hg = divmod(n, HG)
                pe.wait_ge(s["p"], m0 * PAIR * HEADS + 4 * n + 4)
                if n in (4, 6):
                    pe.wait_ge(s["ot"], m0 * PAIR * 2 + n // 2 - 1)
                to = bank[:, 4 + n // 2 % 2, (n % 2) * SEQ:(n % 2 + 1) * SEQ]
                for kt in range(2):
                    for j in range(4):
                        quad = slice(QUAD * j, QUAD * (j + 1))
                        v, p_at = mh_v[:, 2 * b + kt, 4 * hg + j, :], 4 * (n % 2) + j
                        if masked and kt:
                            m = pe.matmul(to[quad, P:SEQ], v, mh_p[:, p_at, SEQ:3 * P], start=False, stop=True,
                                          skip_group_check=True)
                        else:
                            m = pe.matmul(to[quad, :], v, mh_p[:, p_at, kt * SEQ:(kt + 1) * SEQ], start=kt == 0,
                                          stop=kt == 1, skip_group_check=True)
                m.then_inc(s["ot_psum"], 1)

            transposed_scores(0)
            for n in range(PAIR * HG):
                if n == 2:
                    turned_maxima(1, 6)
                if n + 1 < PAIR * HG:
                    transposed_scores(n + 1)
                weighted_values(n)
                if n == 3:
                    head_tensor(pe, unit_no(k, g) + 1, 7)
                if n == 4 and not last:
                    qk_tensor(pe, k, g + 1)
            for i in range(TILES):
                b, qt = divmod(i, 2)
                pe.wait_ge(s["ot"], m0 * PAIR * 2 + 2 * b + 2)
                for hg in range(HG):
                    m = pe.transpose(bank[:, i, hg * P:(hg + 1) * P], mh_ot[:, b * HG + hg, qt * P:(qt + 1) * P], ident[:, :])
                m.then_inc(s["otb_psum"], 1)
            for i in range(TILES):
                pe.wait_ge(s["on"], m0 * TILES + i + 1)
                m = pe.transpose(bank[:, 4, i * P:(i + 1) * P], mh_on[:, i, :, :].rearrange("p h d -> p (h d)"), ident[:, :])
            m.then_inc(s["ont_psum"], 1)
            pe.wait_ge(s["ont"], m0 + 1)
            for i in range(TILES):
                m = pe.matmul(bank[:, 5, i * D:(i + 1) * D], mh_ont[:, i * P:(i + 1) * P], wt[:, 3 * D:4 * D],
                              start=True, stop=True)
            m.then_inc(s["proj"], 1)

        def mh_scalar(act, k, g, last):
            s, masked, m0 = mh, k == "a2", mh_unit(k, g)
            act.wait_ge(s["v_psum"], m0 + 1)
            act.activation(mh_v[:, :, :, 0:HD], bank[:, 6, :].rearrange("p (t h d) -> p t h d", t=TILES, h=HEADS), ACT.Copy)\
               .then_inc(s["v"], 1)
            for n in range(PAIR * HG):
                width = 3 * P if masked else 2 * SEQ
                if n > 1:
                    act.wait_ge(s["ot_psum"], m0 * PAIR * HG + n - 1)
                for j in range(4):
                    act.wait_ge(s["st_psum"], (m0 * PAIR * HG + n) * 4 + j + 1)
                    act.activation(mh_p[:, 4 * (n % 2) + j, 0:width], bank[:, j, 0:width], ACT.Exp).then_inc(s["p"], 1)
                if n % 2 and n > 1:
                    copy_ot(act, s, m0, n // 2 - 1)
                if n == 4:
                    head_scalar(act, unit_no(k, g) + 1, 7)
                if not last:
                    if n == 5:
                        qk_scalar(act, k, g + 1)
                    elif n > 5:
                        round_keys(act, k, g + 1, n - 6)
            if not last:
                round_keys(act, k, g + 1, PARTS - 1)
            copy_ot(act, s, m0, PAIR * HG // 2 - 1)
            act.wait_ge(s["ont_psum"], m0 + 1)
            act.activation(mh_ont[:, :], bank[:, 4, :], ACT.Copy).then_inc(s["ont"], 1)

        def copy_ot(act, s, m0, m):
            act.wait_ge(s["ot_psum"], m0 * PAIR * HG + 2 * m + 2)
            act.activation(mh_ot[:, 2 * m:2 * m + 2, :].rearrange("p a b -> p (a b)"), bank[:, 4 + m % 2, :], ACT.Copy)\
               .then_inc(s["ot"], 1)

        def mh_vector(dve, k, g, last):
            s, masked, m0 = mh, k == "a2", mh_unit(k, g)
            link = Steps(dve, steps[k], g, STEPS[k])
            for b in range(PAIR):
                steps_of = [(n // 2, 8 * (n % 2), 8, 4 * (n % 2)) for n in range(4)] if b == 0 else \
                           [(c // 8, 2 * (c % 8), 2, 6 + c % 2) for c in range(16)]
                for n, (qt, h0, heads, at) in enumerate(steps_of):
                    dve.wait_ge(s["s_psum"], m0 * REDUCES + 4 * b + n + 1)
                    keys = P * (qt + 1) if masked else SEQ
                    scores = bank[:, at:at + heads // 2, :].rearrange("p b (c k) -> p (b c) k", c=2)[:, :, 0:keys]
                    dve.tensor_reduce(mh_max[:, 2 * b + qt, 0, h0:h0 + heads], scores, AX_X, ALU.max, negate=True)\
                       .then_inc(s["max"], 1)
                dve.wait_ge(s["max"], m0 * REDUCES + (REDUCES if b else 4))
                tiles_ = slice(2 * b, 2 * b + 2)
                dve.tensor_copy(mh_max[:, tiles_, 1:PARTS, 0:HEADS],
                                mh_max[:, tiles_, 0:1, 0:HEADS].to_broadcast([P, 2, PARTS - 1, HEADS])).then_inc(s["max3"], 1)
                dve.wait_ge(s["maxt_psum"], m0 * PAIR + b + 1)
                left = bank[0:PARTS * QUAD, 6 * b, 0:SEQ]
                of_b = slice(b * SEQ, (b + 1) * SEQ)
                for part in range(PARTS - 1):
                    link(dve.tensor_copy(max_b[:, of_b], left))
                    link(dve.scalar_tensor_tensor(max_f[:, of_b], max_b[:, of_b], w["part_masks"][0:PARTS * QUAD, part:part + 1],
                                                  left, ALU.mult, ALU.add))
                    left = max_f[:, of_b]
                dve.tensor_copy(max_b[:, of_b], left).then_inc(s["max_parts"], 1)
            if k == "a1":
                norm_of(dve, k, g, 0, normed, LN_EPS, link)
                rows = w["a1_rows"]
                link(dve.tensor_tensor(y[:, :, :], y[:, :, :], rows[:, None, D:2 * D].to_broadcast([P, TILES, D]), ALU.mult))
                link(dve.tensor_tensor(y[:, :, :], y[:, :, :], rows[:, None, 2 * D:3 * D].to_broadcast([P, TILES, D]), ALU.add))
            head_vector(dve, unit_no(k, g) + 1, following(g), link)
            if not last:
                split_queries(dve, k, g + 1, link)
            for i in range(TILES):
                dve.wait_ge(s["otb_psum"], m0 * TILES + i + 1)
                parts = bank[:, i, :].rearrange("p (h r) -> p h r", r=QUAD)
                link(dve.reciprocal(mh_rec[:, i, :], parts[:, :, HD]))
                dve.tensor_tensor(mh_on[:, i, :, :], parts[:, :, 0:HD], mh_rec[:, i, :, None].to_broadcast([P, HEADS, HD]),
                                  ALU.mult).then_inc(s["on"], 1)
            dve.wait_ge(s["proj"], m0 + 1)
            if k == "a1":
                dve.tensor_tensor(y[:, :, :], bank[:, 5, :].rearrange("p (t d) -> p t d", d=D), y[:, :, :], ALU.add)\
                   .then_inc(s["proj_read"], 1)
                dve.wait_ge(s["proj_read"], m0 + 1)
                link(dve.tensor_tensor(y[:, :, :], y[:, :, :],
                                       w["a1_rows"][:, None, 3 * D:4 * D].to_broadcast([P, TILES, D]), ALU.add))
            else:
                dve.tensor_tensor(y[:, :, :], bank[:, 5, :].rearrange("p (t d) -> p t d", d=D),
                                  w["a2_rows"][:, None, D:2 * D].to_broadcast([P, TILES, D]), ALU.add).then_inc(s["proj_read"], 1)
                dve.wait_ge(s["proj_read"], m0 + 1)
            tail_vector(dve, k, g, link)
            link.close(0 if not last else SPLIT)

        def mh_pool(pool, k, g):
            s, left, m0 = mh, mh_room[:, 1, :], mh_unit(k, g)
            for part in range(PARTS - 1):
                pool.wait_ge(s["k_round"], m0 * PARTS + part + 1)
                pool.tensor_tensor(left, left, mh_parts[:, 1, part, :], ALU.subtract).then_inc(s["k_left"], 1)

        def max_rows(sp, m0):
            for b in range(PAIR):
                sp.wait_ge(mh["max_parts"], m0 * PAIR + b + 1)
                for part in range(PARTS):
                    row = MAX_ROWS.start + part
                    sp.dma_start(q_stack[row:row + 1, :, b, :],
                                 max_b[QUAD * part:QUAD * part + HEADS, b * SEQ:(b + 1) * SEQ])\
                      .then_inc(mh["max_rows"], 16)

        def mh_sync(sp, k, g, first):
            s, m0 = mh, mh_unit(k, g)

            def to_scr(scr, first, last, c):
                sp.dma_start(scr[first:last].rearrange("a i h t -> (i h) a t"),
                             mh_parts[:, c, 0:last - first, :]).then_inc(s["written"], 16)

            if not first:
                max_rows(sp, m0 - 1)
            sp.wait_ge(s["q_parts"], m0 + 1)
            to_scr(q_scr, 0, PARTS, 0)
            sp.wait_ge(s["k_round"], (m0 + 1) * PARTS)
            to_scr(k_scr, 0, PARTS, 1)
            to_scr(k_scr, PARTS, 2 * PARTS - 1, 1)
            sp.wait_ge(s["written"], (m0 + 1) * 16 * 3)
            for b in range(PAIR):
                if not first:
                    sp.wait_ge(s["st_psum"], (m0 - 1) * PAIR * HEADS + (b + 1) * HEADS)
                for r in range(PARTS):
                    for stack, scr in ((q_stack, q_scr[:]), (k_stack, k_scr[r:r + PARTS])):
                        sp.dma_start(stack[BLOCK * r:BLOCK * (r + 1), :, b, :],
                                     scr[:, :, :, b * SEQ:(b + 1) * SEQ].rearrange("a i h t -> (a i) h t"))\
                          .then_inc(s[f"stacked{b}"], 16)

        def places(*of):
            return [r[:, n * GT:(n + 1) * GT] for r in of for n in range(r.shape[1] // GT)]

        first_places = places(hidden_room, rooms[1], room_s,
                              mh_parts[:, :, :, :].rearrange("p c a t -> p (c a t)").bitcast(F32))
        second_places = places(hidden_room, rooms_ab[1])
        RING = {"f0": 4, "f1": 1 + E, "f2": 4, "f3": 4}
        AHEAD = {"f0": 3, "f1": 5, "f2": 3, "f3": 3}

        def hidden(k, i, f, tokens=slice(None)):
            place = i % RING[k] * 4 + f if k != "f1" else f if i == 0 else 1 + i
            return (first_places if k in ("f0", "f1") else second_places)[place][:, tokens]

        logits = sb("logits", [P, TILES, E])
        sel = sb("sel", [P, TILES, E])
        work = sb("work", [P, TILES, E])
        work2 = sb("work2", [P, TILES, E])
        hot1 = sb("hot1", [P, TILES, E])
        hot2 = sb("hot2", [P, TILES, E])
        gates = sb("gates", [P, TILES, E])
        gates_t = sb("gates_t", [E, GT])
        top = sb("top", [P, 8, TILES])
        silu1 = room_s[:, :].rearrange("p (f t) -> p f t", f=2)
        MOE_SEMS = ("logit_psum", "exp_in", "exp_out", "gates", "gt_psum", "gt", "b2_psum", "up_psum", "hidden", "down_psum", "added", "silu", "shared")
        ONLY = {"gates": ("f0", "f3"), "gt_psum": ("f0", "f3"), "gt": ("f0", "f3"), "b2_psum": ("f0", "f3"),
                "silu": ("f1",), "shared": ("f1",)}
        moe = {k: {s: sem(f"{k}_{s}") for s in MOE_SEMS if k in ONLY.get(s, (k,))} for k in ("f0", "f1", "f2", "f3")}

        EXPERTS = {"f0": [(4, e) for e in range(E)], "f1": [(2, None)] + [(1, e) for e in range(E)],
                   "f2": [(4, None)] + [(4, e) for e in range(E)], "f3": [(4, e) for e in range(E)]}

        def up_tiles(k, i):
            return sum((2 if k == "f1" and gate is None else 1) * n for n, gate in EXPERTS[k][:i])

        def hid_tiles(k, i):
            return sum(n for n, _ in EXPERTS[k][:i])

        def moe_tensor(pe, k, g):
            s, ex, up, down = moe[k], EXPERTS[k], w[f"{k}_up"], w[f"{k}_down"]
            n_shared = 4 if k == "f1" else 0
            own = up_tiles(k, len(ex)) - n_shared
            pe.wait_ge(normed_t_ready, unit_no(k, g) + 1)
            for i in range(TILES):
                m = pe.matmul(bank[:, 6, i * E:(i + 1) * E], normed_t[:, i * P:(i + 1) * P], w[f"{k}_wr"][:, :],
                              start=True, stop=True)
            m.then_inc(s["logit_psum"], 1)

            def up_to(i):
                n_tiles, gate = ex[i]
                n_up = 2 * n_tiles if k == "f1" and gate is None else n_tiles
                for f in range(n_up):
                    u = up_tiles(k, i) + f
                    if u >= 4:
                        if k == "f1" and u < 6:
                            pe.wait_ge(s["silu"], g * 2 + u - 4 + 1)
                        elif k == "f1" and u < 8:
                            pe.wait_ge(s["shared"], g * 2 + u - 6 + 1)
                        else:
                            pe.wait_ge(s["hidden"], g * own + u - 4 - n_shared + 1)
                    elif u == 0:
                        pe.wait_ge(s["hidden"], g * own)
                    pe.matmul(bank[:, u % 4, :], up[:, u * P:(u + 1) * P], normed_t[:, :], start=True, stop=True)\
                      .then_inc(s["up_psum"], 1)

            def down_from(i):
                n_tiles, _ = ex[i]
                h0 = hid_tiles(k, i)
                if k == "f1" and i == 0:
                    pe.wait_ge(s["shared"], (g + 1) * 2)
                else:
                    pe.wait_ge(s["hidden"], g * own + up_tiles(k, i) + n_tiles - n_shared)
                pe.wait_ge(s["added"], g * len(ex) + max(i - 1, 0))
                for t_ in range(TILES):
                    for f in range(n_tiles):
                        m = pe.matmul(bank[:, 4 + i % 2, t_ * D:(t_ + 1) * D], hidden(k, i, f, slice(t_ * P, (t_ + 1) * P)),
                                      down[:, (h0 + f) * D:(h0 + f + 1) * D], start=f == 0, stop=f == n_tiles - 1)
                m.then_inc(s["down_psum"], 1)

            for i in range(AHEAD[k]):
                up_to(i)
            for i in range(len(ex)):
                if i + AHEAD[k] < len(ex):
                    up_to(i + AHEAD[k])
                if i == 3 and k in ("f0", "f3"):
                    pe.wait_ge(s["gates"], g + 1)
                    for t_ in range(TILES):
                        m = pe.transpose(bank[0:E, 7, t_ * P:(t_ + 1) * P], gates[:, t_, :], ident[:, :])
                    m.then_inc(s["gt_psum"], 1)
                    pe.wait_ge(s["gt"], g + 1)
                    for t_ in range(TILES):
                        m = pe.matmul(bank[:, 6, t_ * D:(t_ + 1) * D], gates_t[:, t_ * P:(t_ + 1) * P], w[f"{k}_b2"][:, :],
                                      start=True, stop=True)
                    m.then_inc(s["b2_psum"], 1)
                if i == len(ex) - AHEAD[k]:
                    head_tensor(pe, unit_no(k, g) + 1, 7)
                down_from(i)

        def moe_scalar(act, k, g):
            s, ex = moe[k], EXPERTS[k]
            ups = up_tiles(k, len(ex))

            def gate_exponential():
                act.wait_ge(s["exp_in"], g + 1)
                if k == "f1":
                    m = act.activation(work[:, :, :], logits[:, :, :], ACT.Exp, scale=-1.0)
                elif k == "f2":
                    m = act.activation(work[:, :, :], work[:, :, :], ACT.Exp)
                else:
                    m = act.activation(top[:, 5, :], top[:, 4, :], ACT.Exp)
                m.then_inc(s["exp_out"], 1)

            for i, (n_tiles, gate) in enumerate(ex):
                if i == AHEAD[k]:
                    gate_exponential()
                if k == "f1" and gate is None:
                    for f in range(n_tiles):
                        act.wait_ge(s["up_psum"], g * ups + f + 1)
                        act.activation(silu1[:, f, :], bank[:, f, :], ACT.Silu).then_inc(s["silu"], 1)
                    continue
                act.wait_ge(s["down_psum"], g * len(ex) + max(i - RING[k] + 1, 0))
                for f in range(n_tiles):
                    u = up_tiles(k, i) + f
                    act.wait_ge(s["up_psum"], g * ups + u + 1)
                    func = ACT.Relu if k == "f3" else ACT.Gelu
                    if k in ("f0", "f3"):
                        m = act.activation(hidden(k, i, f), bank[:, u % 4, :], func, bias=w[f"{k}_b1"][:, u:u + 1])
                    else:
                        m = act.activation(hidden(k, i, f), bank[:, u % 4, :], func)
                    m.then_inc(s["hidden"], 1)
            head_scalar(act, unit_no(k, g) + 1, 7)

        def moe_vector(dve, k, g):
            s, ex = moe[k], EXPERTS[k]
            ups = up_tiles(k, len(ex))
            link = Steps(dve, steps[k], g, STEPS[k])
            dve.wait_ge(s["logit_psum"], g + 1)
            logit_psum = bank[:, 6, 0:TILES * E].rearrange("p (t e) -> p t e", e=E)

            def spread(a):
                return a[:, :, None].to_broadcast([P, TILES, E])

            def top_one(scores, best, hot):
                link(dve.tensor_reduce(best, scores, AX_X, ALU.max))
                link(dve.tensor_tensor(work2[:, :, :], scores, spread(best), ALU.is_ge))
                link(dve.tensor_tensor(work2[:, :, :], work2[:, :, :], rank8[:, :, :], ALU.mult))
                link(dve.tensor_reduce(top[:, 7, :], work2[:, :, :], AX_X, ALU.max))
                link(dve.tensor_tensor(hot, work2[:, :, :], spread(top[:, 7, :]), ALU.is_equal))

            def top_two(scores):
                top_one(scores, top[:, 0, :], hot1[:, :, :])
                link(dve.scalar_tensor_tensor(sel[:, :, :], hot1[:, :, :], BELOW, scores, ALU.mult, ALU.add))
                top_one(sel[:, :, :], top[:, 1, :], hot2[:, :, :])

            if k in ("f0", "f3"):
                link(dve.tensor_tensor(logits[:, :, :], logit_psum, w[f"{k}_br"][:, :, :], ALU.add))
                top_two(logits[:, :, :])
                dve.tensor_tensor(top[:, 4, :], top[:, 1, :], top[:, 0, :], ALU.subtract).then_inc(s["exp_in"], 1)
                dve.wait_ge(s["exp_out"], g + 1)
                link(dve.tensor_scalar(top[:, 6, :], top[:, 5, :], 1.0, None, ALU.add))
                link(dve.reciprocal(top[:, 2, :], top[:, 6, :]))
                link(dve.tensor_tensor(top[:, 3, :], top[:, 5, :], top[:, 2, :], ALU.mult))
                link(dve.tensor_tensor(hot1[:, :, :], hot1[:, :, :], spread(top[:, 2, :]), ALU.mult))
                link(dve.tensor_tensor(hot2[:, :, :], hot2[:, :, :], spread(top[:, 3, :]), ALU.mult))
                dve.tensor_tensor(gates[:, :, :], hot1[:, :, :], hot2[:, :, :], ALU.add).then_inc(s["gates"], 1)
            elif k == "f1":
                dve.tensor_copy(logits[:, :, :], logit_psum).then_inc(s["exp_in"], 1)
                for f in range(2):
                    dve.wait_ge(s["silu"], g * 2 + f + 1)
                    dve.wait_ge(s["up_psum"], g * ups + 2 + f + 1)
                    dve.tensor_tensor(hidden(k, 0, f), bank[:, 2 + f, :], silu1[:, f, :], ALU.mult).then_inc(s["shared"], 1)
                dve.wait_ge(s["exp_out"], g + 1)
                link(dve.tensor_scalar(work[:, :, :], work[:, :, :], 1.0, None, ALU.add))
                link(dve.reciprocal(gates[:, :, :], work[:, :, :]))
                link(dve.tensor_tensor(logits[:, :, :], gates[:, :, :], w["f1_br"][:, :, :], ALU.add))
                top_two(logits[:, :, :])
                link(dve.tensor_tensor(hot1[:, :, :], hot1[:, :, :], hot2[:, :, :], ALU.add))
                link(dve.tensor_tensor(gates[:, :, :], gates[:, :, :], hot1[:, :, :], ALU.mult))
                link(dve.tensor_reduce(top[:, 2, :], gates[:, :, :], AX_X, ALU.add))
                link(dve.tensor_scalar(top[:, 3, :], top[:, 2, :], 1e-9, None, ALU.is_gt))
                link(dve.tensor_scalar(top[:, 4, :], top[:, 2, :], 1e-9, None, ALU.add))
                link(dve.reciprocal(top[:, 5, :], top[:, 4, :]))
                link(dve.tensor_tensor(top[:, 5, :], top[:, 5, :], top[:, 3, :], ALU.mult))
                link(dve.tensor_scalar(top[:, 6, :], top[:, 3, :], -0.5, 0.5, ALU.mult, ALU.add))
                link(dve.tensor_tensor(gates[:, :, :], gates[:, :, :], spread(top[:, 5, :]), ALU.mult))
                link(dve.tensor_tensor(hot1[:, :, :], hot1[:, :, :], spread(top[:, 6, :]), ALU.mult))
                link(dve.tensor_tensor(gates[:, :, :], gates[:, :, :], hot1[:, :, :], ALU.add))
            else:
                link(dve.tensor_reduce(top[:, 2, :], logit_psum, AX_X, ALU.max))
                dve.tensor_tensor(work[:, :, :], logit_psum, spread(top[:, 2, :]), ALU.subtract).then_inc(s["exp_in"], 1)
                dve.wait_ge(s["exp_out"], g + 1)
                link(dve.tensor_reduce(top[:, 3, :], work[:, :, :], AX_X, ALU.add))
                link(dve.reciprocal(top[:, 4, :], top[:, 3, :]))
                link(dve.tensor_tensor(logits[:, :, :], work[:, :, :], spread(top[:, 4, :]), ALU.mult))
                top_two(logits[:, :, :])
                link(dve.tensor_tensor(hot1[:, :, :], hot1[:, :, :], hot2[:, :, :], ALU.add))
                link(dve.tensor_tensor(gates[:, :, :], logits[:, :, :], hot1[:, :, :], ALU.mult))

            if k in ("f0", "f3"):
                dve.wait_ge(s["gates"], g + 1)
            for i, (_, gate) in enumerate(ex):
                if i == 3 and k in ("f0", "f3"):
                    dve.wait_ge(s["gt_psum"], g + 1)
                    dve.tensor_copy(gates_t[:, :], bank[0:E, 7, :]).then_inc(s["gt"], 1)
                if i == 4 and k in ("f0", "f3"):
                    dve.wait_ge(s["b2_psum"], g + 1)
                    link(dve.tensor_tensor(y[:, :, :], bank[:, 6, :].rearrange("p (t d) -> p t d", d=D), y[:, :, :], ALU.add))
                if i == len(ex) - AHEAD[k] - 1:
                    head_vector(dve, unit_no(k, g) + 1, following(g), link)
                dve.wait_ge(s["down_psum"], g * len(ex) + i + 1)
                for t_ in range(TILES):
                    part = bank[:, 4 + i % 2, t_ * D:(t_ + 1) * D]
                    if k == "f3" and i == 0:
                        m = dve.tensor_scalar(y[:, t_, :], part, gates[:, t_, gate:gate + 1], None, ALU.mult)
                    elif k == "f0" and i == 0:
                        m = dve.scalar_tensor_tensor(y[:, t_, :], part, gates[:, t_, gate:gate + 1], normed[:, t_, :],
                                                     ALU.mult, ALU.add)
                    elif gate is not None:
                        m = dve.scalar_tensor_tensor(y[:, t_, :], part, gates[:, t_, gate:gate + 1], y[:, t_, :],
                                                     ALU.mult, ALU.add)
                    elif k == "f1":
                        m = dve.tensor_copy(y[:, t_, :], part)
                    else:
                        m = dve.tensor_tensor(y[:, t_, :], part, normed[:, t_, :], ALU.add)
                m.then_inc(s["added"], 1)
                dve.wait_ge(s["added"], g * len(ex) + i + 1)
            if k == "f0":
                norm_of(dve, k, g, 0, y, 1e-12, link)
                link(dve.tensor_tensor(y[:, :, :], y[:, :, :], w["f0_ln"][:, None, 0:D].to_broadcast([P, TILES, D]), ALU.mult))
                link(dve.tensor_tensor(y[:, :, :], y[:, :, :], w["f0_ln"][:, None, D:2 * D].to_broadcast([P, TILES, D]), ALU.add))
            tail_vector(dve, k, g, link)
            link.close()

        ROW = HALVES * GT
        SSM_SEMS = ("in_psum", "x_raw", "conv", "xc", "bc_psum", "dt_psum", "v", "e", "w1", "ln", "dt", "round", "left", "y0",
                    "bb", "cb", "decay", "c_sb", "dbx", "h", "hc", "y_part", "y_all", "yz", "proj")
        ss = {s: sem(f"a3_{s}") for s in SSM_SEMS}
        def halves(a):
            return a.rearrange("p (h t) -> p h t", h=HALVES)

        def two(a):
            return a.rearrange("p (i h t) -> p i h t", i=2, h=HALVES)

        hs, hc, decay = two(rooms[0][:, :]), two(rooms[1][:, :]), two(rooms[4][:, :])
        xc, zs = halves(rooms[5][:, 0:ROW]), halves(rooms[5][:, ROW:2 * ROW])
        dt_s, u_in = halves(rooms[3][:, 0:ROW]), halves(rooms[3][:, ROW:2 * ROW])
        c_sb = halves(room_s[:, :])
        raw_words = HALVES * PAIR * (TAPS - 1 + SEQ)
        x_raw = rooms[2][:, 0:raw_words].rearrange("p (h b t) -> p h b t", h=HALVES, b=PAIR)
        bc_stack = mh_parts[0:PARTS * QUAD, :, :, :].rearrange("p c a t -> p (c a) t")[:, 0:4, :]
        bc_left = hidden_room[0:PARTS * QUAD, 0:4 * GT].rearrange("p (c t) -> p c t", c=4)
        dbx = hidden_room[:, :].rearrange("p (s h t) -> p s h t", s=4, h=HALVES)
        a_neg = sb("a_neg", [P, HALVES, N_STATE])
        d_diag = sb("d_diag", [P, HALVES, P])
        tmp_a, tmp_b, tmp_c = hs[:, 0, :, :], hs[:, 1, :, :], hc[:, 0, :, :]
        vec = w["a3_vec"]
        DT_BIAS, CONV_B, SKIP = TAPS, TAPS + 1, TAPS + 2

        def ssm_tensor(pe, g):
            pe.wait_ge(normed_t_ready, unit_no("a3", g) + 1)
            for n in range(4):
                pe.matmul(bank[:, n, :], w["a3_win"][:, n * P:(n + 1) * P], normed_t[:, :], start=True, stop=True)\
                  .then_inc(ss["in_psum"], 1)
            pe.wait_ge(ss["xc"], (g + 1) * HALVES)
            rows = PARTS * QUAD
            for h in range(HALVES):
                m = pe.matmul(bank[:, 3, :], w["a3_wx"][:, h, 4 * rows:4 * rows + P], xc[:, h, :], start=h == 0, stop=h == HALVES - 1)
            m.then_inc(ss["dt_psum"], 1)
            for n in range(4):
                for h in range(HALVES):
                    m = pe.matmul(bank[0:rows, 4 + n, :], w["a3_wx"][:, h, n * rows:(n + 1) * rows], xc[:, h, :],
                                  start=h == 0, stop=h == HALVES - 1)
                m.then_inc(ss["bc_psum"], 1)
            for h in range(HALVES):
                m = pe.matmul(bank[:, h, :], d_diag[:, h, :], xc[:, h, :], start=True, stop=False, skip_group_check=True)
            m.then_inc(ss["y0"], 1)
            pe.wait_ge(ss["round"], (g + 1) * 4 * PARTS)

            def spread(c, m, i):
                pe.matmul(bank[:, 4 + 2 * c + i, :], row_sel[:, bass.ds(m, 1)].to_broadcast([rows, P]), bc_stack[:, 2 * c + i, :],
                          start=True, stop=True).then_inc(ss["cb" if c else "bb"], 1)

            def spread_b(q, m, i):
                pe.wait_ge(ss["dbx"], g * N_STATE + q + 1)
                spread(0, m + 1, i)

            def spread_c(q, m, i):
                pe.wait_ge(ss["c_sb"], g * N_STATE + q + 1)
                spread(1, m + 1, i)

            def collect(q, i):
                pe.wait_ge(ss["hc"], g * N_STATE + q + 1)
                for h in range(HALVES):
                    m = pe.matmul(bank[:, h, :], ident[:, :], hc[:, i, h, :], start=False, stop=False, skip_group_check=True)
                m.then_inc(ss["y_part"], 1)

            for i in range(2):
                spread(0, 0, i)
                spread(1, 0, i)
            for i in range(2):
                spread_b(i, 0, i)
                spread_c(i, 0, i)
            with pe.Fori(1, N_STATE // 2 - 1) as m:
                for i in range(2):
                    spread_b(m * 2 + i, m, i)
                    collect(m * 2 + i - 2, i)
                    spread_c(m * 2 + i, m, i)
            for q in range(N_STATE - 4, N_STATE):
                collect(q, q % 2)
            head_tensor(pe, unit_no("a3", g) + 1, 2)
            pe.wait_ge(ss["yz"], (g + 1) * HALVES)
            for t_ in range(TILES):
                for h in range(HALVES):
                    m = pe.matmul(bank[:, 4, t_ * D:(t_ + 1) * D], xc[:, h, t_ * P:(t_ + 1) * P], w["a3_wout"][:, h, :],
                                  start=h == 0, stop=h == HALVES - 1)
            m.then_inc(ss["proj"], 1)

        def ssm_scalar(act, g):
            for h in range(HALVES):
                act.wait_ge(ss["in_psum"], g * 4 + h + 1)
                act.activation(x_raw[:, h, :, TAPS - 1:], bank[:, h, :].rearrange("p (b t) -> p b t", b=PAIR), ACT.Copy)\
                   .then_inc(ss["x_raw"], 1)
            for h in range(HALVES):
                act.wait_ge(ss["in_psum"], g * 4 + 2 + h + 1)
                act.activation(zs[:, h, :], bank[:, 2 + h, :], ACT.Silu)
            for h in range(HALVES):
                act.wait_ge(ss["conv"], g * HALVES + h + 1)
                act.activation(xc[:, h, :], u_in[:, h, :], ACT.Silu, bias=vec[:, h, CONV_B:CONV_B + 1]).then_inc(ss["xc"], 1)
            def round_parts(part):
                for c in range(4):
                    if part == 0:
                        act.wait_ge(ss["bc_psum"], g * 4 + c + 1)
                    else:
                        act.wait_ge(ss["left"], g * 4 * (PARTS - 1) + (part - 1) * 4 + c + 1)
                    source = bank[0:PARTS * QUAD, 4 + c, :] if part == 0 else bc_left[:, c, :]
                    act.activation(bc_stack[:, c, :], source, ACT.Copy).then_inc(ss["round"], 1)

            act.wait_ge(ss["v"], (g + 1) * HALVES)
            act.activation(tmp_b, tmp_b, ACT.Exp, scale=-1.0).then_inc(ss["e"], 1)
            round_parts(0)
            act.wait_ge(ss["w1"], g + 1)
            act.activation(u_in[:, :, :], tmp_c, ACT.Ln).then_inc(ss["ln"], 1)
            round_parts(1)
            round_parts(2)
            act.wait_ge(ss["dt"], g + 1)

            def one(m, i, first):
                n = m * 2 + i
                if not first:
                    act.wait_ge(ss["h"], g * N_STATE + n - 1)
                for h in range(HALVES):
                    a = act.activation(decay[:, i, h, :].rearrange("p (b t) -> p b t", b=PAIR)[:, :, 1:],
                                       dt_s[:, h, :].rearrange("p (b t) -> p b t", b=PAIR)[:, :, 1:], ACT.Exp,
                                       scale=a_neg[:, h, bass.ds(m + i * QUAD, 1)])
                a.then_inc(ss["decay"], 1)
                act.wait_ge(ss["cb"], g * N_STATE + n + 1)
                if not first:
                    act.wait_ge(ss["hc"], g * N_STATE + n - 1)
                act.activation(c_sb[:, i, :], bank[:, 6 + i, :], ACT.Copy).then_inc(ss["c_sb"], 1)

            for i in range(2):
                one(0, i, True)
            with act.Fori(1, N_STATE // 2) as m:
                for i in range(2):
                    one(m, i, False)
            head_scalar(act, unit_no("a3", g) + 1, 2)

        def ssm_pool(pool, g):
            def one(n, i):
                pool.wait_ge(ss["h"], g * N_STATE + n + 1)
                pool.wait_ge(ss["c_sb"], g * N_STATE + n + 1)
                pool.tensor_tensor(hc[:, i, :, :], hs[:, i, :, :], c_sb[:, i:i + 1, :].to_broadcast([P, HALVES, GT]), ALU.mult)\
                    .then_inc(ss["hc"], 1)

            for i in range(2):
                one(i, i)
            with pool.Fori(1, N_STATE // 2) as n2:
                for i in range(2):
                    pool.wait_ge(ss["y_part"], g * N_STATE + n2 * 2 + i - 1)
                    one(n2 * 2 + i, i)
            head_pool(pool, unit_no("a3", g) + 1)

        def ssm_vector(dve, g):
            link = Steps(dve, steps["a3"], g, STEPS["a3"])
            for h in range(HALVES):
                dve.wait_ge(ss["x_raw"], g * HALVES + h + 1)
                acc = u_in[:, h, :].rearrange("p (b t) -> p b t", b=PAIR)
                for k in range(TAPS):
                    x_k = x_raw[:, h, :, k:k + SEQ]
                    if k == 0:
                        link(dve.tensor_scalar(acc, x_k, vec[:, h, 0:1], None, ALU.mult))
                    elif k < TAPS - 1:
                        link(dve.scalar_tensor_tensor(acc, x_k, vec[:, h, k:k + 1], acc, ALU.mult, ALU.add))
                    else:
                        dve.scalar_tensor_tensor(acc, x_k, vec[:, h, k:k + 1], acc, ALU.mult, ALU.add).then_inc(ss["conv"], 1)
            dve.wait_ge(ss["dt_psum"], g + 1)
            for h in range(HALVES):
                link(dve.tensor_scalar(tmp_a[:, h, :], bank[:, 3, :], vec[:, h, DT_BIAS:DT_BIAS + 1], None, ALU.add))
                dve.scalar_tensor_tensor(tmp_b[:, h, :], tmp_a[:, h, :], -1.0, tmp_a[:, h, :], ALU.mult, ALU.max).then_inc(ss["v"], 1)

            def take_parts(part):
                for c in range(4):
                    dve.wait_ge(ss["round"], g * 4 * PARTS + part * 4 + c + 1)
                    if part > 0:
                        dve.wait_ge(ss["left"], g * 4 * (PARTS - 1) + (part - 1) * 4 + c + 1)
                    source = bank[0:PARTS * QUAD, 4 + c, :] if part == 0 else bc_left[:, c, :]
                    dve.scalar_tensor_tensor(bc_left[:, c, :], bc_stack[:, c, :], w["part_masks"][0:PARTS * QUAD, part:part + 1],
                                             source, ALU.mult, ALU.add).then_inc(ss["left"], 1)

            dve.wait_ge(ss["e"], g + 1)
            dve.tensor_scalar(tmp_c, tmp_b, 1.0, None, ALU.add).then_inc(ss["w1"], 1)
            take_parts(0)
            dve.wait_ge(ss["w1"], g + 1)
            link(dve.scalar_tensor_tensor(tmp_b, tmp_c, 1.0, tmp_b, ALU.subtract, ALU.subtract))
            dve.wait_ge(ss["ln"], g + 1)
            link(dve.tensor_tensor(tmp_c, u_in[:, :, :], tmp_b, ALU.subtract))
            dve.scalar_tensor_tensor(dt_s[:, :, :], tmp_a, 0.0, tmp_c, ALU.max, ALU.add).then_inc(ss["dt"], 1)
            take_parts(1)
            dve.wait_ge(ss["dt"], g + 1)
            link(dve.tensor_tensor(u_in[:, :, :], dt_s[:, :, :], xc[:, :, :], ALU.mult))

            def products(q, r):
                dve.wait_ge(ss["bb"], g * N_STATE + q + 1)
                if not (isinstance(q, int) and q < 4):
                    dve.wait_ge(ss["h"], g * N_STATE + q - 3)
                i = r % 2
                dve.tensor_tensor(dbx[:, r, :, :], u_in[:, :, :], bank[:, 4 + i:5 + i, :].to_broadcast([P, HALVES, GT]), ALU.mult)\
                   .then_inc(ss["dbx"], 1)

            def scan(q, r):
                dve.wait_ge(ss["dbx"], g * N_STATE + q + 1)
                dve.wait_ge(ss["decay"], g * N_STATE + q + 1)
                i = r % 2
                if not (isinstance(q, int) and q < 2):
                    dve.wait_ge(ss["hc"], g * N_STATE + q - 1)
                dve.tensor_tensor_scan(hs[:, i, :, :].rearrange("p h t -> p (h t)"),
                                       decay[:, i, :, :].rearrange("p h t -> p (h t)"),
                                       dbx[:, r, :, :].rearrange("p h t -> p (h t)"), 0.0, ALU.mult, ALU.add).then_inc(ss["h"], 1)

            dve.wait_ge(ss["round"], (g + 1) * 4 * PARTS)
            products(0, 0)
            for q in range(4):
                products(q + 1, (q + 1) % 4)
                scan(q, q)
            with dve.Fori(1, N_STATE // 4 - 1) as q4:
                for r in range(4):
                    products(q4 * 4 + r + 1, (r + 1) % 4)
                    scan(q4 * 4 + r, r)
            for q in range(N_STATE - 4, N_STATE):
                if q + 1 < N_STATE:
                    products(q + 1, (q + 1) % 4)
                scan(q, q % 4)
            head_vector(dve, unit_no("a3", g) + 1, following(g), link)
            dve.wait_ge(ss["y_part"], (g + 1) * N_STATE)
            for h in range(HALVES):
                dve.tensor_tensor(xc[:, h, :], bank[:, h, :], zs[:, h, :], ALU.mult).then_inc(ss["yz"], 1)
            dve.wait_ge(ss["proj"], g + 1)
            link(dve.tensor_copy(y[:, :, :], bank[:, 4, :].rearrange("p (t d) -> p t d", d=D)))
            tail_vector(dve, "a3", g, link)
            link.close()

        with_x = t["x"].rearrange("(g t p) d -> g p t d", t=TILES, p=P)
        out_x = out.rearrange("(g t p) d -> g p t d", t=TILES, p=P)
        LOADS = {
            "const": ["ident", "rank8", "causal2", "row_sel", "part_masks"],
            "a0": ["a0_w", "a0_rel", "a0_mask", "a0_slope"],
            "a1": ["a1_w", "a1_rows", "a1_across", "a1_down", "a1_inside", "a1_part"],
            "a2": ["a2_w", "a2_qkb", "a2_rows", "a2_pos"],
            "a3": ["a3_win", "a3_wx", "a3_wout", "a3_vec", "a3_alog"],
            "f0": ["f0_wr", "f0_br", "f0_b1", "f0_b2", "f0_ln", "f0_up", "f0_down"],
            "f1": ["f1_wr", "f1_br", "f1_up", "f1_down"],
            "f2": ["f2_wr", "f2_up", "f2_down"],
            "f3": ["f3_wr", "f3_br", "f3_b1", "f3_b2", "f3_up", "f3_down"],
        }
        causal2_f = rooms[4][:, 0:2 * P].rearrange("p (a c) -> p a c", a=2)
        row_sel_f = rooms[4][0:PARTS * QUAD, 4 * P:4 * P + QUAD]
        tiles = dict(w, ident=ident, rank8=rank8, causal2=causal2_f, row_sel=row_sel_f)

        def need(engine, *names):
            for k in names:
                engine.wait_ge(loaded[k], 16 * (GROUPS if k == "x" else len(LOADS[k])))

        SETUP_SQUARES, SETUP_MAX, SETUP_ALL = 16, 17, 38

        block = ctx.enter_context(nc.Block())

        @block.sync
        def _(sp):
            for g in range(GROUPS):
                sp.dma_start(stream[:, g * TILES:(g + 1) * TILES, :], with_x[g]).then_inc(loaded["x"], 16)
            for k, names in LOADS.items():
                if k == "f3":
                    sp.wait_ge(moe["f0"]["down_psum"], GROUPS * E)
                for name in names:
                    to = tiles[name]
                    sp.dma_start(to[tuple([slice(None)] * len(to.shape))], t[name]).then_inc(loaded[k], 16)
            sp.wait_ge(k_rows, 3)
            for k in ("a1", "a2"):
                if k == "a2":
                    sp.wait_ge(setup, SETUP_ALL)
                    sp.dma_start(pos_scr.rearrange("a h t -> h a t"), pos_b[:, :, :]).then_inc(pos_done, 16)
                    sp.wait_ge(pos_done, 16)
                    sp.wait_ge(mh["st_psum"], GROUPS * PAIR * HEADS)
                    for b in range(PAIR):
                        sp.dma_start(k_stack[POS_ROWS, :, b, :], pos_scr).then_inc(pos_done, 16)
                mh_sync(sp, k, 0, True)
                with sp.Fori(1, GROUPS) as g:
                    mh_sync(sp, k, g, False)
                max_rows(sp, mh_unit(k, GROUPS - 1))
            sp.wait_ge(steps["f3"], GROUPS * STEPS["f3"])
            for g in range(GROUPS):
                sp.dma_start(out_x[g], stream[:, g * TILES:(g + 1) * TILES, :]).then_inc(stored, 16)
            sp.wait_ge(stored, 16 * GROUPS)

        def unit_pool(pool, k, g, last):
            if k == "a3":
                ssm_pool(pool, g)
                norm_pool(pool, k, g, 0)
                return
            if k == "a1":
                norm_pool(pool, k, g, 0)
            head_pool(pool, unit_no(k, g) + 1)
            if k in ("a1", "a2") and not last:
                mh_pool(pool, k, g + 1)
            if k == "f0":
                norm_pool(pool, k, g, 0)
            norm_pool(pool, k, g, norms_per[k] - 1)

        @block.gpsimd
        def _(pool):
            pool.memset(minus_half[:, :], -0.5).then_inc(pool_setup, 1)
            pool.wait_ge(setup, SETUP_MAX)
            pool.partition_all_reduce(far_all[:, :], far[:, :], P, bass.bass_isa.ReduceOp.max).then_inc(pool_setup, 1)

            pool.wait_ge(pool_setup, 2)
            head_pool(pool, 0)
            for k in blocks:
                if k == "f0":
                    pool.wait_ge(rstd_ready, GROUPS)
                    for n, (stack, quad, value) in enumerate(((q_stack, 2, 1.0), (k_stack, 2, 0.0), (k_stack, 3, 1.0))):
                        pool.memset(stack[quad * QUAD:(quad + 1) * QUAD, :, :, :], value).then_inc(k_rows, 1)
                        pool.wait_ge(k_rows, n + 1)
                if k in ("a1", "a2"):
                    mh_pool(pool, k, 0)
                with pool.Fori(0, GROUPS - (k in ("a1", "a2"))) as g:
                    unit_pool(pool, k, g, False)
                if k in ("a1", "a2"):
                    unit_pool(pool, k, GROUPS - 1, True)

        @block.scalar
        def _(act):
            act.wait_ge(setup, SETUP_SQUARES)
            act.activation(a1_dist[:, :, :], a1_dist[:, :, :], ACT.Sqrt).then_inc(act_setup, 1)
            need(act, "a3")
            act.activation(a_neg[:, :, :], w["a3_alog"][:, :, :], ACT.Exp).then_inc(act_setup, 1)
            act.wait_ge(setup, SETUP_ALL)
            need(act, "f0", "a1", "a2")
            head_scalar(act, 0, 7)
            for k in blocks:
                if k == "f3":
                    need(act, "f3")
                if k in ("a1", "a2"):
                    qk_scalar(act, k, 0)
                    for part in range(PARTS):
                        round_keys(act, k, 0, part)
                    with act.Fori(0, GROUPS - 1) as g:
                        mh_scalar(act, k, g, False)
                    mh_scalar(act, k, GROUPS - 1, True)
                    continue
                with act.Fori(0, GROUPS) as g:
                    if k == "a0":
                        a0_scalar(act, g)
                    elif k == "a3":
                        ssm_scalar(act, g)
                    else:
                        moe_scalar(act, k, g)

        @block.tensor
        def _(pe):
            pe.wait_ge(setup, SETUP_ALL)
            for k in blocks:
                need(pe, k)
                if k == "a2":
                    pe.wait_ge(pos_done, 16 * (1 + PAIR))
                if k == "a0":
                    head_tensor(pe, 0, 7)
                else:
                    before = blocks[blocks.index(k) - 1]
                    pe.wait_ge(steps[before], GROUPS * STEPS[before] - (SPLIT if before in ("a1", "a2") else 0))
                if k in ("a1", "a2"):
                    qk_tensor(pe, k, 0)
                    with pe.Fori(0, GROUPS - 1) as g:
                        mh_tensor(pe, k, g, False)
                    mh_tensor(pe, k, GROUPS - 1, True)
                    continue
                with pe.Fori(0, GROUPS) as g:
                    if k == "a0":
                        a0_tensor(pe, g)
                    elif k == "a3":
                        ssm_tensor(pe, g)
                    else:
                        moe_tensor(pe, k, g)

        @block.vector
        def _(dve):
            link = Steps(dve, setup, 0, SETUP_ALL)
            link(dve.memset(rooms[0][:, :], 0.0))
            link(dve.memset(mh_v[:, :, :, HD:HD + 1], 1.0))
            dve.memset(ones_row[:, :], 1.0)
            link(dve.memset(mh_max[:, :, :, :], 0.0))
            dve.memset(a1_last3[:, :], 0.0)
            link(dve.memset(a1_one3[:, :], 0.0))
            link(dve.memset(a1_one3[:, 0:1], 1.0))
            need(dve, "const", "a0", "a1", "a2", "a3")
            link(dve.tensor_copy(ident_b[:, :], ident[:, :]))
            link(dve.tensor_copy(causal[:, :], causal2_f[:, 0, :]))
            link(dve.tensor_copy(causal_t[:, :], causal2_f[:, 1, :]))
            link(dve.tensor_copy(row_sel[:, :], row_sel_f))
            link(dve.scalar_tensor_tensor(a0_bias[:, :], w["a0_rel"][:, :], w["a0_slope"][:, 0:1], w["a0_mask"][:, :],
                                          ALU.mult, ALU.add))
            for n in range(2):
                dx, dy = a1_dist[:, n, :], a1_dy[:, :]
                link(dve.tensor_scalar(dx, w["a1_across"][:, 0, :], w["a1_down"][:, 2 * n:2 * n + 1], None, ALU.subtract))
                link(dve.tensor_tensor(dx, dx, dx, ALU.mult))
                dve.tensor_scalar(dy, w["a1_across"][:, 1, :], w["a1_down"][:, 2 * n + 1:2 * n + 2], None, ALU.subtract)\
                   .then_inc(dy_sem, 1)
                dve.wait_ge(dy_sem, 2 * n + 1)
                dve.tensor_tensor(dy, dy, dy, ALU.mult).then_inc(dy_sem, 1)
                dve.wait_ge(dy_sem, 2 * n + 2)
                link(dve.tensor_tensor(dx, dx, dy, ALU.add))
            assert link.n == SETUP_SQUARES
            dve.wait_ge(act_setup, 1)
            link(dve.tensor_reduce(far[:, :], a1_dist[:, :, :].rearrange("p a c -> p (a c)"), AX_X, ALU.max))
            assert link.n == SETUP_MAX
            dve.wait_ge(pool_setup, 2)
            link(dve.tensor_scalar(far[:, :], far_all[:, :], 1e-6, -0.1, ALU.is_gt, ALU.mult))
            link(dve.tensor_scalar(far_all[:, :], far_all[:, :], 1e-6, None, ALU.max))
            link(dve.reciprocal(far_all[:, :], far_all[:, :]))
            link(dve.tensor_tensor(far[:, :], far[:, :], far_all[:, :], ALU.mult))
            link(dve.scalar_tensor_tensor(a1_dist[:, :, :], a1_dist[:, :, :], far[:, 0:1], w["a1_inside"][:, :, :],
                                          ALU.mult, ALU.mult))
            for part in range(3):
                link(dve.tensor_copy(a1_bias3[:, part, :], a1_dist[:, 0, :]))
                if part < 2:
                    link(dve.tensor_tensor(a1_dist[:, 0, :], a1_dist[:, 0, :], a1_bias3[:, part, :], ALU.subtract))
            link(dve.memset(a1_dy[0:3, :], 0.0))
            for part in range(3):
                dve.tensor_copy(a1_last3[0:3, :], a1_dist[0:3, 1, :]).then_inc(dy_sem, 1)
                dve.wait_ge(dy_sem, 4 + 3 * part + 1)
                dve.scalar_tensor_tensor(a1_dy[0:3, :], a1_last3[0:3, :], w["a1_part"][:, part:part + 1], a1_dy[0:3, :],
                                         ALU.mult, ALU.add).then_inc(dy_sem, 1)
                dve.tensor_tensor(a1_dist[0:3, 1, :], a1_dist[0:3, 1, :], a1_last3[0:3, :], ALU.subtract).then_inc(dy_sem, 1)
                dve.wait_ge(dy_sem, 4 + 3 * part + 3)
            link(dve.tensor_copy(a1_last3[0:3, :], a1_dy[0:3, :]))
            for part in range(PARTS):
                link(dve.tensor_copy(pos_b[:, part, :], w["a2_pos"][:, :]))
                if part < PARTS - 1:
                    link(dve.tensor_tensor(w["a2_pos"][:, :], w["a2_pos"][:, :], pos_b[:, part, :], ALU.subtract))
            link(dve.tensor_scalar(w["a2_qkb"][:, 0:1], w["a2_qkb"][:, 0:1], float(HD) ** -0.5, None, ALU.mult))
            dve.wait_ge(act_setup, 2)
            link(dve.tensor_scalar(a_neg[:, :, :], a_neg[:, :, :], -1.0, None, ALU.mult))
            for h in range(HALVES):
                link(dve.tensor_scalar(d_diag[:, h, :], ident[:, :], vec[:, h, SKIP:SKIP + 1], None, ALU.mult))
            link.close()
            need(dve, "x", "f0", "f1")
            for k in blocks:
                if k == "f3":
                    need(dve, "f3")
                if k == "a3":
                    dve.memset(x_raw[:, :, :, 0:TAPS - 1], 0.0).then_inc(dy_sem, 1)
                    dve.memset(rooms[4][:, :].rearrange("p (r t) -> p r t", t=SEQ)[:, :, 0:1], 0.0).then_inc(dy_sem, 1)
                    dve.wait_ge(dy_sem, 4 + 3 * 3 + 2)
                if k == "a0":
                    first = Steps(dve, first_steps, 0, HEAD)
                    head_vector(dve, 0, 0, first)
                    first.close()
                if k in ("a1", "a2"):
                    first = Steps(dve, first_qk, 0 if k == "a1" else 1, SPLIT)
                    split_queries(dve, k, 0, first)
                    first.close()
                    with dve.Fori(0, GROUPS - 1) as g:
                        mh_vector(dve, k, g, False)
                    mh_vector(dve, k, GROUPS - 1, True)
                    continue
                with dve.Fori(0, GROUPS) as g:
                    if k == "a0":
                        a0_vector(dve, g)
                    elif k == "a3":
                        ssm_vector(dve, g)
                    else:
                        moe_vector(dve, k, g)


def by_feature(mat):
    return mat.reshape(-1, HEADS, HD).transpose(0, 2, 1).reshape(-1, D)


def arrange(a):
    f = np.float32

    def cat(*parts):
        return np.concatenate(parts, axis=1)

    def rows(*vs):
        return np.broadcast_to(np.concatenate(vs)[None, :], (P, sum(len(v) for v in vs)))

    def tiled(v):
        return np.broadcast_to(v[None, None, :], (P, TILES, E))

    def halves(mat):
        return mat.reshape(HALVES, P, -1).transpose(1, 0, 2)

    t = {"x": a["L0_attn_x"].reshape(-1, D)}
    pos = np.arange(P)
    late = (pos[None, :] > pos[:, None])
    t["ident"] = np.eye(P, dtype=f)
    t["rank8"] = tiled(np.arange(E, 0, -1).astype(f))
    t["causal2"] = np.stack([late * f(MASKED), late.T * f(MASKED)], axis=1).astype(f)
    row = np.arange(PARTS * QUAD)
    t["row_sel"] = (row[:, None] % QUAD == np.arange(QUAD)).astype(f)
    t["part_masks"] = -(pos[:, None] // QUAD > np.arange(PARTS - 1)).astype(f)
    rel = (pos[None, :] - pos[:, None]).astype(f)
    t["a0_rel"] = cat(rel, rel - P, rel)
    t["a0_mask"] = cat(late * f(BELOW), 0 * late, late * f(BELOW)).astype(f)
    t["a0_slope"] = np.broadcast_to(a["L0_attn_alibi_slope"][None, :], (P, 1))
    t["a0_w"] = cat(a["L0_attn_W_qk"], a["L0_attn_W_v"].T)

    wq, wk, wv = a["L1_attn_W_qkv"].reshape(3, D, D).transpose(0, 2, 1)
    t["a1_w"] = cat(by_feature(wq), by_feature(wk), wv, a["L1_attn_W_proj"].T)
    t["a1_rows"] = rows(np.zeros(D, f), a["L1_attn_ln_gamma"], a["L1_attn_ln_beta"], a["L1_attn_b_proj"])
    at = np.clip(np.arange(BW) - 1, 0, P - 1)
    c = a["L1_attn_spatial_centers"]
    t["a1_across"] = np.broadcast_to(c[at].T[None], (P, 2, BW))
    t["a1_down"] = cat(c[at[0:P]], np.broadcast_to(c[P - 1][None], (P, 2)))
    inside = np.zeros((P, 2, BW), f)
    inside[1:, 0, 1:P + 1] = 1
    inside[:, 1, 1:P + 1] = 1
    t["a1_inside"] = inside
    t["a1_part"] = np.eye(3, dtype=f)

    t["a2_w"] = cat(by_feature(a["L2_attn_Wq"]), by_feature(a["L2_attn_Wk"]), a["L2_attn_Wv"], a["L2_attn_Wo"])
    t["a2_qkb"] = cat(by_feature(a["L2_attn_bq"]).T, by_feature(a["L2_attn_bk"]).T)
    start = 2 ** (-2 ** (-(np.log2(HEADS) - 3)))
    slopes = np.array([start * start ** i for i in range(HEADS)]).astype(f)
    t["a2_pos"] = slopes[:, None] * (np.arange(SEQ) - (SEQ - 1)).astype(f)
    t["a2_rows"] = rows(a["L2_attn_bv"], a["L2_attn_bo"])

    t["a3_win"] = a["L3_attn_W_in"]
    wx = a["L3_attn_W_x"]
    b_, c_, d_ = wx[:, 0:N_STATE], wx[:, N_STATE:2 * N_STATE], wx[:, 2 * N_STATE:]
    t["a3_wx"] = halves(cat(*[m[:, n * QUAD:(n + 1) * QUAD] for m in (b_, c_) for n in range(N_STATE // QUAD) for _ in range(PARTS)],
                            np.broadcast_to(d_, (HALVES * P, P))))
    t["a3_wout"] = halves(a["L3_attn_W_out"])
    t["a3_vec"] = halves(cat(a["L3_attn_conv_w"], a["L3_attn_dt_bias"][:, None], a["L3_attn_conv_b"][:, None],
                             a["L3_attn_D"][:, None]))
    t["a3_alog"] = halves(a["L3_attn_A_log"])

    def up(m):
        return m.transpose(1, 0, 2).reshape(D, -1)

    def down(m):
        return m.reshape(-1, P, D).transpose(1, 0, 2).reshape(P, -1)

    t["f0_wr"], t["f0_br"] = a["L0_ffn_Wr"].T, tiled(a["L0_ffn_br"])
    t["f0_up"], t["f0_down"] = up(a["L0_ffn_W1"].transpose(0, 2, 1)), down(a["L0_ffn_W2"].transpose(0, 2, 1))
    t["f0_b1"], t["f0_b2"] = a["L0_ffn_b1"].reshape(-1, P).T, a["L0_ffn_b2"]
    t["f0_ln"] = rows(a["L0_ffn_ln_w"], a["L0_ffn_ln_b"])
    t["f1_wr"], t["f1_br"] = a["L1_ffn_router_w"].T, tiled(a["L1_ffn_router_bias"])
    t["f1_up"] = cat(a["L1_ffn_sw1"], a["L1_ffn_sw3"], up(a["L1_ffn_ew1"]))
    t["f1_down"] = cat(down(a["L1_ffn_sw2"]), down(a["L1_ffn_ew2"]))
    t["f2_wr"] = a["L2_ffn_router_w"]
    t["f2_up"] = cat(up(a["L2_ffn_shared_up"]), up(a["L2_ffn_routed_up"]))
    t["f2_down"] = cat(down(a["L2_ffn_shared_down"]), down(a["L2_ffn_routed_down"]))
    t["f3_wr"], t["f3_br"] = a["L3_ffn_Wr"], tiled(a["L3_ffn_br"])
    t["f3_up"], t["f3_down"] = up(a["L3_ffn_W1"]), down(a["L3_ffn_W2"])
    t["f3_b1"], t["f3_b2"] = a["L3_ffn_b1"].reshape(-1, P).T, a["L3_ffn_b2"]
    return t


def kernel(**inputs):
    import concourse.bacc as bacc
    from concourse.bass_utils import run_bass_kernel_spmd

    nc = bacc.Bacc("TRN2", target_bir_lowering=False, num_devices=1)
    arrays = {k: np.ascontiguousarray(v) for k, v in arrange({k: np.asarray(v) for k, v in inputs.items()}).items()}
    t = {k: nc.dram_tensor(f"in_{k}", v.shape, mybir.dt.from_np(v.dtype), kind="ExternalInput").ap()
         for k, v in arrays.items()}
    out = nc.dram_tensor("out_x", (NSEQ * SEQ, D), F32, kind="ExternalOutput").ap()
    build(nc, t, out)
    r = run_bass_kernel_spmd(nc, [{f"in_{k}": v for k, v in arrays.items()}], core_ids=[0])
    return r.results[0]["out_x"].reshape(NSEQ, SEQ, D)
```

```python
from contextlib import ExitStack

import numpy as np

import concourse.bass as bass
from concourse import mybir

ALU = mybir.AluOpType
ACT = mybir.ActivationFunctionType
F32 = mybir.dt.float32
BF16 = mybir.dt.bfloat16
AX_X = mybir.AxisListType.X

P = 128
D = 128
SEQ = 256
NSEQ = 8
GT = 512
GROUPS = NSEQ * SEQ // GT
TILES = GT // P
PAIR = GT // SEQ
HEADS = 16
HD = D // HEADS
QUAD = 32
HG = HEADS // 4
PARTS = 3
BLOCK = PARTS * HD
PRODUCTS = PARTS * BLOCK
E = 8
N_STATE = 64
HALVES = 2
TAPS = 4
LN_EPS = 1e-5
BW = P + 2
MASKED = -1e30
BELOW = -3e38


class Steps:

    def __init__(self, engine, sem, g, per):
        self.engine, self.sem, self.g, self.per, self.n = engine, sem, g, per, 0

    def __call__(self, instruction):
        instruction.then_inc(self.sem, 1)
        self.n += 1
        self.engine.wait_ge(self.sem, self.g * self.per + self.n)

    def close(self, missing=0):
        assert self.n + missing == self.per, f"{self.n} linked steps, {self.per} stated"


HEAD = 3
NORM = HEAD + 1
TAIL = NORM + 1
SPLIT = 2 * (PARTS - 1)
TOP2 = 11
CONV = HALVES * (TAPS - 1)
STEPS = {
    "a0": HEAD + PAIR + 1 + TILES + TAIL,
    "f0": HEAD + 1 + TOP2 + 5 + 1 + NORM + 2 + TAIL,
    "a1": 1 + HEAD + SPLIT + NORM + 2 + PAIR * SPLIT + TILES + 1 + TAIL,
    "f1": HEAD + 3 + TOP2 + 11 + TAIL,
    "a2": HEAD + SPLIT + PAIR * SPLIT + TILES + TAIL,
    "f2": HEAD + 1 + 3 + TOP2 + 2 + TAIL,
    "a3": HEAD + CONV + HALVES + 2 + 1 + TAIL,
    "f3": HEAD + 1 + TOP2 + 5 + 1 + TAIL,
}


def build(nc, t, out):
    ctx = ExitStack()
    with ctx:
        def sb(name, shape, dt=F32):
            return ctx.enter_context(nc.sbuf_tensor(name, shape, dt))

        def sem(name):
            return ctx.enter_context(nc.semaphore(name))

        bank = ctx.enter_context(nc.psum_tensor("bank", [P, 8, 512], F32))

        stream = sb("stream", [P, GROUPS * TILES, D])
        normed = sb("normed", [P, TILES, D])
        normed_t = sb("normed_t", [P, GT])
        y = sb("y", [P, TILES, D])
        stats = sb("stats", [P, TILES, 6])
        mean = sb("mean", [P, TILES, 1])
        spread_ = sb("spread_", [P, 4, TILES])
        var_eps = sb("var_eps", [P, TILES])
        rstd = sb("rstd", [P, TILES])
        minus_half = sb("minus_half", [P, TILES])

        ident = sb("ident", [P, P])
        ident_b = sb("ident_b", [P, P], BF16)
        causal = sb("causal", [P, P], BF16)
        causal_t = sb("causal_t", [P, P], BF16)
        row_sel = sb("row_sel", [PARTS * QUAD, QUAD], BF16)
        rank8 = sb("rank8", [P, TILES, E])

        hidden_room = sb("hidden_room", [P, 8 * GT])
        rooms_ab = [sb(f"rooms_{n}", [P, 8 * GT]) for n in range(2)]
        rooms = [sb(f"room{n}", [P, 4 * GT]) for n in range(2)]
        rooms += [r[:, n * 4 * GT:(n + 1) * 4 * GT] for r in rooms_ab for n in range(2)]
        room_s = sb("room_s", [P, 2 * GT])

        w = {}
        for name, shape, dt in [
            ("a0_w", [P, 2 * D], F32), ("a0_slope", [P, 1], F32),
            ("a1_w", [P, 4 * D], F32),
            ("a1_rows", [P, 4 * D], F32), ("a1_down", [P, 4], F32),
            ("a1_part", [3, 3], F32),
            ("a2_w", [P, 4 * D], F32), ("a2_qkb", [P, 2], F32), ("part_masks", [P, PARTS - 1], F32),
            ("a2_rows", [P, 2 * D], F32),
            ("a3_win", [P, 4 * P], F32), ("a3_wx", [P, HALVES, 4 * P], F32), ("a3_wout", [P, HALVES, D], F32),
            ("a3_vec", [P, HALVES, TAPS + 3], F32), ("a3_alog", [P, HALVES, N_STATE], F32),
            ("f0_wr", [P, E], F32), ("f1_wr", [P, E], F32), ("f2_wr", [P, E], F32), ("f3_wr", [P, E], F32),
            ("f0_br", [P, TILES, E], F32), ("f1_br", [P, TILES, E], F32), ("f3_br", [P, TILES, E], F32),
            ("f0_b1", [P, E * 4], F32), ("f3_b1", [P, E * 4], F32), ("f0_b2", [E, D], F32), ("f3_b2", [E, D], F32),
            ("f0_ln", [P, 2 * D], F32),
            ("f1_up", [P, 2 * 256 + E * P], F32), ("f1_down", [P, (2 + E) * D], F32),
            ("f2_up", [P, (1 + E) * 512], F32), ("f2_down", [P, (1 + E) * 512], F32),
            ("f3_up", [P, E * 512], F32), ("f3_down", [P, E * 512], F32),
        ]:
            w[name] = sb(name, shape, dt)
        w["a0_rel"], w["a0_mask"] = rooms[2][:, 0:3 * P], rooms[2][:, 3 * P:6 * P]
        w["a2_pos"] = rooms[3][0:HEADS, 0:SEQ]
        w["a1_across"], w["a1_inside"], a1_dist = (rooms[5][:, 2 * BW * n:2 * BW * (n + 1)].rearrange("p (a c) -> p a c", a=2)
                                                   for n in range(3))
        a1_dy = rooms[5][:, 6 * BW:7 * BW]
        w["f0_up"], w["f0_down"] = w["f3_up"], w["f3_down"]

        loaded = {k: sem(f"loaded_{k}") for k in ("x", "const", "a0", "f0", "a1", "f1", "a2", "f2", "a3", "f3")}
        setup = sem("setup")
        pool_setup = sem("pool_setup")
        act_setup = sem("act_setup")
        head_var = sem("head_var")
        head_rstd = sem("head_rstd")
        var_ready = sem("var_ready")
        rstd_ready = sem("rstd_ready")
        normed_ready = sem("normed_ready")
        xt_ready = sem("xt_ready")
        normed_t_ready = sem("normed_t_ready")
        stored = sem("stored")
        blocks = ("a0", "f0", "a1", "f1", "a2", "f2", "a3", "f3")
        steps = {k: sem(f"steps_{k}") for k in blocks}
        first_steps = sem("first_steps")
        first_max = sem("first_max")
        first_conv = sem("first_conv")
        first_qk = sem("first_qk")
        norms_per = {k: 1 for k in blocks} | {"f0": 2, "a1": 2}
        norms_before = {k: GROUPS * sum(norms_per[b] for b in blocks[:i]) for i, k in enumerate(blocks)}

        def norm_no(k, g, i):
            return norms_before[k] + g * norms_per[k] + i + 1

        def past_outputs(engine, k, g):
            engine.wait_ge(var_ready, norm_no(k, g, 0) - 1)

        def unit_no(k, g):
            return GROUPS * blocks.index(k) + g

        def following(g):
            return (g + 1) % GROUPS

        def moments(dve, rows, eps, link, done):
            for i in range(TILES):
                m = dve.bn_stats(stats[:, i, :], rows(i))
            link(m)
            total, apart, inner, outer = (spread_[:, n, :] for n in range(4))
            dve.tensor_tensor(total, stats[:, :, 1], stats[:, :, 4], ALU.add)
            dve.tensor_tensor(apart, stats[:, :, 1], stats[:, :, 4], ALU.subtract)
            link(dve.tensor_tensor(inner, stats[:, :, 2], stats[:, :, 5], ALU.add))
            dve.tensor_scalar(mean[:, :, 0], total, 0.5, None, ALU.mult)
            dve.tensor_scalar(inner, inner, 1.0 / D, eps, ALU.mult, ALU.add)
            link(dve.scalar_tensor_tensor(outer, apart, 0.25, apart, ALU.mult, ALU.mult))
            dve.tensor_tensor(var_eps[:, :], inner, outer, ALU.add).then_inc(done, 1)

        def stream_tile(g, i):
            return stream[:, bass.ds(g * TILES + i, 1), :].rearrange("p a d -> p (a d)")

        def head_moments(dve, g, link):
            moments(dve, lambda i: stream_tile(g, i), LN_EPS, link, head_var)

        def head_normalize(dve, u, g):
            dve.wait_ge(head_rstd, u + 1)
            for i in range(TILES):
                dve.tensor_scalar(normed[:, i, :], stream_tile(g, i), mean[:, i, :], rstd[:, i:i + 1],
                                  ALU.subtract, ALU.mult).then_inc(normed_ready, 1)

        def head_vector(dve, u, g, link):
            head_moments(dve, g, link)
            head_normalize(dve, u, g)

        def head_pool(pool, u):
            pool.wait_ge(head_var, u + 1)
            pool.tensor_tensor(rstd[:, :], var_eps[:, :], minus_half[:, :], ALU.pow).then_inc(head_rstd, 1)

        def head_tensor(pe, u, b):
            for i in range(TILES):
                pe.wait_ge(normed_ready, u * TILES + i + 1)
                m = pe.transpose(bank[:, b, i * P:(i + 1) * P], normed[:, i, :], ident[:, :])
            m.then_inc(xt_ready, 1)

        def head_scalar(act, u, b):
            act.wait_ge(xt_ready, u + 1)
            act.activation(normed_t[:, :], bank[:, b, :], ACT.Copy).then_inc(normed_t_ready, 1)

        def norm_of(dve, k, g, i, source, eps, link):
            moments(dve, lambda n: source[:, n, :], eps, link, var_ready)
            dve.wait_ge(rstd_ready, norm_no(k, g, i))
            for n in range(TILES):
                m = dve.tensor_scalar(y[:, n, :], source[:, n, :], mean[:, n, :], rstd[:, n:n + 1],
                                      ALU.subtract, ALU.mult)
            link(m)

        def norm_pool(pool, k, g, i):
            pool.wait_ge(var_ready, norm_no(k, g, i))
            pool.tensor_tensor(rstd[:, :], var_eps[:, :], minus_half[:, :], ALU.pow).then_inc(rstd_ready, 1)

        def tail_vector(dve, k, g, link):
            norm_of(dve, k, g, norms_per[k] - 1, y, LN_EPS, link)
            rows = stream[:, bass.ds(g * TILES, TILES), :]
            link(dve.tensor_tensor(rows, rows, y[:, :, :], ALU.add))

        a0 = {k: sem(f"a0_{k}") for k in ("q_psum", "q", "v_psum", "v", "s_psum", "s", "p", "pt_psum", "pt", "o_psum")}
        a0_room = hidden_room[:, 0:2 * GT + 9 * PAIR * P]
        a0_q = a0_room[:, 0:GT]
        a0_v = a0_room[:, GT:2 * GT].rearrange("p (t d) -> p t d", d=D)
        a0_s, a0_p, a0_pt = (a0_room[:, 2 * GT + n * 3 * PAIR * P:2 * GT + (n + 1) * 3 * PAIR * P]
                             .rearrange("p (b c) -> p b c", b=PAIR) for n in range(3))
        a0_bias = sb("a0_bias", [P, 3 * P])
        row_max = sb("row_max", [P, TILES])
        row_sum = sb("row_sum", [P, TILES])
        row_rec = sb("row_rec", [P, TILES])

        def a0_tensor(pe, g):
            pe.wait_ge(normed_t_ready, unit_no("a0", g) + 1)
            pe.matmul(bank[:, 0, :], w["a0_w"][:, 0:D], normed_t[:, :], start=True, stop=True).then_inc(a0["q_psum"], 1)
            for i in range(TILES):
                m = pe.matmul(bank[:, 1, i * D:(i + 1) * D], normed_t[:, i * P:(i + 1) * P], w["a0_w"][:, D:2 * D],
                              start=True, stop=True)
            m.then_inc(a0["v_psum"], 1)
            pe.wait_ge(a0["q"], g + 1)
            for b in range(PAIR):
                at = b * SEQ
                pe.matmul(bank[:, 2 + b, 0:P], a0_q[:, at:at + P], normed_t[:, at:at + P], start=True, stop=True)
                pe.matmul(bank[:, 2 + b, P:3 * P], a0_q[:, at + P:at + 2 * P], normed_t[:, at:at + 2 * P],
                          start=True, stop=True).then_inc(a0["s_psum"], 1)
            for b in range(PAIR):
                pe.wait_ge(a0["p"], (g * PAIR + b) * 2 + 2)
                for n in range(3):
                    m = pe.transpose(bank[:, 4 + b, n * P:(n + 1) * P], a0_p[:, b, n * P:(n + 1) * P], ident[:, :])
                m.then_inc(a0["pt_psum"], 1)
            pe.wait_ge(a0["v"], g + 1)
            for b in range(PAIR):
                pe.wait_ge(a0["pt"], g * PAIR + b + 1)
                o = bank[:, 6, b * 2 * D:(b + 1) * 2 * D]
                pe.matmul(o[:, 0:D], a0_pt[:, b, 0:P], a0_v[:, 2 * b, :], start=True, stop=True)
                pe.matmul(o[:, D:2 * D], a0_pt[:, b, P:2 * P], a0_v[:, 2 * b, :], start=True, stop=False)
                pe.matmul(o[:, D:2 * D], a0_pt[:, b, 2 * P:3 * P], a0_v[:, 2 * b + 1, :], start=False,
                          stop=True).then_inc(a0["o_psum"], 1)
            head_tensor(pe, unit_no("a0", g) + 1, 7)

        def a0_scalar(act, g):
            act.wait_ge(a0["q_psum"], g + 1)
            act.activation(a0_q[:, :], bank[:, 0, :], ACT.Copy, scale=float(D) ** -0.5).then_inc(a0["q"], 1)
            for b in range(PAIR):
                act.wait_ge(a0["s"], (g * PAIR + b) * 2 + 2)
                for n, (lo, hi) in enumerate(((0, P), (P, 3 * P))):
                    r = 2 * b + n
                    act.activation(a0_p[:, b, lo:hi], a0_s[:, b, lo:hi], ACT.Exp, bias=row_max[:, r:r + 1],
                                   accum_out=row_sum[:, r:r + 1]).then_inc(a0["p"], 1)
            for b in range(PAIR):
                act.wait_ge(a0["pt_psum"], g * PAIR + b + 1)
                act.activation(a0_pt[:, b, :], bank[:, 4 + b, 0:3 * P], ACT.Copy).then_inc(a0["pt"], 1)
            head_scalar(act, unit_no("a0", g) + 1, 7)

        def a0_vector(dve, g):
            link = Steps(dve, steps["a0"], g, STEPS["a0"])
            dve.wait_ge(a0["v_psum"], g + 1)
            dve.tensor_copy(a0_v[:, :, :], bank[:, 1, :].rearrange("p (t d) -> p t d", d=D)).then_inc(a0["v"], 1)
            for b in range(PAIR):
                dve.wait_ge(a0["s_psum"], g * PAIR + b + 1)
                link(dve.tensor_tensor(a0_s[:, b, :], bank[:, 2 + b, 0:3 * P], a0_bias[:, :], ALU.add))
                for n, (lo, hi) in enumerate(((0, P), (P, 3 * P))):
                    r = 2 * b + n
                    dve.tensor_reduce(row_max[:, r:r + 1], a0_s[:, b, lo:hi], AX_X, ALU.max, negate=True)\
                       .then_inc(a0["s"], 1)
            head_vector(dve, unit_no("a0", g) + 1, following(g), link)
            dve.wait_ge(a0["p"], (g * PAIR + PAIR) * 2)
            link(dve.reciprocal(row_rec[:, :], row_sum[:, :]))
            dve.wait_ge(a0["o_psum"], (g + 1) * PAIR)
            for i in range(TILES):
                link(dve.tensor_scalar(y[:, i, :], bank[:, 6, i * D:(i + 1) * D], row_rec[:, i:i + 1], None, ALU.mult))
            tail_vector(dve, "a0", g, link)
            link.close()

        mh_room = room_s[:, :].rearrange("p (c t) -> p c t", c=2)
        mh_parts = sb("mh_parts", [P, 2, PARTS, GT], BF16)

        q_stack, k_stack = (r[:, :].bitcast(BF16).rearrange("p (h b t) -> p h b t", b=PAIR, h=HEADS) for r in rooms_ab)
        POS_ROWS = slice(PRODUCTS, PRODUCTS + PARTS)
        ROWS = 3 * QUAD
        MAX_ROWS = slice(ROWS, ROWS + PARTS)
        mh_v = rooms[0][:, :].rearrange("p (t h r) -> p t h r", t=TILES, h=HEADS)
        mh_max = sb("mh_max", [P, TILES, PARTS, QUAD])
        pos_b = sb("pos_b", [HEADS, PARTS, SEQ], BF16)
        pos_done = sem("pos_done")
        k_rows = sem("k_rows")
        max_f = sb("max_f", [PARTS * QUAD, GT])
        max_b = sb("max_b", [PARTS * QUAD, GT], BF16)
        mh_p = hidden_room[:, :].rearrange("p (j c) -> p j c", j=8)
        mh_ot = rooms[1][:, :].rearrange("p (n q) -> p n q", q=SEQ)
        ones_row = sb("ones_row", [1, P])
        mh_rec = sb("mh_rec", [P, TILES, HEADS])
        mh_on = hidden_room[:, 0:GT].rearrange("p (t h d) -> p t h d", t=TILES, h=HEADS)
        mh_ont = hidden_room[:, GT:2 * GT]
        q_scr = nc.dram_tensor("q_scr", [PARTS, HD, HEADS, GT], BF16).ap()
        k_scr = nc.dram_tensor("k_scr", [2 * PARTS - 1, HD, HEADS, GT], BF16).ap()
        pos_scr = nc.dram_tensor("pos_scr", [PARTS, HEADS, SEQ], BF16).ap()
        a1_bias3 = sb("a1_bias3", [P, 3, BW], BF16)
        a1_last3 = sb("a1_last3", [P, BW], BF16)
        a1_one3 = sb("a1_one3", [P, P], BF16)
        far = sb("far", [P, 1])
        far_all = sb("far_all", [P, 1])
        dy_sem = sem("dy_sem")
        MH_SEMS = ("q_psum", "q", "q_parts", "k_psum", "k", "k_round", "k_left", "v_psum", "v", "written", "stacked0", "stacked1",
                   "s_psum", "max", "max3", "maxt_psum", "max_parts", "max_rows", "st_psum",
                   "p", "ot_psum", "ot", "otb_psum", "on", "ont_psum", "ont", "proj", "proj_read")
        mh = {s: sem(f"mh_{s}") for s in MH_SEMS}

        CHUNKS = 16

        def mh_unit(k, g):
            return g if k == "a1" else g + GROUPS

        def qk_tensor(pe, k, g, c, b):
            pe.wait_ge(normed_t_ready, unit_no(k, g) + 1)
            pe.matmul(bank[:, b, :], w[f"{k}_w"][:, c * D:(c + 1) * D], normed_t[:, :], start=True, stop=True)\
              .then_inc(mh["k_psum" if c else "q_psum"], 1)

        def qk_scalar(act, k, g, banks):
            s, masked, m0 = mh, k == "a2", mh_unit(k, g)
            for c, (name, scale) in enumerate((("q", float(HD) ** -0.5), ("k", 1.0))):
                act.wait_ge(s[f"{name}_psum"], m0 + 1)
                if masked:
                    m = act.activation(mh_room[:, c, :], bank[:, banks[c], :], ACT.Identity, bias=w["a2_qkb"][:, c:c + 1],
                                       scale=scale)
                else:
                    m = act.activation(mh_room[:, c, :], bank[:, banks[c], :], ACT.Copy, scale=scale)
                m.then_inc(s[name], 1)

        def round_keys(act, k, g, part):
            m0 = mh_unit(k, g)
            if part == 0:
                act.wait_ge(mh["k"], m0 + 1)
            else:
                act.wait_ge(mh["k_left"], m0 * (PARTS - 1) + part)
            act.activation(mh_parts[:, 1, part, :], mh_room[:, 1, :], ACT.Copy).then_inc(mh["k_round"], 1)

        def split_queries(dve, k, g, link):
            dve.wait_ge(mh["q"], mh_unit(k, g) + 1)
            left = mh_room[:, 0, :]
            for part in range(PARTS - 1):
                link(dve.tensor_copy(mh_parts[:, 0, part, :], left))
                link(dve.tensor_tensor(left, left, mh_parts[:, 0, part, :], ALU.subtract))
            dve.tensor_copy(mh_parts[:, 0, PARTS - 1, :], left).then_inc(mh["q_parts"], 1)

        def row_chunk(pe, k, m, b, c):
            qt, h0, to = c // 8, 2 * (c % 8), bank[:, 6 + c % 2, :].rearrange("p (c k) -> p c k", c=2)
            rows, keys = slice(0, ROWS), P * (qt + 1) if k == "a2" else SEQ
            if c == 0:
                pe.wait_ge(mh[f"stacked{b}"], (m + 1) * 16 * 2 * PARTS)
            if c >= 2:
                pe.wait_ge(mh["max"], (m * PAIR + b) * CHUNKS + c - 1)
            for j in range(2):
                i = pe.matmul(to[:, j, 0:keys], q_stack[rows, h0 + j, b, qt * P:(qt + 1) * P], k_stack[rows, h0 + j, b, 0:keys],
                              start=not (k == "a2" and j), stop=True, skip_group_check=k == "a2" and j == 1)
            if k == "a2":
                i = pe.matmul(to[:, :, qt * P:(qt + 1) * P], ident_b[:, :], causal[:, None, :].to_broadcast([P, 2, P]),
                              start=False, stop=True, skip_group_check=True)
            i.then_inc(mh["s_psum"], 1)

        def turned_maxima(pe, m, b):
            pe.wait_ge(mh["max3"], m * PAIR + b + 1)
            for i in range(2):
                t_ = pe.transpose(bank[0:PARTS * QUAD, 6, i * P:(i + 1) * P],
                                  mh_max[:, 2 * b + i, :, :].rearrange("p a h -> p (a h)"), ident[:, :])
            t_.then_inc(mh["maxt_psum"], 1)

        def row_maxima(dve, k, m, b, link, between=None):
            for c in range(CHUNKS):
                if c == CHUNKS // 2 and between is not None:
                    between()
                qt, h0 = c // 8, 2 * (c % 8)
                dve.wait_ge(mh["s_psum"], (m * PAIR + b) * CHUNKS + c + 1)
                keys = P * (qt + 1) if k == "a2" else SEQ
                scores = bank[:, 6 + c % 2, :].rearrange("p (c k) -> p c k", c=2)[:, :, 0:keys]
                dve.tensor_reduce(mh_max[:, 2 * b + qt, 0, h0:h0 + 2], scores, AX_X, ALU.max, negate=True)\
                   .then_inc(mh["max"], 1)
            dve.wait_ge(mh["max"], (m * PAIR + b + 1) * CHUNKS)
            tiles_ = slice(2 * b, 2 * b + 2)
            dve.tensor_copy(mh_max[:, tiles_, 1:PARTS, 0:HEADS],
                            mh_max[:, tiles_, 0:1, 0:HEADS].to_broadcast([P, 2, PARTS - 1, HEADS])).then_inc(mh["max3"], 1)
            dve.wait_ge(mh["maxt_psum"], m * PAIR + b + 1)
            left = bank[0:PARTS * QUAD, 6, 0:SEQ]
            of_b = slice(b * SEQ, (b + 1) * SEQ)
            for part in range(PARTS - 1):
                link(dve.tensor_copy(max_b[:, of_b], left))
                link(dve.scalar_tensor_tensor(max_f[:, of_b], max_b[:, of_b], w["part_masks"][0:PARTS * QUAD, part:part + 1],
                                              left, ALU.mult, ALU.add))
                left = max_f[:, of_b]
            dve.tensor_copy(max_b[:, of_b], left).then_inc(mh["max_parts"], 1)

        def mh_tensor(pe, k, g, last):
            s, masked, m0, wt = mh, k == "a2", mh_unit(k, g), w[f"{k}_w"]
            all_rows = slice(0, MAX_ROWS.stop)

            def transposed_scores(n):
                b, hg = divmod(n, HG)
                if n in (0, HG):
                    pe.wait_ge(s["max_rows"], (m0 * PAIR + b + 1) * 16 * PARTS)
                for j in range(4):
                    h = 4 * hg + j
                    if n > 0:
                        pe.wait_ge(s["p"], m0 * PAIR * HEADS + 4 * (n - 1) + j + 1)
                    k0, k1 = k_stack[all_rows, h, b, 0:P], k_stack[all_rows, h, b, P:2 * P]
                    q = q_stack[all_rows, h, b, :]
                    pe.matmul(bank[:, j, 0:SEQ], k0, q, start=True, stop=True)
                    if masked:
                        pe.matmul(bank[:, j, 0:P], ident_b[:, :], causal_t[:, :], start=False, stop=False,
                                  skip_group_check=True)
                        pe.matmul(bank[:, j, SEQ:3 * P], k1, q[:, P:SEQ], start=False, stop=False, skip_group_check=True)
                        m = pe.matmul(bank[:, j, SEQ:3 * P], ident_b[:, :], causal_t[:, :], start=False, stop=True,
                                      skip_group_check=True)
                    else:
                        for part in range(3):
                            pe.matmul(bank[:, j, 0:BW], ident_b[:, :], a1_bias3[:, part, :], start=False, stop=False,
                                      skip_group_check=True)
                        pe.matmul(bank[:, j, SEQ:2 * SEQ], k1, q, start=False, stop=False, skip_group_check=True)
                        m = pe.matmul(bank[:, j, SEQ:SEQ + BW], a1_one3[:, :], a1_last3[:, :], start=False, stop=True,
                                      skip_group_check=True)
                    m.then_inc(s["st_psum"], 1)
                    if n == 2:
                        for c in range(2):
                            row_chunk(pe, k, m0, 1, 8 + 2 * j + c)
                    if n in (6, 7) and not last:
                        for c in range(2):
                            row_chunk(pe, k, m0 + 1, 0, 8 * (n - 6) + 2 * j + c)

            def weighted_values(n):
                b, hg = divmod(n, HG)
                pe.wait_ge(s["p"], m0 * PAIR * HEADS + 4 * n + 4)
                if n == 0:
                    pe.wait_ge(s["v"], m0 + 1)
                if n == 2:
                    if last:
                        pe.wait_ge(normed_t_ready, unit_no(k, g) + 2)
                    else:
                        pe.wait_ge(s["k"], m0 + 2)
                if n in (4, 6):
                    pe.wait_ge(s["ot"], m0 * PAIR * 2 + n // 2 - 1)
                to = bank[:, 4 + n // 2 % 2, (n % 2) * SEQ:(n % 2 + 1) * SEQ]
                for kt in range(2):
                    for j in range(4):
                        quad = slice(QUAD * j, QUAD * (j + 1))
                        v, p_at = mh_v[:, 2 * b + kt, 4 * hg + j, :], 4 * (n % 2) + j
                        if masked and kt:
                            m = pe.matmul(to[quad, P:SEQ], v, mh_p[:, p_at, SEQ:3 * P], start=False, stop=True,
                                          skip_group_check=True)
                        else:
                            m = pe.matmul(to[quad, :], v, mh_p[:, p_at, kt * SEQ:(kt + 1) * SEQ], start=kt == 0,
                                          stop=kt == 1, skip_group_check=True)
                m.then_inc(s["ot_psum"], 1)

            transposed_scores(0)
            for i in range(TILES):
                m = pe.matmul(bank[:, 6, i * D:(i + 1) * D], normed_t[:, i * P:(i + 1) * P], wt[:, 2 * D:3 * D],
                              start=True, stop=not masked)
                if masked:
                    m = pe.matmul(bank[:, 6, i * D:(i + 1) * D], ones_row[:, :], w["a2_rows"][0:1, 0:D], start=False, stop=True)
            m.then_inc(s["v_psum"], 1)
            transposed_scores(1)
            weighted_values(0)
            past_outputs(pe, k, g)
            head_tensor(pe, unit_no(k, g) + 1, 5)
            for c in range(8):
                if c in (4, 7) and not last:
                    if c == 7:
                        pe.wait_ge(s["q"], m0 + 2)
                    qk_tensor(pe, k, g + 1, int(c == 7), 5)
                row_chunk(pe, k, m0, 1, c)
            for n in range(1, PAIR * HG):
                if n == 3:
                    turned_maxima(pe, m0, 1)
                    weighted_values(n)
                if n + 1 < PAIR * HG:
                    transposed_scores(n + 1)
                if n != 3:
                    weighted_values(n)
            if not last:
                turned_maxima(pe, m0 + 1, 0)
            for i in range(TILES):
                b, qt = divmod(i, 2)
                pe.wait_ge(s["ot"], m0 * PAIR * 2 + 2 * b + 2)
                for hg in range(HG):
                    m = pe.transpose(bank[:, i, hg * P:(hg + 1) * P], mh_ot[:, b * HG + hg, qt * P:(qt + 1) * P], ident[:, :])
                m.then_inc(s["otb_psum"], 1)
            for i in range(TILES):
                pe.wait_ge(s["on"], m0 * TILES + i + 1)
                m = pe.transpose(bank[:, 4, i * P:(i + 1) * P], mh_on[:, i, :, :].rearrange("p h d -> p (h d)"), ident[:, :])
            m.then_inc(s["ont_psum"], 1)
            pe.wait_ge(s["ont"], m0 + 1)
            for i in range(TILES):
                m = pe.matmul(bank[:, 5, i * D:(i + 1) * D], mh_ont[:, i * P:(i + 1) * P], wt[:, 3 * D:4 * D],
                              start=True, stop=True)
            m.then_inc(s["proj"], 1)

        def mh_scalar(act, k, g, last):
            s, masked, m0 = mh, k == "a2", mh_unit(k, g)
            for n in range(PAIR * HG):
                width = 3 * P if masked else 2 * SEQ
                if n > 1:
                    act.wait_ge(s["ot_psum"], m0 * PAIR * HG + n - 1)
                for j in range(4):
                    act.wait_ge(s["st_psum"], (m0 * PAIR * HG + n) * 4 + j + 1)
                    act.activation(mh_p[:, 4 * (n % 2) + j, 0:width], bank[:, j, 0:width], ACT.Exp).then_inc(s["p"], 1)
                if n == 3:
                    max_rows(act, m0, 1)
                if n % 2 and n > 1:
                    copy_ot(act, s, m0, n // 2 - 1)
                if n == 0:
                    act.wait_ge(s["v_psum"], m0 + 1)
                    act.activation(mh_v[:, :, :, 0:HD], bank[:, 6, :].rearrange("p (t h d) -> p t h d", t=TILES, h=HEADS),
                                   ACT.Copy).then_inc(s["v"], 1)
                if n == 1:
                    head_scalar(act, unit_no(k, g) + 1, 5)
                    if not last:
                        qk_scalar(act, k, g + 1, (5, 5))
                        for part in range(PARTS):
                            round_keys(act, k, g + 1, part)
            copy_ot(act, s, m0, PAIR * HG // 2 - 1)
            if not last:
                max_rows(act, m0 + 1, 0)
            act.wait_ge(s["ont_psum"], m0 + 1)
            act.activation(mh_ont[:, :], bank[:, 4, :], ACT.Copy).then_inc(s["ont"], 1)

        def copy_ot(act, s, m0, m):
            act.wait_ge(s["ot_psum"], m0 * PAIR * HG + 2 * m + 2)
            act.activation(mh_ot[:, 2 * m:2 * m + 2, :].rearrange("p a b -> p (a b)"), bank[:, 4 + m % 2, :], ACT.Copy)\
               .then_inc(s["ot"], 1)

        def mh_vector(dve, k, g, last):
            s, masked, m0 = mh, k == "a2", mh_unit(k, g)
            link = Steps(dve, steps[k], g, STEPS[k])
            if k == "a1":
                link(dve.tensor_copy(y[:, :, :], normed[:, :, :]))
            head_vector(dve, unit_no(k, g) + 1, following(g), link)
            row_maxima(dve, k, m0, 1, link, None if last else lambda: split_queries(dve, k, g + 1, link))
            if k == "a1":
                norm_of(dve, k, g, 0, y, LN_EPS, link)
                rows = w["a1_rows"]
                link(dve.tensor_tensor(y[:, :, :], y[:, :, :], rows[:, None, D:2 * D].to_broadcast([P, TILES, D]), ALU.mult))
                link(dve.tensor_tensor(y[:, :, :], y[:, :, :], rows[:, None, 2 * D:3 * D].to_broadcast([P, TILES, D]), ALU.add))
            if not last:
                row_maxima(dve, k, m0 + 1, 0, link)
            for i in range(TILES):
                dve.wait_ge(s["otb_psum"], m0 * TILES + i + 1)
                parts = bank[:, i, :].rearrange("p (h r) -> p h r", r=QUAD)
                link(dve.reciprocal(mh_rec[:, i, :], parts[:, :, HD]))
                dve.tensor_tensor(mh_on[:, i, :, :], parts[:, :, 0:HD], mh_rec[:, i, :, None].to_broadcast([P, HEADS, HD]),
                                  ALU.mult).then_inc(s["on"], 1)
            dve.wait_ge(s["proj"], m0 + 1)
            if k == "a1":
                dve.tensor_tensor(y[:, :, :], bank[:, 5, :].rearrange("p (t d) -> p t d", d=D), y[:, :, :], ALU.add)\
                   .then_inc(s["proj_read"], 1)
                dve.wait_ge(s["proj_read"], m0 + 1)
                link(dve.tensor_tensor(y[:, :, :], y[:, :, :],
                                       w["a1_rows"][:, None, 3 * D:4 * D].to_broadcast([P, TILES, D]), ALU.add))
            else:
                dve.tensor_tensor(y[:, :, :], bank[:, 5, :].rearrange("p (t d) -> p t d", d=D),
                                  w["a2_rows"][:, None, D:2 * D].to_broadcast([P, TILES, D]), ALU.add).then_inc(s["proj_read"], 1)
                dve.wait_ge(s["proj_read"], m0 + 1)
            tail_vector(dve, k, g, link)
            link.close(0 if not last else 2 * SPLIT)

        def mh_pool(pool, k, g):
            s, left, m0 = mh, mh_room[:, 1, :], mh_unit(k, g)
            for part in range(PARTS - 1):
                pool.wait_ge(s["k_round"], m0 * PARTS + part + 1)
                pool.tensor_tensor(left, left, mh_parts[:, 1, part, :], ALU.subtract).then_inc(s["k_left"], 1)

        def max_rows(act, m, b):
            act.wait_ge(mh["max_parts"], m * PAIR + b + 1)
            for part in range(PARTS):
                row = MAX_ROWS.start + part
                act.dma_start(q_stack[row:row + 1, :, b, :],
                             max_b[QUAD * part:QUAD * part + HEADS, b * SEQ:(b + 1) * SEQ]).then_inc(mh["max_rows"], 16)

        def stacks(sp, k, g, first):
            s, m0 = mh, mh_unit(k, g)

            def to_scr(scr, first, last, c):
                sp.dma_start(scr[first:last].rearrange("a i h t -> (i h) a t"),
                             mh_parts[:, c, 0:last - first, :]).then_inc(s["written"], 16)

            sp.wait_ge(s["q_parts"], m0 + 1)
            to_scr(q_scr, 0, PARTS, 0)
            sp.wait_ge(s["k_round"], (m0 + 1) * PARTS)
            to_scr(k_scr, 0, PARTS, 1)
            to_scr(k_scr, PARTS, 2 * PARTS - 1, 1)
            sp.wait_ge(s["written"], (m0 + 1) * 16 * 3)
            for b in range(PAIR):
                if not first:
                    sp.wait_ge(s["st_psum"], (m0 - 1) * PAIR * HEADS + (b + 1) * HEADS)
                for r in range(PARTS):
                    for stack, scr in ((q_stack, q_scr[:]), (k_stack, k_scr[r:r + PARTS])):
                        sp.dma_start(stack[BLOCK * r:BLOCK * (r + 1), :, b, :],
                                     scr[:, :, :, b * SEQ:(b + 1) * SEQ].rearrange("a i h t -> (a i) h t"))\
                          .then_inc(s[f"stacked{b}"], 16)

        def places(*of):
            return [r[:, n * GT:(n + 1) * GT] for r in of for n in range(r.shape[1] // GT)]

        PLACES = {"f0": places(rooms[1], room_s, mh_parts[:, :, :, :].rearrange("p c a t -> p (c a t)").bitcast(F32)[:, 0:2 * GT],
                               hidden_room),
                  "f1": places(hidden_room, rooms[1]),
                  "f2": places(hidden_room, rooms_ab[1]), "f3": places(hidden_room, rooms_ab[1])}
        RING = {"f0": 4, "f1": 1 + E, "f2": 4, "f3": 4}
        AHEAD = {"f0": 3, "f1": 5, "f2": 3, "f3": 3}

        def hidden(k, i, f, tokens=slice(None)):
            place = i % RING[k] * 4 + f if k != "f1" else f if i == 0 else 1 + i
            return PLACES[k][place][:, tokens]

        THEN = {"f0": "a1", "f1": "a2"}

        logits = sb("logits", [P, TILES, E])
        sel = sb("sel", [P, TILES, E])
        work = sb("work", [P, TILES, E])
        work2 = sb("work2", [P, TILES, E])
        hot1 = sb("hot1", [P, TILES, E])
        hot2 = sb("hot2", [P, TILES, E])
        gates = sb("gates", [P, TILES, E])
        gates_t = sb("gates_t", [E, GT])
        top = sb("top", [P, 8, TILES])
        silu1 = room_s[:, :].rearrange("p (f t) -> p f t", f=2)
        MOE_SEMS = ("logit_psum", "exp_in", "exp_out", "gates", "gt_psum", "gt", "b2_psum", "up_psum", "hidden", "down_psum", "added", "silu", "shared")
        ONLY = {"gates": ("f0", "f3"), "gt_psum": ("f0", "f3"), "gt": ("f0", "f3"), "b2_psum": ("f0", "f3"),
                "silu": ("f1",), "shared": ("f1",)}
        moe = {k: {s: sem(f"{k}_{s}") for s in MOE_SEMS if k in ONLY.get(s, (k,))} for k in ("f0", "f1", "f2", "f3")}

        EXPERTS = {"f0": [(4, e) for e in range(E)], "f1": [(2, None)] + [(1, e) for e in range(E)],
                   "f2": [(4, None)] + [(4, e) for e in range(E)], "f3": [(4, e) for e in range(E)]}

        def up_tiles(k, i):
            return sum((2 if k == "f1" and gate is None else 1) * n for n, gate in EXPERTS[k][:i])

        def hid_tiles(k, i):
            return sum(n for n, _ in EXPERTS[k][:i])

        def moe_tensor(pe, k, g, last):
            s, ex, up, down = moe[k], EXPERTS[k], w[f"{k}_up"], w[f"{k}_down"]
            n_shared = 4 if k == "f1" else 0
            own = up_tiles(k, len(ex)) - n_shared
            pe.wait_ge(normed_t_ready, unit_no(k, g) + 1)
            for i in range(TILES):
                m = pe.matmul(bank[:, 6, i * E:(i + 1) * E], normed_t[:, i * P:(i + 1) * P], w[f"{k}_wr"][:, :],
                              start=True, stop=True)
            m.then_inc(s["logit_psum"], 1)

            def up_to(i):
                n_tiles, gate = ex[i]
                n_up = 2 * n_tiles if k == "f1" and gate is None else n_tiles
                for f in range(n_up):
                    u = up_tiles(k, i) + f
                    if u >= 4:
                        if k == "f1" and u < 6:
                            pe.wait_ge(s["silu"], g * 2 + u - 4 + 1)
                        elif k == "f1" and u < 8:
                            pe.wait_ge(s["shared"], g * 2 + u - 6 + 1)
                        else:
                            pe.wait_ge(s["hidden"], g * own + u - 4 - n_shared + 1)
                    pe.matmul(bank[:, u % 4, :], up[:, u * P:(u + 1) * P], normed_t[:, :], start=True, stop=True)\
                      .then_inc(s["up_psum"], 1)

            def down_from(i):
                n_tiles, _ = ex[i]
                h0 = hid_tiles(k, i)
                if k == "f1" and i == 0:
                    pe.wait_ge(s["shared"], (g + 1) * 2)
                else:
                    pe.wait_ge(s["hidden"], g * own + up_tiles(k, i) + n_tiles - n_shared)
                if i < 2:
                    past_outputs(pe, k, g)
                else:
                    pe.wait_ge(s["added"], g * len(ex) + i - 1)
                for t_ in range(TILES):
                    for f in range(n_tiles):
                        m = pe.matmul(bank[:, 4 + i % 2, t_ * D:(t_ + 1) * D], hidden(k, i, f, slice(t_ * P, (t_ + 1) * P)),
                                      down[:, (h0 + f) * D:(h0 + f + 1) * D], start=f == 0, stop=f == n_tiles - 1)
                m.then_inc(s["down_psum"], 1)

            for i in range(AHEAD[k]):
                up_to(i)
            for i in range(len(ex)):
                if i + AHEAD[k] < len(ex):
                    up_to(i + AHEAD[k])
                if i == 3 and k in ("f0", "f3"):
                    pe.wait_ge(s["gates"], g + 1)
                    for t_ in range(TILES):
                        m = pe.transpose(bank[0:E, 7, t_ * P:(t_ + 1) * P], gates[:, t_, :], ident[:, :])
                    m.then_inc(s["gt_psum"], 1)
                    pe.wait_ge(s["gt"], g + 1)
                    for t_ in range(TILES):
                        m = pe.matmul(bank[:, 6, t_ * D:(t_ + 1) * D], gates_t[:, t_ * P:(t_ + 1) * P], w[f"{k}_b2"][:, :],
                                      start=True, stop=True)
                    m.then_inc(s["b2_psum"], 1)
                if i == len(ex) - AHEAD[k]:
                    head_tensor(pe, unit_no(k, g) + 1, 7)
                if i == len(ex) - AHEAD[k] + 1 and last and k in THEN:
                    for c in range(2):
                        qk_tensor(pe, THEN[k], 0, c, 7 - c)
                down_from(i)

        def moe_scalar(act, k, g, last):
            s, ex = moe[k], EXPERTS[k]
            ups = up_tiles(k, len(ex))

            def gate_exponential():
                act.wait_ge(s["exp_in"], g + 1)
                if k == "f1":
                    m = act.activation(work[:, :, :], logits[:, :, :], ACT.Exp, scale=-1.0)
                elif k == "f2":
                    m = act.activation(work[:, :, :], work[:, :, :], ACT.Exp)
                else:
                    m = act.activation(top[:, 5, :], top[:, 4, :], ACT.Exp)
                m.then_inc(s["exp_out"], 1)

            for i, (n_tiles, gate) in enumerate(ex):
                if i == AHEAD[k]:
                    gate_exponential()
                if k == "f1" and gate is None:
                    for f in range(n_tiles):
                        act.wait_ge(s["up_psum"], g * ups + f + 1)
                        act.activation(silu1[:, f, :], bank[:, f, :], ACT.Silu).then_inc(s["silu"], 1)
                    continue
                if i >= RING[k]:
                    act.wait_ge(s["down_psum"], g * len(ex) + i - RING[k] + 1)
                for f in range(n_tiles):
                    u = up_tiles(k, i) + f
                    act.wait_ge(s["up_psum"], g * ups + u + 1)
                    func = ACT.Relu if k == "f3" else ACT.Gelu
                    if k in ("f0", "f3"):
                        m = act.activation(hidden(k, i, f), bank[:, u % 4, :], func, bias=w[f"{k}_b1"][:, u:u + 1])
                    else:
                        m = act.activation(hidden(k, i, f), bank[:, u % 4, :], func)
                    m.then_inc(s["hidden"], 1)
            head_scalar(act, unit_no(k, g) + 1, 7)
            if last and k in THEN:
                qk_scalar(act, THEN[k], 0, (7, 6))
                for part in range(PARTS):
                    round_keys(act, THEN[k], 0, part)

        def moe_vector(dve, k, g, last):
            s, ex = moe[k], EXPERTS[k]
            ups = up_tiles(k, len(ex))
            link = Steps(dve, steps[k], g, STEPS[k])
            dve.wait_ge(s["logit_psum"], g + 1)
            logit_psum = bank[:, 6, 0:TILES * E].rearrange("p (t e) -> p t e", e=E)

            def spread(a):
                return a[:, :, None].to_broadcast([P, TILES, E])

            def top_one(scores, best, hot):
                link(dve.tensor_reduce(best, scores, AX_X, ALU.max))
                link(dve.tensor_tensor(work2[:, :, :], scores, spread(best), ALU.is_ge))
                link(dve.tensor_tensor(work2[:, :, :], work2[:, :, :], rank8[:, :, :], ALU.mult))
                link(dve.tensor_reduce(top[:, 7, :], work2[:, :, :], AX_X, ALU.max))
                link(dve.tensor_tensor(hot, work2[:, :, :], spread(top[:, 7, :]), ALU.is_equal))

            def top_two(scores):
                top_one(scores, top[:, 0, :], hot1[:, :, :])
                link(dve.scalar_tensor_tensor(sel[:, :, :], hot1[:, :, :], BELOW, scores, ALU.mult, ALU.add))
                top_one(sel[:, :, :], top[:, 1, :], hot2[:, :, :])

            if k in ("f0", "f3"):
                link(dve.tensor_tensor(logits[:, :, :], logit_psum, w[f"{k}_br"][:, :, :], ALU.add))
                top_two(logits[:, :, :])
                dve.tensor_tensor(top[:, 4, :], top[:, 1, :], top[:, 0, :], ALU.subtract).then_inc(s["exp_in"], 1)
                dve.wait_ge(s["exp_out"], g + 1)
                link(dve.tensor_scalar(top[:, 6, :], top[:, 5, :], 1.0, None, ALU.add))
                link(dve.reciprocal(top[:, 2, :], top[:, 6, :]))
                link(dve.tensor_tensor(top[:, 3, :], top[:, 5, :], top[:, 2, :], ALU.mult))
                link(dve.tensor_tensor(hot1[:, :, :], hot1[:, :, :], spread(top[:, 2, :]), ALU.mult))
                link(dve.tensor_tensor(hot2[:, :, :], hot2[:, :, :], spread(top[:, 3, :]), ALU.mult))
                dve.tensor_tensor(gates[:, :, :], hot1[:, :, :], hot2[:, :, :], ALU.add).then_inc(s["gates"], 1)
            elif k == "f1":
                dve.tensor_copy(logits[:, :, :], logit_psum).then_inc(s["exp_in"], 1)
                for f in range(2):
                    dve.wait_ge(s["silu"], g * 2 + f + 1)
                    dve.wait_ge(s["up_psum"], g * ups + 2 + f + 1)
                    dve.tensor_tensor(hidden(k, 0, f), bank[:, 2 + f, :], silu1[:, f, :], ALU.mult).then_inc(s["shared"], 1)
                dve.wait_ge(s["exp_out"], g + 1)
                link(dve.tensor_scalar(work[:, :, :], work[:, :, :], 1.0, None, ALU.add))
                link(dve.reciprocal(gates[:, :, :], work[:, :, :]))
                link(dve.tensor_tensor(logits[:, :, :], gates[:, :, :], w["f1_br"][:, :, :], ALU.add))
                top_two(logits[:, :, :])
                link(dve.tensor_tensor(hot1[:, :, :], hot1[:, :, :], hot2[:, :, :], ALU.add))
                link(dve.tensor_tensor(gates[:, :, :], gates[:, :, :], hot1[:, :, :], ALU.mult))
                link(dve.tensor_reduce(top[:, 2, :], gates[:, :, :], AX_X, ALU.add))
                link(dve.tensor_scalar(top[:, 3, :], top[:, 2, :], 1e-9, None, ALU.is_gt))
                link(dve.tensor_scalar(top[:, 4, :], top[:, 2, :], 1e-9, None, ALU.add))
                link(dve.reciprocal(top[:, 5, :], top[:, 4, :]))
                link(dve.tensor_tensor(top[:, 5, :], top[:, 5, :], top[:, 3, :], ALU.mult))
                link(dve.tensor_scalar(top[:, 6, :], top[:, 3, :], -0.5, 0.5, ALU.mult, ALU.add))
                link(dve.tensor_tensor(gates[:, :, :], gates[:, :, :], spread(top[:, 5, :]), ALU.mult))
                link(dve.tensor_tensor(hot1[:, :, :], hot1[:, :, :], spread(top[:, 6, :]), ALU.mult))
                link(dve.tensor_tensor(gates[:, :, :], gates[:, :, :], hot1[:, :, :], ALU.add))
            else:
                link(dve.tensor_reduce(top[:, 2, :], logit_psum, AX_X, ALU.max))
                dve.tensor_tensor(work[:, :, :], logit_psum, spread(top[:, 2, :]), ALU.subtract).then_inc(s["exp_in"], 1)
                dve.wait_ge(s["exp_out"], g + 1)
                link(dve.tensor_reduce(top[:, 3, :], work[:, :, :], AX_X, ALU.add))
                link(dve.reciprocal(top[:, 4, :], top[:, 3, :]))
                link(dve.tensor_tensor(logits[:, :, :], work[:, :, :], spread(top[:, 4, :]), ALU.mult))
                top_two(logits[:, :, :])
                link(dve.tensor_tensor(hot1[:, :, :], hot1[:, :, :], hot2[:, :, :], ALU.add))
                link(dve.tensor_tensor(gates[:, :, :], logits[:, :, :], hot1[:, :, :], ALU.mult))

            if k in ("f0", "f3"):
                dve.wait_ge(s["gates"], g + 1)
            for i, (_, gate) in enumerate(ex):
                if i == 3 and k in ("f0", "f3"):
                    dve.wait_ge(s["gt_psum"], g + 1)
                    dve.tensor_copy(gates_t[:, :], bank[0:E, 7, :]).then_inc(s["gt"], 1)
                if i == 4 and k in ("f0", "f3"):
                    dve.wait_ge(s["b2_psum"], g + 1)
                    link(dve.tensor_tensor(y[:, :, :], bank[:, 6, :].rearrange("p (t d) -> p t d", d=D), y[:, :, :], ALU.add))
                if i == len(ex) - AHEAD[k] - 1:
                    head_vector(dve, unit_no(k, g) + 1, following(g), link)
                if i == len(ex) - 1 and last and k in THEN:
                    first = Steps(dve, first_qk, 0 if k == "f0" else 1, SPLIT)
                    split_queries(dve, THEN[k], 0, first)
                    first.close()
                dve.wait_ge(s["down_psum"], g * len(ex) + i + 1)
                for t_ in range(TILES):
                    part = bank[:, 4 + i % 2, t_ * D:(t_ + 1) * D]
                    if k == "f3" and i == 0:
                        m = dve.tensor_scalar(y[:, t_, :], part, gates[:, t_, gate:gate + 1], None, ALU.mult)
                    elif k == "f0" and i == 0:
                        m = dve.scalar_tensor_tensor(y[:, t_, :], part, gates[:, t_, gate:gate + 1], normed[:, t_, :],
                                                     ALU.mult, ALU.add)
                    elif gate is not None:
                        m = dve.scalar_tensor_tensor(y[:, t_, :], part, gates[:, t_, gate:gate + 1], y[:, t_, :],
                                                     ALU.mult, ALU.add)
                    elif k == "f1":
                        m = dve.tensor_copy(y[:, t_, :], part)
                    else:
                        m = dve.tensor_tensor(y[:, t_, :], part, normed[:, t_, :], ALU.add)
                m.then_inc(s["added"], 1)
                dve.wait_ge(s["added"], g * len(ex) + i + 1)
            if k == "f0":
                norm_of(dve, k, g, 0, y, 1e-12, link)
                link(dve.tensor_tensor(y[:, :, :], y[:, :, :], w["f0_ln"][:, None, 0:D].to_broadcast([P, TILES, D]), ALU.mult))
                link(dve.tensor_tensor(y[:, :, :], y[:, :, :], w["f0_ln"][:, None, D:2 * D].to_broadcast([P, TILES, D]), ALU.add))
            tail_vector(dve, k, g, link)
            link.close()

        ROW = HALVES * GT
        SSM_SEMS = ("x_psum", "z_psum", "x_raw", "conv", "xc", "bc_psum", "dt_psum", "v", "e", "w1", "ln", "dt", "round", "left", "y0",
                    "bb", "cb", "decay", "c_sb", "dbx", "h", "hc", "y_part", "y_all", "yz", "proj", "out")
        ss = {s: sem(f"a3_{s}") for s in SSM_SEMS}
        def halves(a):
            return a.rearrange("p (h t) -> p h t", h=HALVES)

        def two(a):
            return a.rearrange("p (i h t) -> p i h t", i=2, h=HALVES)

        hs, hc, decay = two(rooms[0][:, :]), two(rooms[1][:, :]), two(rooms[4][:, :])
        xc, zs = halves(rooms[5][:, 0:ROW]), halves(rooms[5][:, ROW:2 * ROW])
        dt_s, u_in = halves(rooms[3][:, 0:ROW]), halves(rooms[3][:, ROW:2 * ROW])
        c_sb = halves(room_s[:, :])
        raw_words = HALVES * PAIR * (TAPS - 1 + SEQ)
        x_raw = rooms[2][:, 0:raw_words].rearrange("p (h b t) -> p h b t", h=HALVES, b=PAIR)
        bc_stack = mh_parts[0:PARTS * QUAD, :, :, :].rearrange("p c a t -> p (c a) t")[:, 0:4, :]
        bc_left = hidden_room[0:PARTS * QUAD, 0:4 * GT].rearrange("p (c t) -> p c t", c=4)
        dbx = hidden_room[:, :].rearrange("p (s h t) -> p s h t", s=4, h=HALVES)
        a_neg = sb("a_neg", [P, HALVES, N_STATE])
        d_diag = sb("d_diag", [P, HALVES, P])
        tmp_a, tmp_b, tmp_c = hs[:, 0, :, :], hs[:, 1, :, :], hc[:, 0, :, :]
        vec = w["a3_vec"]
        DT_BIAS, CONV_B, SKIP = TAPS, TAPS + 1, TAPS + 2

        def conv_tensor(pe, g):
            pe.wait_ge(normed_t_ready, unit_no("a3", g) + 1)
            for h in range(HALVES):
                pe.matmul(bank[:, 2 + h, :], w["a3_win"][:, h * P:(h + 1) * P], normed_t[:, :], start=True, stop=True)\
                  .then_inc(ss["x_psum"], 1)

        def conv_scalar(act, g):
            for h in range(HALVES):
                act.wait_ge(ss["x_psum"], g * HALVES + h + 1)
                act.activation(x_raw[:, h, :, TAPS - 1:], bank[:, 2 + h, :].rearrange("p (b t) -> p b t", b=PAIR), ACT.Copy)\
                   .then_inc(ss["x_raw"], 1)

        def conv_vector(dve, g, link):
            for h in range(HALVES):
                dve.wait_ge(ss["x_raw"], g * HALVES + h + 1)
                acc = u_in[:, h, :].rearrange("p (b t) -> p b t", b=PAIR)
                for k in range(TAPS):
                    x_k = x_raw[:, h, :, k:k + SEQ]
                    if k == 0:
                        link(dve.tensor_scalar(acc, x_k, vec[:, h, 0:1], None, ALU.mult))
                    elif k < TAPS - 1:
                        link(dve.scalar_tensor_tensor(acc, x_k, vec[:, h, k:k + 1], acc, ALU.mult, ALU.add))
                    else:
                        dve.scalar_tensor_tensor(acc, x_k, vec[:, h, k:k + 1], acc, ALU.mult, ALU.add).then_inc(ss["conv"], 1)

        def ssm_tensor(pe, g, last):
            for h in range(HALVES):
                pe.matmul(bank[:, h, :], w["a3_win"][:, (HALVES + h) * P:(HALVES + h + 1) * P], normed_t[:, :],
                          start=True, stop=True).then_inc(ss["z_psum"], 1)
            pe.wait_ge(ss["xc"], (g + 1) * HALVES)
            rows = PARTS * QUAD
            for h in range(HALVES):
                m = pe.matmul(bank[:, 3, :], w["a3_wx"][:, h, 4 * rows:4 * rows + P], xc[:, h, :], start=h == 0, stop=h == HALVES - 1)
            m.then_inc(ss["dt_psum"], 1)
            past_outputs(pe, "a3", g)
            for n in range(4):
                for h in range(HALVES):
                    m = pe.matmul(bank[0:rows, 4 + n, :], w["a3_wx"][:, h, n * rows:(n + 1) * rows], xc[:, h, :],
                                  start=h == 0, stop=h == HALVES - 1)
                m.then_inc(ss["bc_psum"], 1)
            for h in range(HALVES):
                m = pe.matmul(bank[:, h, :], d_diag[:, h, :], xc[:, h, :], start=True, stop=False, skip_group_check=True)
            m.then_inc(ss["y0"], 1)
            pe.wait_ge(ss["round"], (g + 1) * 4 * PARTS)

            def spread(c, m, i):
                pe.matmul(bank[:, 4 + 2 * c + i, :], row_sel[:, bass.ds(m, 1)].to_broadcast([rows, P]), bc_stack[:, 2 * c + i, :],
                          start=True, stop=True).then_inc(ss["cb" if c else "bb"], 1)

            def spread_b(q, m, i):
                pe.wait_ge(ss["dbx"], g * N_STATE + q + 1)
                spread(0, m + 1, i)

            def spread_c(q, m, i):
                pe.wait_ge(ss["c_sb"], g * N_STATE + q + 1)
                spread(1, m + 1, i)

            def collect(q, i):
                pe.wait_ge(ss["hc"], g * N_STATE + q + 1)
                for h in range(HALVES):
                    m = pe.matmul(bank[:, h, :], ident[:, :], hc[:, i, h, :], start=False, stop=False, skip_group_check=True)
                m.then_inc(ss["y_part"], 1)

            for i in range(2):
                spread(0, 0, i)
                spread(1, 0, i)
            for i in range(2):
                spread_b(i, 0, i)
                spread_c(i, 0, i)
            with pe.Fori(1, N_STATE // 2 - 1) as m:
                for i in range(2):
                    spread_b(m * 2 + i, m, i)
                    collect(m * 2 + i - 2, i)
                    spread_c(m * 2 + i, m, i)
            for q in range(N_STATE - 4, N_STATE):
                collect(q, q % 2)
            head_tensor(pe, unit_no("a3", g) + 1, 2)
            if not last:
                conv_tensor(pe, g + 1)
            pe.wait_ge(ss["yz"], (g + 1) * HALVES)
            for t_ in range(TILES):
                for h in range(HALVES):
                    m = pe.matmul(bank[:, 4, t_ * D:(t_ + 1) * D], xc[:, h, t_ * P:(t_ + 1) * P], w["a3_wout"][:, h, :],
                                  start=h == 0, stop=h == HALVES - 1)
            m.then_inc(ss["proj"], 1)

        def ssm_scalar(act, g, last):
            for h in range(HALVES):
                act.wait_ge(ss["z_psum"], g * HALVES + h + 1)
                act.activation(zs[:, h, :], bank[:, h, :], ACT.Silu)
            for h in range(HALVES):
                act.wait_ge(ss["conv"], g * HALVES + h + 1)
                act.activation(xc[:, h, :], u_in[:, h, :], ACT.Silu, bias=vec[:, h, CONV_B:CONV_B + 1]).then_inc(ss["xc"], 1)
            def round_parts(part):
                for c in range(4):
                    if part == 0:
                        act.wait_ge(ss["bc_psum"], g * 4 + c + 1)
                    else:
                        act.wait_ge(ss["left"], g * 4 * (PARTS - 1) + (part - 1) * 4 + c + 1)
                    source = bank[0:PARTS * QUAD, 4 + c, :] if part == 0 else bc_left[:, c, :]
                    act.activation(bc_stack[:, c, :], source, ACT.Copy).then_inc(ss["round"], 1)

            act.wait_ge(ss["v"], (g + 1) * HALVES)
            act.activation(tmp_b, tmp_b, ACT.Exp, scale=-1.0).then_inc(ss["e"], 1)
            round_parts(0)
            act.wait_ge(ss["w1"], g + 1)
            act.activation(u_in[:, :, :], tmp_c, ACT.Ln).then_inc(ss["ln"], 1)
            round_parts(1)
            round_parts(2)
            act.wait_ge(ss["dt"], g + 1)

            def one(m, i, first):
                n = m * 2 + i
                if not first:
                    act.wait_ge(ss["h"], g * N_STATE + n - 1)
                for h in range(HALVES):
                    a = act.activation(decay[:, i, h, :].rearrange("p (b t) -> p b t", b=PAIR)[:, :, 1:],
                                       dt_s[:, h, :].rearrange("p (b t) -> p b t", b=PAIR)[:, :, 1:], ACT.Exp,
                                       scale=a_neg[:, h, bass.ds(m + i * QUAD, 1)])
                a.then_inc(ss["decay"], 1)
                act.wait_ge(ss["cb"], g * N_STATE + n + 1)
                if not first:
                    act.wait_ge(ss["hc"], g * N_STATE + n - 1)
                act.activation(c_sb[:, i, :], bank[:, 6 + i, :], ACT.Copy).then_inc(ss["c_sb"], 1)

            for i in range(2):
                one(0, i, True)
            with act.Fori(1, N_STATE // 2) as m:
                for i in range(2):
                    one(m, i, False)
            head_scalar(act, unit_no("a3", g) + 1, 2)
            if not last:
                conv_scalar(act, g + 1)

        def ssm_pool(pool, g):
            def one(n, i):
                pool.wait_ge(ss["h"], g * N_STATE + n + 1)
                pool.wait_ge(ss["c_sb"], g * N_STATE + n + 1)
                pool.tensor_tensor(hc[:, i, :, :], hs[:, i, :, :], c_sb[:, i:i + 1, :].to_broadcast([P, HALVES, GT]), ALU.mult)\
                    .then_inc(ss["hc"], 1)

            for i in range(2):
                one(i, i)
            with pool.Fori(1, N_STATE // 2 - 1) as n2:
                for i in range(2):
                    pool.wait_ge(ss["y_part"], g * N_STATE + n2 * 2 + i - 1)
                    one(n2 * 2 + i, i)
            head_pool(pool, unit_no("a3", g) + 1)
            for i in range(2):
                pool.wait_ge(ss["y_part"], (g + 1) * N_STATE - 2 + i - 1)
                one(N_STATE - 2 + i, i)

        def ssm_vector(dve, g, last):
            link = Steps(dve, steps["a3"], g, STEPS["a3"])
            dve.wait_ge(ss["dt_psum"], g + 1)
            for h in range(HALVES):
                link(dve.tensor_scalar(tmp_a[:, h, :], bank[:, 3, :], vec[:, h, DT_BIAS:DT_BIAS + 1], None, ALU.add))
                dve.scalar_tensor_tensor(tmp_b[:, h, :], tmp_a[:, h, :], -1.0, tmp_a[:, h, :], ALU.mult, ALU.max).then_inc(ss["v"], 1)

            def take_parts(part):
                for c in range(4):
                    dve.wait_ge(ss["round"], g * 4 * PARTS + part * 4 + c + 1)
                    if part > 0:
                        dve.wait_ge(ss["left"], g * 4 * (PARTS - 1) + (part - 1) * 4 + c + 1)
                    source = bank[0:PARTS * QUAD, 4 + c, :] if part == 0 else bc_left[:, c, :]
                    dve.scalar_tensor_tensor(bc_left[:, c, :], bc_stack[:, c, :], w["part_masks"][0:PARTS * QUAD, part:part + 1],
                                             source, ALU.mult, ALU.add).then_inc(ss["left"], 1)

            dve.wait_ge(ss["e"], g + 1)
            dve.tensor_scalar(tmp_c, tmp_b, 1.0, None, ALU.add).then_inc(ss["w1"], 1)
            take_parts(0)
            dve.wait_ge(ss["w1"], g + 1)
            link(dve.scalar_tensor_tensor(tmp_b, tmp_c, 1.0, tmp_b, ALU.subtract, ALU.subtract))
            dve.wait_ge(ss["ln"], g + 1)
            link(dve.tensor_tensor(tmp_c, u_in[:, :, :], tmp_b, ALU.subtract))
            dve.scalar_tensor_tensor(dt_s[:, :, :], tmp_a, 0.0, tmp_c, ALU.max, ALU.add).then_inc(ss["dt"], 1)
            take_parts(1)
            dve.wait_ge(ss["dt"], g + 1)
            link(dve.tensor_tensor(u_in[:, :, :], dt_s[:, :, :], xc[:, :, :], ALU.mult))

            def products(q, r):
                dve.wait_ge(ss["bb"], g * N_STATE + q + 1)
                if not (isinstance(q, int) and q < 4):
                    dve.wait_ge(ss["h"], g * N_STATE + q - 3)
                i = r % 2
                dve.tensor_tensor(dbx[:, r, :, :], u_in[:, :, :], bank[:, 4 + i:5 + i, :].to_broadcast([P, HALVES, GT]), ALU.mult)\
                   .then_inc(ss["dbx"], 1)

            def scan(q, r):
                dve.wait_ge(ss["dbx"], g * N_STATE + q + 1)
                dve.wait_ge(ss["decay"], g * N_STATE + q + 1)
                i = r % 2
                if not (isinstance(q, int) and q < 2):
                    dve.wait_ge(ss["hc"], g * N_STATE + q - 1)
                dve.tensor_tensor_scan(hs[:, i, :, :].rearrange("p h t -> p (h t)"),
                                       decay[:, i, :, :].rearrange("p h t -> p (h t)"),
                                       dbx[:, r, :, :].rearrange("p h t -> p (h t)"), 0.0, ALU.mult, ALU.add).then_inc(ss["h"], 1)

            dve.wait_ge(ss["round"], (g + 1) * 4 * PARTS)
            products(0, 0)
            for q in range(4):
                products(q + 1, (q + 1) % 4)
                scan(q, q)
            with dve.Fori(1, N_STATE // 4 - 1) as q4:
                for r in range(4):
                    products(q4 * 4 + r + 1, (r + 1) % 4)
                    scan(q4 * 4 + r, r)
            for q in range(N_STATE - 4, N_STATE):
                if q + 1 < N_STATE:
                    products(q + 1, (q + 1) % 4)
                scan(q, q % 4)
                if q == N_STATE - 3:
                    head_moments(dve, following(g), link)
            head_normalize(dve, unit_no("a3", g) + 1, following(g))
            dve.wait_ge(ss["y_part"], (g + 1) * N_STATE)
            for h in range(HALVES):
                dve.tensor_tensor(xc[:, h, :], bank[:, h, :], zs[:, h, :], ALU.mult).then_inc(ss["yz"], 1)
            if not last:
                conv_vector(dve, g + 1, link)
            dve.wait_ge(ss["proj"], g + 1)
            dve.tensor_copy(y[:, :, :], bank[:, 4, :].rearrange("p (t d) -> p t d", d=D)).then_inc(ss["out"], 1)
            dve.wait_ge(ss["out"], g + 1)
            tail_vector(dve, "a3", g, link)
            link.close(CONV if last else 0)

        with_x = t["x"].rearrange("(g t p) d -> g p t d", t=TILES, p=P)
        out_x = out.rearrange("(g t p) d -> g p t d", t=TILES, p=P)
        LOADS = {
            "const": ["ident", "rank8", "causal2", "row_sel", "part_masks"],
            "a0": ["a0_w", "a0_rel", "a0_mask", "a0_slope"],
            "a1": ["a1_w", "a1_rows", "a1_across", "a1_down", "a1_inside", "a1_part"],
            "a2": ["a2_w", "a2_qkb", "a2_rows", "a2_pos"],
            "a3": ["a3_win", "a3_wx", "a3_wout", "a3_vec", "a3_alog"],
            "f0": ["f0_wr", "f0_br", "f0_b1", "f0_b2", "f0_ln", "f0_up", "f0_down"],
            "f1": ["f1_wr", "f1_br", "f1_up", "f1_down"],
            "f2": ["f2_wr", "f2_up", "f2_down"],
            "f3": ["f3_wr", "f3_br", "f3_b1", "f3_b2", "f3_up", "f3_down"],
        }
        causal2_f = rooms[4][:, 0:2 * P].rearrange("p (a c) -> p a c", a=2)
        row_sel_f = rooms[4][0:PARTS * QUAD, 4 * P:4 * P + QUAD]
        tiles = dict(w, ident=ident, rank8=rank8, causal2=causal2_f, row_sel=row_sel_f)

        def need(engine, *names):
            for k in names:
                engine.wait_ge(loaded[k], 16 * (GROUPS if k == "x" else len(LOADS[k])))

        SETUP_SQUARES, SETUP_MAX, SETUP_ALL = 16, 17, 38

        block = ctx.enter_context(nc.Block())

        @block.sync
        def _(sp):
            for g in range(GROUPS):
                sp.dma_start(stream[:, g * TILES:(g + 1) * TILES, :], with_x[g]).then_inc(loaded["x"], 16)

            def load(k):
                for name in LOADS[k]:
                    to = tiles[name]
                    sp.dma_start(to[tuple([slice(None)] * len(to.shape))], t[name]).then_inc(loaded[k], 16)

            for k in LOADS:
                if k != "f3":
                    load(k)
            sp.wait_ge(k_rows, 3)
            for k in ("a1", "a2"):
                if k == "a2":
                    sp.wait_ge(setup, SETUP_ALL)
                    sp.dma_start(pos_scr.rearrange("a h t -> h a t"), pos_b[:, :, :]).then_inc(pos_done, 16)
                    sp.wait_ge(pos_done, 16)
                    sp.wait_ge(mh["st_psum"], GROUPS * PAIR * HEADS)
                    for b in range(PAIR):
                        sp.dma_start(k_stack[POS_ROWS, :, b, :], pos_scr).then_inc(pos_done, 16)
                stacks(sp, k, 0, True)
                with sp.Fori(1, GROUPS) as g:
                    stacks(sp, k, g, False)
            load("f3")
            sp.wait_ge(steps["f3"], GROUPS * STEPS["f3"])
            for g in range(GROUPS):
                sp.dma_start(out_x[g], stream[:, g * TILES:(g + 1) * TILES, :]).then_inc(stored, 16)
            sp.wait_ge(stored, 16 * GROUPS)

        PEELED = ("f0", "a1", "f1", "a2", "a3")

        def unit_pool(pool, k, g, last):
            if k == "a3":
                ssm_pool(pool, g)
                norm_pool(pool, k, g, 0)
                return
            head_pool(pool, unit_no(k, g) + 1)
            if k in ("a1", "a2") and not last:
                mh_pool(pool, k, g + 1)
            if last and k in THEN:
                mh_pool(pool, THEN[k], 0)
            if norms_per[k] == 2:
                norm_pool(pool, k, g, 0)
            norm_pool(pool, k, g, norms_per[k] - 1)

        @block.gpsimd
        def _(pool):
            pool.memset(minus_half[:, :], -0.5).then_inc(pool_setup, 1)
            pool.wait_ge(setup, SETUP_MAX)
            pool.partition_all_reduce(far_all[:, :], far[:, :], P, bass.bass_isa.ReduceOp.max).then_inc(pool_setup, 1)

            pool.wait_ge(pool_setup, 2)
            head_pool(pool, 0)
            for k in blocks:
                if k == "f0":
                    pool.wait_ge(rstd_ready, GROUPS)
                    for n, (stack, quad, value) in enumerate(((q_stack, 2, 1.0), (k_stack, 2, 0.0), (k_stack, 3, 1.0))):
                        pool.memset(stack[quad * QUAD:(quad + 1) * QUAD, :, :, :], value).then_inc(k_rows, 1)
                        pool.wait_ge(k_rows, n + 1)
                with pool.Fori(0, GROUPS - (k in PEELED)) as g:
                    unit_pool(pool, k, g, False)
                if k in PEELED:
                    unit_pool(pool, k, GROUPS - 1, True)

        def unit_scalar(act, k, g, last):
            if k == "a0":
                a0_scalar(act, g)
            elif k in ("a1", "a2"):
                mh_scalar(act, k, g, last)
            elif k == "a3":
                ssm_scalar(act, g, last)
            else:
                moe_scalar(act, k, g, last)

        @block.scalar
        def _(act):
            act.wait_ge(setup, SETUP_SQUARES)
            act.activation(a1_dist[:, :, :], a1_dist[:, :, :], ACT.Sqrt).then_inc(act_setup, 1)
            need(act, "a3")
            act.activation(a_neg[:, :, :], w["a3_alog"][:, :, :], ACT.Exp).then_inc(act_setup, 1)
            act.wait_ge(setup, SETUP_ALL)
            need(act, "f0", "a1", "a2")
            head_scalar(act, 0, 7)
            for k in blocks:
                if k == "f3":
                    need(act, "f3")
                if k in ("a1", "a2"):
                    max_rows(act, mh_unit(k, 0), 0)
                if k == "a3":
                    conv_scalar(act, 0)
                with act.Fori(0, GROUPS - (k in PEELED)) as g:
                    unit_scalar(act, k, g, False)
                if k in PEELED:
                    unit_scalar(act, k, GROUPS - 1, True)

        def banks_free(pe, before):
            if before in moe:
                pe.wait_ge(moe[before]["added"], GROUPS * len(EXPERTS[before]))
            elif before in ("a1", "a2"):
                pe.wait_ge(mh["proj_read"], mh_unit(before, GROUPS - 1) + 1)
            elif before == "a3":
                pe.wait_ge(ss["out"], GROUPS)
            else:
                pe.wait_ge(steps[before], GROUPS * STEPS[before] - TAIL)

        def unit_tensor(pe, k, g, last):
            if k == "a0":
                a0_tensor(pe, g)
            elif k in ("a1", "a2"):
                mh_tensor(pe, k, g, last)
            elif k == "a3":
                ssm_tensor(pe, g, last)
            else:
                moe_tensor(pe, k, g, last)

        @block.tensor
        def _(pe):
            pe.wait_ge(setup, SETUP_ALL)
            for k in blocks:
                need(pe, k)
                if k == "a2":
                    pe.wait_ge(pos_done, 16 * (1 + PAIR))
                if k == "a0":
                    head_tensor(pe, 0, 7)
                else:
                    banks_free(pe, blocks[blocks.index(k) - 1])
                if k in ("a1", "a2"):
                    for c in range(CHUNKS):
                        row_chunk(pe, k, mh_unit(k, 0), 0, c)
                    turned_maxima(pe, mh_unit(k, 0), 0)
                if k == "a3":
                    conv_tensor(pe, 0)
                with pe.Fori(0, GROUPS - (k in PEELED)) as g:
                    unit_tensor(pe, k, g, False)
                if k in PEELED:
                    unit_tensor(pe, k, GROUPS - 1, True)

        def unit_vector(dve, k, g, last):
            if k == "a0":
                a0_vector(dve, g)
            elif k in ("a1", "a2"):
                mh_vector(dve, k, g, last)
            elif k == "a3":
                ssm_vector(dve, g, last)
            else:
                moe_vector(dve, k, g, last)

        @block.vector
        def _(dve):
            link = Steps(dve, setup, 0, SETUP_ALL)
            link(dve.memset(rooms[0][:, :], 0.0))
            link(dve.memset(mh_v[:, :, :, HD:HD + 1], 1.0))
            dve.memset(ones_row[:, :], 1.0)
            link(dve.memset(mh_max[:, :, :, :], 0.0))
            dve.memset(a1_last3[:, :], 0.0)
            link(dve.memset(a1_one3[:, :], 0.0))
            link(dve.memset(a1_one3[:, 0:1], 1.0))
            need(dve, "const", "a0", "a1", "a2", "a3")
            link(dve.tensor_copy(ident_b[:, :], ident[:, :]))
            link(dve.tensor_copy(causal[:, :], causal2_f[:, 0, :]))
            link(dve.tensor_copy(causal_t[:, :], causal2_f[:, 1, :]))
            link(dve.tensor_copy(row_sel[:, :], row_sel_f))
            link(dve.scalar_tensor_tensor(a0_bias[:, :], w["a0_rel"][:, :], w["a0_slope"][:, 0:1], w["a0_mask"][:, :],
                                          ALU.mult, ALU.add))
            for n in range(2):
                dx, dy = a1_dist[:, n, :], a1_dy[:, :]
                link(dve.tensor_scalar(dx, w["a1_across"][:, 0, :], w["a1_down"][:, 2 * n:2 * n + 1], None, ALU.subtract))
                link(dve.tensor_tensor(dx, dx, dx, ALU.mult))
                dve.tensor_scalar(dy, w["a1_across"][:, 1, :], w["a1_down"][:, 2 * n + 1:2 * n + 2], None, ALU.subtract)\
                   .then_inc(dy_sem, 1)
                dve.wait_ge(dy_sem, 2 * n + 1)
                dve.tensor_tensor(dy, dy, dy, ALU.mult).then_inc(dy_sem, 1)
                dve.wait_ge(dy_sem, 2 * n + 2)
                link(dve.tensor_tensor(dx, dx, dy, ALU.add))
            assert link.n == SETUP_SQUARES
            dve.wait_ge(act_setup, 1)
            link(dve.tensor_reduce(far[:, :], a1_dist[:, :, :].rearrange("p a c -> p (a c)"), AX_X, ALU.max))
            assert link.n == SETUP_MAX
            dve.wait_ge(pool_setup, 2)
            link(dve.tensor_scalar(far[:, :], far_all[:, :], 1e-6, -0.1, ALU.is_gt, ALU.mult))
            link(dve.tensor_scalar(far_all[:, :], far_all[:, :], 1e-6, None, ALU.max))
            link(dve.reciprocal(far_all[:, :], far_all[:, :]))
            link(dve.tensor_tensor(far[:, :], far[:, :], far_all[:, :], ALU.mult))
            link(dve.scalar_tensor_tensor(a1_dist[:, :, :], a1_dist[:, :, :], far[:, 0:1], w["a1_inside"][:, :, :],
                                          ALU.mult, ALU.mult))
            for part in range(3):
                link(dve.tensor_copy(a1_bias3[:, part, :], a1_dist[:, 0, :]))
                if part < 2:
                    link(dve.tensor_tensor(a1_dist[:, 0, :], a1_dist[:, 0, :], a1_bias3[:, part, :], ALU.subtract))
            link(dve.memset(a1_dy[0:3, :], 0.0))
            for part in range(3):
                dve.tensor_copy(a1_last3[0:3, :], a1_dist[0:3, 1, :]).then_inc(dy_sem, 1)
                dve.wait_ge(dy_sem, 4 + 3 * part + 1)
                dve.scalar_tensor_tensor(a1_dy[0:3, :], a1_last3[0:3, :], w["a1_part"][:, part:part + 1], a1_dy[0:3, :],
                                         ALU.mult, ALU.add).then_inc(dy_sem, 1)
                dve.tensor_tensor(a1_dist[0:3, 1, :], a1_dist[0:3, 1, :], a1_last3[0:3, :], ALU.subtract).then_inc(dy_sem, 1)
                dve.wait_ge(dy_sem, 4 + 3 * part + 3)
            link(dve.tensor_copy(a1_last3[0:3, :], a1_dy[0:3, :]))
            for part in range(PARTS):
                link(dve.tensor_copy(pos_b[:, part, :], w["a2_pos"][:, :]))
                if part < PARTS - 1:
                    link(dve.tensor_tensor(w["a2_pos"][:, :], w["a2_pos"][:, :], pos_b[:, part, :], ALU.subtract))
            link(dve.tensor_scalar(w["a2_qkb"][:, 0:1], w["a2_qkb"][:, 0:1], float(HD) ** -0.5, None, ALU.mult))
            dve.wait_ge(act_setup, 2)
            link(dve.tensor_scalar(a_neg[:, :, :], a_neg[:, :, :], -1.0, None, ALU.mult))
            for h in range(HALVES):
                link(dve.tensor_scalar(d_diag[:, h, :], ident[:, :], vec[:, h, SKIP:SKIP + 1], None, ALU.mult))
            link.close()
            need(dve, "x")
            for k in blocks:
                if k in moe:
                    need(dve, k)
                if k == "a3":
                    dve.memset(x_raw[:, :, :, 0:TAPS - 1], 0.0).then_inc(dy_sem, 1)
                    dve.memset(rooms[4][:, :].rearrange("p (r t) -> p r t", t=SEQ)[:, :, 0:1], 0.0).then_inc(dy_sem, 1)
                    dve.wait_ge(dy_sem, 4 + 3 * 3 + 2)
                if k == "a0":
                    first = Steps(dve, first_steps, 0, HEAD)
                    head_vector(dve, 0, 0, first)
                    first.close()
                if k in ("a1", "a2"):
                    first = Steps(dve, first_max, 0 if k == "a1" else 1, SPLIT)
                    row_maxima(dve, k, mh_unit(k, 0), 0, first)
                    first.close()
                if k == "a3":
                    first = Steps(dve, first_conv, 0, CONV)
                    conv_vector(dve, 0, first)
                    first.close()
                with dve.Fori(0, GROUPS - (k in PEELED)) as g:
                    unit_vector(dve, k, g, False)
                if k in PEELED:
                    unit_vector(dve, k, GROUPS - 1, True)


def by_feature(mat):
    return mat.reshape(-1, HEADS, HD).transpose(0, 2, 1).reshape(-1, D)


def arrange(a):
    f = np.float32

    def cat(*parts):
        return np.concatenate(parts, axis=1)

    def rows(*vs):
        return np.broadcast_to(np.concatenate(vs)[None, :], (P, sum(len(v) for v in vs)))

    def tiled(v):
        return np.broadcast_to(v[None, None, :], (P, TILES, E))

    def halves(mat):
        return mat.reshape(HALVES, P, -1).transpose(1, 0, 2)

    t = {"x": a["L0_attn_x"].reshape(-1, D)}
    pos = np.arange(P)
    late = (pos[None, :] > pos[:, None])
    t["ident"] = np.eye(P, dtype=f)
    t["rank8"] = tiled(np.arange(E, 0, -1).astype(f))
    t["causal2"] = np.stack([late * f(MASKED), late.T * f(MASKED)], axis=1).astype(f)
    row = np.arange(PARTS * QUAD)
    t["row_sel"] = (row[:, None] % QUAD == np.arange(QUAD)).astype(f)
    t["part_masks"] = -(pos[:, None] // QUAD > np.arange(PARTS - 1)).astype(f)
    rel = (pos[None, :] - pos[:, None]).astype(f)
    t["a0_rel"] = cat(rel, rel - P, rel)
    t["a0_mask"] = cat(late * f(BELOW), 0 * late, late * f(BELOW)).astype(f)
    t["a0_slope"] = np.broadcast_to(a["L0_attn_alibi_slope"][None, :], (P, 1))
    t["a0_w"] = cat(a["L0_attn_W_qk"], a["L0_attn_W_v"].T)

    wq, wk, wv = a["L1_attn_W_qkv"].reshape(3, D, D).transpose(0, 2, 1)
    t["a1_w"] = cat(by_feature(wq), by_feature(wk), wv, a["L1_attn_W_proj"].T)
    t["a1_rows"] = rows(np.zeros(D, f), a["L1_attn_ln_gamma"], a["L1_attn_ln_beta"], a["L1_attn_b_proj"])
    at = np.clip(np.arange(BW) - 1, 0, P - 1)
    c = a["L1_attn_spatial_centers"]
    t["a1_across"] = np.broadcast_to(c[at].T[None], (P, 2, BW))
    t["a1_down"] = cat(c[at[0:P]], np.broadcast_to(c[P - 1][None], (P, 2)))
    inside = np.zeros((P, 2, BW), f)
    inside[1:, 0, 1:P + 1] = 1
    inside[:, 1, 1:P + 1] = 1
    t["a1_inside"] = inside
    t["a1_part"] = np.eye(3, dtype=f)

    t["a2_w"] = cat(by_feature(a["L2_attn_Wq"]), by_feature(a["L2_attn_Wk"]), a["L2_attn_Wv"], a["L2_attn_Wo"])
    t["a2_qkb"] = cat(by_feature(a["L2_attn_bq"]).T, by_feature(a["L2_attn_bk"]).T)
    start = 2 ** (-2 ** (-(np.log2(HEADS) - 3)))
    slopes = np.array([start * start ** i for i in range(HEADS)]).astype(f)
    t["a2_pos"] = slopes[:, None] * (np.arange(SEQ) - (SEQ - 1)).astype(f)
    t["a2_rows"] = rows(a["L2_attn_bv"], a["L2_attn_bo"])

    t["a3_win"] = a["L3_attn_W_in"]
    wx = a["L3_attn_W_x"]
    b_, c_, d_ = wx[:, 0:N_STATE], wx[:, N_STATE:2 * N_STATE], wx[:, 2 * N_STATE:]
    t["a3_wx"] = halves(cat(*[m[:, n * QUAD:(n + 1) * QUAD] for m in (b_, c_) for n in range(N_STATE // QUAD) for _ in range(PARTS)],
                            np.broadcast_to(d_, (HALVES * P, P))))
    t["a3_wout"] = halves(a["L3_attn_W_out"])
    t["a3_vec"] = halves(cat(a["L3_attn_conv_w"], a["L3_attn_dt_bias"][:, None], a["L3_attn_conv_b"][:, None],
                             a["L3_attn_D"][:, None]))
    t["a3_alog"] = halves(a["L3_attn_A_log"])

    def up(m):
        return m.transpose(1, 0, 2).reshape(D, -1)

    def down(m):
        return m.reshape(-1, P, D).transpose(1, 0, 2).reshape(P, -1)

    t["f0_wr"], t["f0_br"] = a["L0_ffn_Wr"].T, tiled(a["L0_ffn_br"])
    t["f0_up"], t["f0_down"] = up(a["L0_ffn_W1"].transpose(0, 2, 1)), down(a["L0_ffn_W2"].transpose(0, 2, 1))
    t["f0_b1"], t["f0_b2"] = a["L0_ffn_b1"].reshape(-1, P).T, a["L0_ffn_b2"]
    t["f0_ln"] = rows(a["L0_ffn_ln_w"], a["L0_ffn_ln_b"])
    t["f1_wr"], t["f1_br"] = a["L1_ffn_router_w"].T, tiled(a["L1_ffn_router_bias"])
    t["f1_up"] = cat(a["L1_ffn_sw1"], a["L1_ffn_sw3"], up(a["L1_ffn_ew1"]))
    t["f1_down"] = cat(down(a["L1_ffn_sw2"]), down(a["L1_ffn_ew2"]))
    t["f2_wr"] = a["L2_ffn_router_w"]
    t["f2_up"] = cat(up(a["L2_ffn_shared_up"]), up(a["L2_ffn_routed_up"]))
    t["f2_down"] = cat(down(a["L2_ffn_shared_down"]), down(a["L2_ffn_routed_down"]))
    t["f3_wr"], t["f3_br"] = a["L3_ffn_Wr"], tiled(a["L3_ffn_br"])
    t["f3_up"], t["f3_down"] = up(a["L3_ffn_W1"]), down(a["L3_ffn_W2"])
    t["f3_b1"], t["f3_b2"] = a["L3_ffn_b1"].reshape(-1, P).T, a["L3_ffn_b2"]
    return t


def kernel(**inputs):
    import concourse.bacc as bacc
    from concourse.bass_utils import run_bass_kernel_spmd

    nc = bacc.Bacc("TRN2", target_bir_lowering=False, num_devices=1)
    arrays = {k: np.ascontiguousarray(v) for k, v in arrange({k: np.asarray(v) for k, v in inputs.items()}).items()}
    t = {k: nc.dram_tensor(f"in_{k}", v.shape, mybir.dt.from_np(v.dtype), kind="ExternalInput").ap()
         for k, v in arrays.items()}
    out = nc.dram_tensor("out_x", (NSEQ * SEQ, D), F32, kind="ExternalOutput").ap()
    build(nc, t, out)
    r = run_bass_kernel_spmd(nc, [{f"in_{k}": v for k, v in arrays.items()}], core_ids=[0])
    return r.results[0]["out_x"].reshape(NSEQ, SEQ, D)
```
